# Optimizing a Trainium2 kernel written in Bass

```python
import numpy as np
import jax
import jax.numpy as jnp

def _softmax(x, axis=-1):
    return jax.nn.softmax(x, axis=axis)

def _gelu(x):
    return jax.nn.gelu(x, approximate=True)

def _silu(x):
    return jax.nn.silu(x)

def _sigmoid(x):
    return jax.nn.sigmoid(x)

def _layernorm(x, axis=-1, eps=1e-05):
    m = jnp.mean(x, axis=axis, keepdims=True)
    v = jnp.var(x, axis=axis, keepdims=True)
    return (x - m) / jnp.sqrt(v + eps)

def _scatter_add(tgt, idx, src, axis=0):
    return tgt.at[idx].add(src)

def _segment_sum(src, seg, n):
    return jax.ops.segment_sum(src, seg, n)
kernel_name = 'mk_gnn_resnorm_d4_gnn_r8_608753'

def setup_inputs(seed: int=0):
    np.random.seed(seed)
    _w = jnp.asarray

    def _rec_inputs():
        import jax
        import jax.numpy as jnp
        _gk = jax.random.key(seed)
        x = -0.0003713 + 1 * jax.random.normal(jax.random.fold_in(_gk, 1), (6250, 256), jnp.float32)
        src = jax.random.randint(jax.random.fold_in(_gk, 2), (100000,), 0, 6250, jnp.int32)
        dst = jax.random.randint(jax.random.fold_in(_gk, 3), (100000,), 0, 6250, jnp.int32)
        _o = jnp.argsort(dst, stable=True)
        src = src[_o]
        dst = dst[_o]
        edge_attr_65 = 0.000166551 + 1.00014 * jax.random.normal(jax.random.fold_in(_gk, 13), (100000, 65), jnp.float32)
        edge_weight = jax.random.uniform(jax.random.fold_in(_gk, 15), (100000,), jnp.float32, 0.0, 1)
        return (x, src, dst, edge_attr_65, edge_weight)
    x, src, dst, edge_attr_65, edge_weight = _rec_inputs()

    def _L0_gnn_setup():
        import jax, jax.numpy as jnp
        import numpy as np
        N_NODES = 6250
        N_EDGES = 100000
        D = 256
        F_EDGE = 64
        LN_EPS = 1e-05
        key = jax.random.key(seed)
        ks = jax.random.split(key, 12)
        s = 0.05
        return {'x': jax.random.normal(ks[0], (N_NODES, D), jnp.float32), 'edge_index': jax.random.randint(ks[1], (2, N_EDGES), 0, N_NODES, jnp.int64), 'edge_attr': jax.random.normal(ks[2], (N_EDGES, F_EDGE + 1), jnp.float32), 'W_e1': jax.random.normal(ks[3], (D, F_EDGE), jnp.float32) * s, 'b_e1': jnp.zeros((D,), jnp.float32), 'W_e2': jax.random.normal(ks[4], (D, D), jnp.float32) * s, 'b_e2': jnp.zeros((D,), jnp.float32), 'W_le': jax.random.normal(ks[5], (D, D), jnp.float32) * s, 'b_le': jnp.zeros((D,), jnp.float32), 'W_g1': jax.random.normal(ks[6], (D, D), jnp.float32) * s, 'b_g1': jnp.zeros((D,), jnp.float32), 'ln_g': jnp.ones((D,), jnp.float32), 'ln_b': jnp.zeros((D,), jnp.float32), 'W_g2': jax.random.normal(ks[7], (D, D), jnp.float32) * s, 'b_g2': jnp.zeros((D,), jnp.float32)}
    _L0_gnn_all = _L0_gnn_setup()
    _L0_gnn_in = {k: v for k, v in _L0_gnn_all.items() if k in ('W_e1', 'b_e1', 'W_e2', 'b_e2', 'W_le', 'b_le', 'W_g1', 'b_g1', 'ln_g', 'ln_b', 'W_g2', 'b_g2')}
    del _L0_gnn_all

    def _L1_gnn_setup():
        import jax, jax.numpy as jnp
        import numpy as np
        N = 6250
        E = 100000
        IN = 256
        POS = 16
        H = 4
        D = 64
        D4 = D // 4

        def _xavier(key, shape):
            fan_out, fan_in = (shape[0], shape[1])
            lim = np.sqrt(6.0 / (fan_in + fan_out)).astype(np.float32)
            return jax.random.uniform(key, shape, jnp.float32, -lim, lim)
        key = jax.random.key(seed)
        ks = jax.random.split(key, 10)
        feat = jax.random.normal(ks[0], (N, IN), jnp.float32)
        src = jax.random.randint(ks[1], (E,), 0, N, jnp.int32)
        dst = jax.random.randint(ks[2], (E,), 0, N, jnp.int32)
        cd = IN - POS
        Wc = _xavier(ks[3], (H * D, cd))
        Wp = _xavier(ks[4], (H * D4, POS))
        attn_src = _xavier(ks[5], (H, D)).reshape(1, H, D)
        attn_dst = _xavier(ks[6], (H, D)).reshape(1, H, D)
        pos_attn_src = _xavier(ks[7], (H, D4)).reshape(1, H, D4)
        pos_attn_dst = _xavier(ks[8], (H, D4)).reshape(1, H, D4)
        att_comb = jnp.full((H, 2), 0.5, jnp.float32)
        return {'feat': feat, 'src': src, 'dst': dst, 'Wc': Wc, 'Wp': Wp, 'attn_src': attn_src, 'attn_dst': attn_dst, 'pos_attn_src': pos_attn_src, 'pos_attn_dst': pos_attn_dst, 'att_comb': att_comb}
    _L1_gnn_all = _L1_gnn_setup()
    _L1_gnn_in = {k: v for k, v in _L1_gnn_all.items() if k in ('Wc', 'Wp', 'attn_src', 'attn_dst', 'pos_attn_src', 'pos_attn_dst', 'att_comb')}
    del _L1_gnn_all

    def _L2_gnn_setup():
        import jax, jax.numpy as jnp
        import numpy as np
        N_NODES = 6250
        N_EDGES = 100000
        H = 256

        def sage_layer(x, src, dst, Wl, bl, Wr, n_nodes):
            msg = x[src]
            agg = jax.ops.segment_sum(msg, dst, num_segments=n_nodes)
            deg = jax.ops.segment_sum(jnp.ones_like(src, dtype=x.dtype), dst, num_segments=n_nodes)
            agg = agg / jnp.maximum(deg, 1.0)[:, None]
            return agg @ Wl.T + bl + x @ Wr.T
        key = jax.random.key(seed)
        ks = jax.random.split(key, 12)
        scale = 1.0 / np.sqrt(H)
        inp = {'x': jax.random.normal(ks[0], (N_NODES, H), dtype=jnp.float32), 'edge_index': jax.random.randint(ks[1], (2, N_EDGES), 0, N_NODES, dtype=jnp.int64)}
        for i, name in enumerate(['Wl1', 'Wr1', 'Wl2', 'Wr2', 'Wl3', 'Wr3']):
            inp[name] = jax.random.normal(ks[2 + i], (H, H), dtype=jnp.float32) * scale
        for name in ['bl1', 'bl2', 'bl3']:
            inp[name] = jnp.zeros((H,), dtype=jnp.float32)
        return inp
    _L2_gnn_all = _L2_gnn_setup()
    _L2_gnn_in = {k: v for k, v in _L2_gnn_all.items() if k in ('Wl1', 'bl1', 'Wr1', 'Wl2', 'bl2', 'Wr2', 'Wl3', 'bl3', 'Wr3')}
    del _L2_gnn_all

    def _L3_gnn_setup():
        import jax, jax.numpy as jnp
        import numpy as np
        N, E, C = (6250, 100000, 256)
        EPS = 1e-05
        key = jax.random.key(seed)
        ks = jax.random.split(key, 6)
        s = 1.0 / np.sqrt(C)
        return {'x': jax.random.normal(ks[0], (N, C), jnp.float32), 'edge_weight': jax.random.uniform(ks[1], (E,), jnp.float32), 'W_rel': jax.random.normal(ks[2], (C, C), jnp.float32) * s, 'b_rel': jnp.zeros((C,), jnp.float32), 'W_root': jax.random.normal(ks[3], (C, C), jnp.float32) * s, 'gamma': jnp.ones((C,), jnp.float32), 'beta': jnp.zeros((C,), jnp.float32), 'edge_index': jax.random.randint(ks[4], (2, E), 0, N, jnp.int32), 'batch': jnp.zeros((N,), jnp.int32)}
    _L3_gnn_all = _L3_gnn_setup()
    _L3_gnn_in = {k: v for k, v in _L3_gnn_all.items() if k in ('W_rel', 'b_rel', 'W_root', 'gamma', 'beta')}
    del _L3_gnn_all
    return {'x': x, 'src': src, 'dst': dst, 'edge_attr_65': edge_attr_65, 'edge_weight': edge_weight, 'L0_gnn_W_e1': _L0_gnn_in['W_e1'], 'L0_gnn_b_e1': _L0_gnn_in['b_e1'], 'L0_gnn_W_e2': _L0_gnn_in['W_e2'], 'L0_gnn_b_e2': _L0_gnn_in['b_e2'], 'L0_gnn_W_le': _L0_gnn_in['W_le'], 'L0_gnn_b_le': _L0_gnn_in['b_le'], 'L0_gnn_W_g1': _L0_gnn_in['W_g1'], 'L0_gnn_b_g1': _L0_gnn_in['b_g1'], 'L0_gnn_ln_g': _L0_gnn_in['ln_g'], 'L0_gnn_ln_b': _L0_gnn_in['ln_b'], 'L0_gnn_W_g2': _L0_gnn_in['W_g2'], 'L0_gnn_b_g2': _L0_gnn_in['b_g2'], 'L1_gnn_Wc': _L1_gnn_in['Wc'], 'L1_gnn_Wp': _L1_gnn_in['Wp'], 'L1_gnn_attn_src': _L1_gnn_in['attn_src'], 'L1_gnn_attn_dst': _L1_gnn_in['attn_dst'], 'L1_gnn_pos_attn_src': _L1_gnn_in['pos_attn_src'], 'L1_gnn_pos_attn_dst': _L1_gnn_in['pos_attn_dst'], 'L1_gnn_att_comb': _L1_gnn_in['att_comb'], 'L2_gnn_Wl1': _L2_gnn_in['Wl1'], 'L2_gnn_bl1': _L2_gnn_in['bl1'], 'L2_gnn_Wr1': _L2_gnn_in['Wr1'], 'L2_gnn_Wl2': _L2_gnn_in['Wl2'], 'L2_gnn_bl2': _L2_gnn_in['bl2'], 'L2_gnn_Wr2': _L2_gnn_in['Wr2'], 'L2_gnn_Wl3': _L2_gnn_in['Wl3'], 'L2_gnn_bl3': _L2_gnn_in['bl3'], 'L2_gnn_Wr3': _L2_gnn_in['Wr3'], 'L3_gnn_W_rel': _L3_gnn_in['W_rel'], 'L3_gnn_b_rel': _L3_gnn_in['b_rel'], 'L3_gnn_W_root': _L3_gnn_in['W_root'], 'L3_gnn_gamma': _L3_gnn_in['gamma'], 'L3_gnn_beta': _L3_gnn_in['beta']}

def reference(x, src, dst, edge_attr_65, edge_weight, L0_gnn_W_e1, L0_gnn_b_e1, L0_gnn_W_e2, L0_gnn_b_e2, L0_gnn_W_le, L0_gnn_b_le, L0_gnn_W_g1, L0_gnn_b_g1, L0_gnn_ln_g, L0_gnn_ln_b, L0_gnn_W_g2, L0_gnn_b_g2, L1_gnn_Wc, L1_gnn_Wp, L1_gnn_attn_src, L1_gnn_attn_dst, L1_gnn_pos_attn_src, L1_gnn_pos_attn_dst, L1_gnn_att_comb, L2_gnn_Wl1, L2_gnn_bl1, L2_gnn_Wr1, L2_gnn_Wl2, L2_gnn_bl2, L2_gnn_Wr2, L2_gnn_Wl3, L2_gnn_bl3, L2_gnn_Wr3, L3_gnn_W_rel, L3_gnn_b_rel, L3_gnn_W_root, L3_gnn_gamma, L3_gnn_beta):
    import jax
    import jax.numpy as jnp

    def _L0_gnn_ref(x, edge_index, edge_attr, W_e1, b_e1, W_e2, b_e2, W_le, b_le, W_g1, b_g1, ln_g, ln_b, W_g2, b_g2):
        import jax, jax.numpy as jnp
        import numpy as np
        N_NODES = 6250
        N_EDGES = 100000
        D = 256
        F_EDGE = 64
        LN_EPS = 1e-05
        polarity = jnp.clip(edge_attr[:, 0:1], 0.0, 1.0)
        raw = edge_attr[:, 1:]
        e = jax.nn.relu(raw @ W_e1.T + b_e1) @ W_e2.T + b_e2
        gated = e * (polarity + 0.01)
        edge_emb = gated @ W_le.T + b_le
        src, dst = (edge_index[0], edge_index[1])
        msg = jax.nn.relu(x[src] + edge_emb)
        aggr = jax.ops.segment_sum(msg, dst, num_segments=x.shape[0])
        h = (x + aggr) @ W_g1.T + b_g1
        mu = jnp.mean(h, axis=-1, keepdims=True)
        var = jnp.mean(jnp.square(h - mu), axis=-1, keepdims=True)
        hn = (h - mu) * jax.lax.rsqrt(var + LN_EPS) * ln_g + ln_b
        return jax.nn.relu(hn) @ W_g2.T + b_g2

    def _L1_gnn_ref(feat, src, dst, Wc, Wp, attn_src, attn_dst, pos_attn_src, pos_attn_dst, att_comb):
        import jax, jax.numpy as jnp
        import numpy as np
        N = 6250
        E = 100000
        IN = 256
        POS = 16
        H = 4
        D = 64
        D4 = D // 4

        def _xavier(key, shape):
            fan_out, fan_in = (shape[0], shape[1])
            lim = np.sqrt(6.0 / (fan_in + fan_out)).astype(np.float32)
            return jax.random.uniform(key, shape, jnp.float32, -lim, lim)
        n = feat.shape[0]
        content = feat[:, :IN - POS]
        pos = feat[:, IN - POS:]
        hc = (content @ Wc.T).reshape(n, H, D)
        hp = (pos @ Wp.T).reshape(n, H, D4)
        s_c = jnp.einsum('nhd,hd->nh', hc, attn_src[0])
        d_c = jnp.einsum('nhd,hd->nh', hc, attn_dst[0])
        s_p = jnp.einsum('nhd,hd->nh', hp, pos_attn_src[0])
        d_p = jnp.einsum('nhd,hd->nh', hp, pos_attn_dst[0])
        content_e = s_c[src] + d_c[dst]
        pos_e = s_p[src] + d_p[dst]
        e = content_e * att_comb[:, 0] + pos_e * att_comb[:, 1]
        e = jax.nn.leaky_relu(e, negative_slope=0.2)
        m = jax.ops.segment_max(e, dst, num_segments=n)
        m = jax.lax.stop_gradient(jnp.where(jnp.isfinite(m), m, 0.0))
        ee = jnp.exp(e - m[dst])
        denom = jax.ops.segment_sum(ee, dst, num_segments=n)
        a = ee / denom[dst]
        msg = hc[src] * a[..., None]
        ft = jax.ops.segment_sum(msg, dst, num_segments=n)
        h = ft.reshape(n, H * D)
        h = h + feat
        return h

    def _L2_gnn_ref(x, edge_index, Wl1, bl1, Wr1, Wl2, bl2, Wr2, Wl3, bl3, Wr3):
        import jax, jax.numpy as jnp
        import numpy as np
        N_NODES = 6250
        N_EDGES = 100000
        H = 256

        def sage_layer(x, src, dst, Wl, bl, Wr, n_nodes):
            msg = x[src]
            agg = jax.ops.segment_sum(msg, dst, num_segments=n_nodes)
            deg = jax.ops.segment_sum(jnp.ones_like(src, dtype=x.dtype), dst, num_segments=n_nodes)
            agg = agg / jnp.maximum(deg, 1.0)[:, None]
            return agg @ Wl.T + bl + x @ Wr.T
        src, dst = (edge_index[0], edge_index[1])
        n = x.shape[0]
        h = jax.nn.elu(sage_layer(x, src, dst, Wl1, bl1, Wr1, n))
        h = jax.nn.elu(sage_layer(h, src, dst, Wl2, bl2, Wr2, n))
        h = jax.nn.elu(sage_layer(h, src, dst, Wl3, bl3, Wr3, n))
        return h

    def _L3_gnn_ref(x, edge_weight, W_rel, b_rel, W_root, gamma, beta, edge_index, batch):
        import jax, jax.numpy as jnp
        import numpy as np
        N, E, C = (6250, 100000, 256)
        EPS = 1e-05
        src, dst = (edge_index[0], edge_index[1])
        msg = x[src] * edge_weight[:, None]
        agg = jax.ops.segment_sum(msg, dst, num_segments=x.shape[0])
        out = agg @ W_rel.T + b_rel + x @ W_root.T
        mean = out.mean(axis=0)
        var = out.var(axis=0)
        out = (out - mean) * jax.lax.rsqrt(var + EPS) * gamma + beta
        out = jax.nn.relu(out)
        out = jax.nn.relu(out + x)
        return out
    edge_index = jnp.stack([src, dst])
    batch0 = jnp.zeros((6250,), jnp.int32)
    x = _layernorm(x + _L0_gnn_ref(x, edge_index, edge_attr_65, L0_gnn_W_e1, L0_gnn_b_e1, L0_gnn_W_e2, L0_gnn_b_e2, L0_gnn_W_le, L0_gnn_b_le, L0_gnn_W_g1, L0_gnn_b_g1, L0_gnn_ln_g, L0_gnn_ln_b, L0_gnn_W_g2, L0_gnn_b_g2), axis=-1)
    x = _layernorm(x + _L1_gnn_ref(x, src, dst, L1_gnn_Wc, L1_gnn_Wp, L1_gnn_attn_src, L1_gnn_attn_dst, L1_gnn_pos_attn_src, L1_gnn_pos_attn_dst, L1_gnn_att_comb), axis=-1)
    x = _layernorm(x + _L2_gnn_ref(x, edge_index, L2_gnn_Wl1, L2_gnn_bl1, L2_gnn_Wr1, L2_gnn_Wl2, L2_gnn_bl2, L2_gnn_Wr2, L2_gnn_Wl3, L2_gnn_bl3, L2_gnn_Wr3), axis=-1)
    x = _layernorm(x + _L3_gnn_ref(x, edge_weight, L3_gnn_W_rel, L3_gnn_b_rel, L3_gnn_W_root, L3_gnn_gamma, L3_gnn_beta, edge_index, batch0), axis=-1)
    return x

_drawn_inputs = setup_inputs


def setup_inputs(seed=0):
    import zlib

    import numpy as np

    out = dict(_drawn_inputs(seed))
    spreads = {'L0_gnn_b_e1': (0.0, 0.8),
     'L0_gnn_b_e2': (0.0, 0.46),
     'L0_gnn_b_le': (0.0, 0.1),
     'L0_gnn_b_g1': (0.0, 0.533),
     'L0_gnn_ln_g': (1.0, 0.2),
     'L0_gnn_ln_b': (0.0, 0.1),
     'L0_gnn_b_g2': (0.0, 0.1),
     'L1_gnn_att_comb': (0.5, 0.6),
     'L2_gnn_bl1': (0.0, 0.1),
     'L2_gnn_bl2': (0.0, 0.1),
     'L2_gnn_bl3': (0.0, 0.1),
     'L3_gnn_b_rel': (0.0, 0.8),
     'L3_gnn_gamma': (1.0, 0.2),
     'L3_gnn_beta': (0.0, 0.1)}
    factors = {'edge_attr_65': 3.257, 'L0_gnn_W_e1': 3.904, 'L1_gnn_pos_attn_dst': 5.795}
    for name, (base, spread) in spreads.items():
        noise = np.random.default_rng([zlib.crc32(name.encode()), seed]).standard_normal(out[name].shape)
        drawn = base * np.exp(spread * noise) if base else spread * noise
        out[name] = jnp.asarray(drawn.astype(out[name].dtype))
    for name, factor in factors.items():
        out[name] = (out[name] * factor).astype(out[name].dtype)
    return out
```

```python
import concourse.bass as bass
from concourse import mybir
from contextlib import ExitStack, contextmanager

FP32 = mybir.dt.float32
I32 = mybir.dt.int32
ALU = mybir.AluOpType
ACT = mybir.ActivationFunctionType
AX = mybir.AxisListType

P = 128
D = 256
KH = D // P
GE = 512
TI = GE // P
W = 64
WSHIFT = 6
H = 4
DH = D // H
RING = 4
BIG = 1.7e38
EPS = 1e-5
NOWHERE = -1.0e4


def pipelined(eng, count, unroll, stages):
    lags = max(lag for lag, _ in stages)

    def step(base, u):
        for lag, f in stages:
            t = base + u - lag
            if isinstance(t, int) and not 0 <= t < count:
                continue
            f(t, (u - lag) % unroll)

    head = -(-(lags + 4) // unroll) * unroll
    loops = max(0, (count - 1 - head) // unroll)
    if loops < 2:
        head, loops = 0, 0
    for s in range(head):
        step(s - s % unroll, s % unroll)
    if loops:
        with eng.Fori(0, loops) as it:
            base = it * unroll + head
            for u in range(unroll):
                step(base, u)
    for s in range(head + loops * unroll, count + lags):
        step(s - s % unroll, s % unroll)


@contextmanager
def between(eng, lo, hi):
    with eng.If(lo < hi):
        with eng.Fori(lo, hi) as q:
            yield q


def later(t, n):
    return not isinstance(t, int) or t >= n


def gnn_kernel(nc, ins, out, depth):
    N = ins["x"].shape[0]
    E = ins["src"].shape[0]
    NG = -(-E // GE)
    TAILP = (E - GE * (NG - 1)) // TI
    NT = -(-N // P)
    LASTR = N - P * (NT - 1)
    NW = N + W + P
    HCW = D + H
    NKW = -(-N // W) + 1
    MAXX = NKW + 1

    def rows(t):
        return LASTR if isinstance(t, int) and t == NT - 1 else P

    ctx = ExitStack()
    taken = []

    def sems(tag, names):
        got = [nc.alloc_semaphore(f"{tag}_{n}") for n in names.split()]
        taken.extend(got)
        return got

    def phase(build, *args, **kwargs):
        build(*args, **kwargs)
        nc.clear_and_free_semaphores(taken)
        taken.clear()
        nc.all_engine_barrier()

    def scoped(scope, tag):
        def sb(name, shape, dt=FP32):
            return scope.enter_context(nc.sbuf_tensor(f"{tag}_{name}", shape, dt))

        def ps(name, shape):
            free = 1
            for n in shape[1:]:
                free *= n
            whole = scope.enter_context(nc.psum_tensor(f"{tag}_{name}", [P, -(-free // 512) * 512], FP32))
            flat = whole[0:shape[0], 0:free]
            if len(shape) == 3:
                return flat.rearrange("p (a b) -> p a b", b=shape[2])
            return flat
        return sb, ps

    def dram(name, shape, dt=FP32):
        return nc.dram_tensor(name, shape, dt, kind="Internal").ap()

    with ctx:
        sb, _ = scoped(ctx, "all")
        t_x0 = dram("t_x0", (N, D))
        t_hc = dram("t_hc", (N, HCW))
        t_dst = dram("t_dst", (N + W * 2, H))
        t_x1 = dram("t_x1", (N, D))
        t_x2 = dram("t_x2", (N, D))
        t_h1 = dram("t_h1", (N, D))
        t_h2 = dram("t_h2", (N, D))
        t_x3 = dram("t_x3", (N, D))
        t_r = [dram(f"t_r{i}", (N, D)) for i in range(3)]
        t_flag = dram("t_flag", (NG, GE))

        agg = sb("agg", [P, KH, NW])
        aux = sb("aux", [P, KH, NW])
        den = aux[0:H + 1, 0, :]
        srcT = sb("srcT", [P, NG * TI], I32)
        relT = sb("relT", [P, NG * TI])
        ewT = sb("ewT", [P, NG * TI])
        nbase = sb("nbase", [W, NG])
        starts = sb("starts", [P, MAXX])
        ctrl = sb("ctrl", [1, 2 * NG + 1], I32)
        c_first, c_extra = 0, NG
        iotaw = sb("iotaw", [P, W])
        ident = sb("ident", [P, P])
        ones = sb("ones", [1, P])
        epsc = sb("epsc", [P, 1])
        idx = [sb(f"idx{s}", [P, TI], I32) for s in range(RING)]
        invdeg = sb("invdeg", [P, NT])
        wT = {}
        for n in "W_g1 W_g2 Wl1 Wr1 Wl2 Wr2 Wl3 Wr3 W_rel W_root fuse".split():
            wT[n] = sb("T" + n, [P, KH, D])
        wT["attn"] = sb("Tattn", [P, KH, D + 2 * H])
        w_e1T = sb("w_e1T", [65, D])
        rows_of = {}
        for n in "b_le c2 b_g1 b_g2 bl1 bl2 bl3".split():
            rows_of[n] = sb("R" + n, [P, D])
        cols_of = {}
        for n in "b_e1 ln_g ln_b b_rel gamma beta".split():
            cols_of[n] = sb("C" + n, [P, KH])
        headmask = sb("headmask", [H, D])

        def extra_lo(eng, g):
            return eng.value_load(ctrl[0:1, bass.ds(g + c_extra, 1)], min_val=0, max_val=NG * NKW)

        def extra_hi(eng, g):
            return eng.value_load(ctrl[0:1, bass.ds(g + c_extra + 1, 1)], min_val=0, max_val=NG * NKW)

        def bounded(eng, value, most):
            return eng.snap(value.with_bounds(min_val=0, max_val=most))

        def first_dst(eng, g):
            return eng.value_load(ctrl[0:1, bass.ds(g + c_first, 1)], min_val=0, max_val=N - 1)

        def edge_tables():
            with ExitStack() as scope:
                sb, ps = scoped(scope, "et")
                blocks = [(a, min(P, NG - a)) for a in range(0, NG, P)]
                NB = len(blocks)
                d_i = sb("d_i", [P, NB, GE], I32)
                q_i = sb("q_i", [P, NB, GE], I32)
                s_i = sb("s_i", [P, NB, GE], I32)
                w_f = sb("w_f", [P, NB, GE])
                d_f = sb("d_f", [P, NB, GE])
                q_f = sb("q_f", [P, NB, GE])
                s_f = sb("s_f", [P, NB, GE])
                flag = sb("flag", [P, NB, GE])
                last = sb("last", [P, NB])
                frow = sb("frow", [1, NG])
                lrow = sb("lrow", [1, NG])
                span = sb("span", [1, NG])
                spani = sb("spani", [1, NG], I32)
                spanf = sb("spanf", [1, NG])
                xrow = sb("xrow", [1, NG])
                zrow = sb("zrow", [1, NG])
                pidx = sb("pidx", [P, 1])
                ps_t = [ps(f"ps_t{i}", [P, 4, P]) for i in range(3)]
                ps_r = ps("ps_r", [1, 2, NG])
                ps_b = ps("ps_b", [P, NG])
                (filled, loaded, cast, lasted, turned, copied, rowed, v, flagged, based, made, consts, filled2,
                 bmade) = sems("et", "filled loaded cast lasted turned copied rowed v flagged based made consts filled2 bmade")
                made_flags, = sems("et", "made_flags")
                n_loads = 0
                for a, n in blocks:
                    full = min(a + n, NG - 1) - a
                    n_loads += 3 * ((full > 0) + (full < n)) + (a == 0) + (full > (1 if a == 0 else 0)) + (full < n)
                with nc.Block() as block:
                    @block.gpsimd
                    def _(pool):
                        nc.gpsimd.memset(ident[:, :], 0.0).then_inc(made, 1)
                        nc.gpsimd.iota(iotaw[:, :], [[1, W]], base=0, channel_multiplier=0,
                                       allow_small_or_imprecise_dtypes=True).then_inc(made, 1)
                        nc.gpsimd.iota(starts[:, :], [[W, MAXX]], base=0, channel_multiplier=0,
                                       allow_small_or_imprecise_dtypes=True).then_inc(made, 1)
                        nc.gpsimd.iota(pidx[:, :], [[0, 1]], base=0, channel_multiplier=1,
                                       allow_small_or_imprecise_dtypes=True).then_inc(made, 1)
                        nc.gpsimd.memset(headmask[:, :], 1.0).then_inc(made, 1)
                        pool.wait_ge(made, 5)
                        nc.gpsimd.affine_select(out=ident[:, :], in_=ident[:, :], compare_op=ALU.not_equal, fill=1.0,
                                                base=0, pattern=[[-1, P]], channel_multiplier=1).then_inc(consts, 1)
                        nc.gpsimd.affine_select(out=headmask[:, :], in_=headmask[:, :], compare_op=ALU.is_ge,
                                                fill=0.0, base=0, pattern=[[1, D]],
                                                channel_multiplier=-DH).then_inc(made, 1)
                        pool.wait_ge(made, 6)
                        nc.gpsimd.affine_select(out=headmask[:, :], in_=headmask[:, :], compare_op=ALU.is_ge,
                                                fill=0.0, base=DH - 1, pattern=[[-1, D]],
                                                channel_multiplier=DH).then_inc(consts, 1)
                        pool.wait_ge(consts, 2)

                    def grouped(dram_vec, a, n):
                        return dram_vec[a * GE:(a + n) * GE].rearrange("(g e) -> g e", e=GE)

                    @block.sync
                    def _(sp):
                        sp.wait_ge(filled, 1)
                        for b, (a, n) in enumerate(blocks):
                            full = min(a + n, NG - 1) - a
                            for tile, vec in ((d_i, ins["dst"]), (s_i, ins["src"]), (w_f, ins["edge_weight"])):
                                if full:
                                    sp.dma_start(tile[0:full, b, :], grouped(vec, a, full)).then_inc(loaded, 16)
                                if full < n:
                                    sp.dma_start(tile[full:n, b, 0:TAILP * TI],
                                                 vec[(a + full) * GE:E].rearrange("(g e) -> g e", g=1)
                                                 ).then_inc(loaded, 16)
                            lo = 1 if a == 0 else 0
                            if a == 0:
                                sp.dma_start(q_i[0:1, b, 1:GE],
                                             ins["dst"][0:GE - 1].rearrange("(g e) -> g e", g=1)).then_inc(loaded, 16)
                            if full > lo:
                                sp.dma_start(q_i[lo:full, b, :],
                                             ins["dst"][(a + lo) * GE - 1:(a + full) * GE - 1].rearrange(
                                                 "(g e) -> g e", e=GE)).then_inc(loaded, 16)
                            if full < n:
                                sp.dma_start(q_i[full:n, b, 0:TAILP * TI + 1],
                                             ins["dst"][(a + full) * GE - 1:E].rearrange("(g e) -> g e", g=1)
                                             ).then_inc(loaded, 16)
                        for b, (a, n) in enumerate(blocks):
                            sp.wait_ge(flagged, b + 1)
                            sp.dma_start(t_flag[a:a + n, :], flag[0:n, b, :]).then_inc(made_flags, 16)
                        sp.wait_ge(made_flags, 16 * NB)

                    @block.vector
                    def _(dve):
                        nc.vector.memset(d_i[:, :, :], int(NOWHERE))
                        nc.vector.memset(q_i[:, :, :], -1)
                        nc.vector.memset(s_i[:, :, :], 0)
                        nc.vector.memset(w_f[:, :, :], 0.0).then_inc(filled, 1)
                        nc.vector.memset(ones[:, :], 1.0)
                        nc.vector.memset(epsc[:, :], EPS)
                        nc.vector.memset(zrow[:, :], 0.0).then_inc(filled2, 1)
                        dve.wait_ge(loaded, 16 * n_loads)
                        nc.vector.tensor_copy(d_f[:, :, :], d_i[:, :, :]).then_inc(cast, 1)
                        nc.vector.tensor_copy(q_f[:, :, :], q_i[:, :, :]).then_inc(cast, 1)
                        nc.vector.tensor_copy(s_f[:, :, :], s_i[:, :, :]).then_inc(cast, 1)
                        dve.wait_ge(cast, 2)
                        nc.vector.tensor_reduce(last[:, :], d_f[:, :, :], AX.X, ALU.max).then_inc(lasted, 1)
                        nc.vector.tensor_tensor(flag[:, :, :], d_f[:, :, :], q_f[:, :, :],
                                                ALU.not_equal).then_inc(v, 1)
                        dve.wait_ge(v, 1)
                        for b in range(NB):
                            nc.vector.tensor_scalar(flag[:, b, :], flag[:, b, :], -2 * BIG, BIG, ALU.mult,
                                                    ALU.add).then_inc(flagged, 1)
                        dve.wait_ge(rowed, 1)
                        nc.vector.tensor_copy(frow[:, :], ps_r[0:1, 0, :]).then_inc(based, 1)
                        nc.vector.tensor_copy(lrow[:, :], ps_r[0:1, 1, :]).then_inc(v, 1)
                        dve.wait_ge(based, 1)
                        dve.wait_ge(v, 2)
                        nc.vector.tensor_copy(ctrl[0:1, 0:NG], frow[:, :])
                        nc.vector.tensor_tensor(span[:, :], lrow[:, :], frow[:, :], ALU.subtract).then_inc(v, 1)
                        dve.wait_ge(v, 3)
                        nc.vector.tensor_copy(spani[:, :], span[:, :]).then_inc(v, 1)
                        dve.wait_ge(v, 4)
                        nc.vector.tensor_scalar(spani[:, :], spani[:, :], WSHIFT, None,
                                                ALU.arith_shift_right).then_inc(v, 1)
                        dve.wait_ge(v, 5)
                        nc.vector.tensor_copy(spanf[:, :], spani[:, :]).then_inc(v, 1)
                        dve.wait_ge(v, 6)
                        dve.wait_ge(filled2, 1)
                        nc.vector.tensor_tensor_scan(xrow[:, :], spanf[:, :], zrow[:, :], 0.0, ALU.add,
                                                     ALU.add).then_inc(v, 1)
                        nc.vector.memset(ctrl[0:1, NG:NG + 1], 0)
                        dve.wait_ge(v, 7)
                        nc.vector.tensor_copy(ctrl[0:1, NG + 1:2 * NG + 1], xrow[:, :])
                        n_done = 0
                        for b, (a, n) in enumerate(blocks):
                            for k, dest in enumerate((relT, srcT, ewT)):
                                n_done += 1
                                dve.wait_ge(turned, n_done)
                                nc.vector.tensor_copy(
                                    dest[:, a * TI:(a + n) * TI].rearrange("p (g i) -> p i g", i=TI),
                                    ps_t[k][:, :, 0:n]).then_inc(copied, 1)
                        dve.wait_ge(bmade, 1)
                        dve.wait_ge(copied, 3 * NB)
                        rv = relT[:, :].rearrange("p (g i) -> p g i", i=TI)
                        nc.vector.tensor_tensor(rv, rv, ps_b[:, :].unsqueeze(2).broadcast_to([P, NG, TI]),
                                                ALU.subtract).then_inc(v, 1)
                        dve.wait_ge(consts, 2)
                        nc.vector.tensor_scalar(nbase[:, :], ps_b[0:W, :], pidx[0:W, :], None, ALU.add).then_inc(v, 1)
                        dve.wait_ge(v, 9)

                    @block.tensor
                    def _(pe):
                        pe.wait_ge(consts, 1)
                        pe.wait_ge(lasted, 1)
                        for b, (a, n) in enumerate(blocks):
                            nc.tensor.transpose(ps_r[0:1, 0, a:a + n], d_f[0:n, b, 0:1], ident[0:n, 0:n])
                            m = nc.tensor.transpose(ps_r[0:1, 1, a:a + n], last[0:n, b:b + 1], ident[0:n, 0:n])
                        m.then_inc(rowed, 1)
                        pe.wait_ge(cast, 3)
                        for b, (a, n) in enumerate(blocks):
                            if b:
                                pe.wait_ge(copied, 3 * b)
                            for k, tile in enumerate((d_f, s_f, w_f)):
                                tv = tile[0:n, b, :].rearrange("g (p i) -> g i p", i=TI)
                                for i in range(TI):
                                    m = nc.tensor.transpose(ps_t[k][:, i, 0:n], tv[:, i, :], ident[0:n, 0:n])
                                m.then_inc(turned, 1)
                        pe.wait_ge(based, 1)
                        pe.wait_ge(filled2, 1)
                        nc.tensor.matmul(ps_b[:, :], ones[0:1, :], frow[0:1, :], start=True, stop=True).then_inc(bmade, 1)

        def weights():
            with ExitStack() as scope:
                sb, ps = scoped(scope, "wt")
                names = dict(W_g1="L0_gnn_W_g1", W_g2="L0_gnn_W_g2", Wl1="L2_gnn_Wl1", Wr1="L2_gnn_Wr1",
                             Wl2="L2_gnn_Wl2", Wr2="L2_gnn_Wr2", Wl3="L2_gnn_Wl3", Wr3="L2_gnn_Wr3",
                             W_rel="L3_gnn_W_rel", W_root="L3_gnn_W_root", W_le="L0_gnn_W_le")
                raw = {n: sb("w" + n, [P, KH, D]) for n in names}
                w_leT = sb("w_leT", [P, KH, D])
                targets = {**{n: wT[n] for n in names if n != "W_le"}, "W_le": w_leT}
                we2 = sb("we2", [P, KH, D])
                we1 = sb("we1", [P, KH, 65])
                CD = ins["L1_gnn_Wc"].shape[1]
                POS = D - CD
                D4 = DH // 4
                wc = sb("wc", [P, KH, CD])
                wp_ = sb("wp", [H * D4, POS])
                av = [sb(f"av{j}", [P, KH]) for j in range(2)]
                ap_ = sb("ap", [H * D4, 2])
                avm = sb("avm", [P, KH, 2 * H])
                apm = sb("apm", [H * D4, 2 * H])
                hm_c = sb("hm_c", [P, KH, H])
                hm_p = sb("hm_p", [H * D4, H])
                comb = sb("comb", [P, H, 2])
                be2 = sb("be2", [P, KH])
                be2b = sb("be2b", [P, KH, P])
                vrow = sb("vrow", [2 * H, D])
                wpz = sb("wpz", [H * D4, D])
                wcz = sb("wcz", [P, KH, D])
                onesb = sb("onesb", [P, P])
                ps_w = [ps(f"ps_w{i}", [P, 512]) for i in range(2)]
                ps_f = [ps(f"ps_f{i}", [P, 256]) for i in range(2)]
                ps_c = ps("ps_c", [P, 256])
                ps_v = ps("ps_v", [2 * H, D])
                ps_vt = ps("ps_vt", [P, KH, 2 * H])
                loads = []
                for n, k in names.items():
                    loads.append((raw[n][:, :, :], ins[k].rearrange("(h p) c -> p h c", p=P)))
                loads.append((we2[:, :, :], ins["L0_gnn_W_e2"].rearrange("(h p) c -> p h c", p=P)))
                loads.append((we1[:, :, 1:65], ins["L0_gnn_W_e1"].rearrange("(h p) c -> p h c", p=P)))
                loads.append((wc[:, :, :], ins["L1_gnn_Wc"].rearrange("(h p) c -> p h c", p=P)))
                loads.append((wp_[:, :], ins["L1_gnn_Wp"]))
                for j, n in enumerate(("attn_src", "attn_dst")):
                    loads.append((av[j][:, :], ins["L1_gnn_" + n].rearrange("o (a b) d -> (b d) (o a)", a=KH)))
                for j, n in enumerate(("pos_attn_src", "pos_attn_dst")):
                    loads.append((ap_[:, j:j + 1], ins["L1_gnn_" + n].rearrange("o a (d z) -> (o a d) z", z=1)))
                loads.append((comb[:, :, :], ins["L1_gnn_att_comb"].unsqueeze(0).broadcast_to([P, H, 2])))
                loads.append((be2[:, :], ins["L0_gnn_b_e2"].rearrange("(h p) -> p h", p=P)))
                for n, k in dict(b_le="L0_gnn_b_le", b_g1="L0_gnn_b_g1", b_g2="L0_gnn_b_g2", bl1="L2_gnn_bl1",
                                 bl2="L2_gnn_bl2", bl3="L2_gnn_bl3").items():
                    loads.append((rows_of[n][:, :], ins[k].unsqueeze(0).broadcast_to([P, D])))
                for n, k in dict(b_e1="L0_gnn_b_e1", ln_g="L0_gnn_ln_g", ln_b="L0_gnn_ln_b", b_rel="L3_gnn_b_rel",
                                 gamma="L3_gnn_gamma", beta="L3_gnn_beta").items():
                    loads.append((cols_of[n][:, :], ins[k].rearrange("(h p) -> p h", p=P)))
                (loaded, turned, copied, fused, v, vmade, vturned, made, c2made, spread) = sems(
                    "wt", "loaded turned copied fused v vmade vturned made c2made spread")
                order = ["W_le"] + [n for n in names if n != "W_le"]
                with nc.Block() as block:
                    @block.sync
                    def _(sp):
                        with nc.allow_non_contiguous_dma(reason="a few vectors by feature, once"):
                            for o, i in loads:
                                sp.dma_start(o, i).then_inc(loaded, 16)
                        sp.wait_ge(loaded, 16 * len(loads))

                    @block.gpsimd
                    def _(pool):
                        for k, (t, width) in enumerate(((hm_c[:, 0, :], DH), (hm_c[:, 1, :], DH), (hm_p[:, :], D4))):
                            base = P if k == 1 else 0
                            nc.gpsimd.memset(t, 1.0).then_inc(made, 1)
                            pool.wait_ge(made, 3 * k + 1)
                            nc.gpsimd.affine_select(out=t, in_=t, compare_op=ALU.is_ge, fill=0.0, base=base,
                                                    pattern=[[-width, H]], channel_multiplier=1).then_inc(made, 1)
                            pool.wait_ge(made, 3 * k + 2)
                            nc.gpsimd.affine_select(out=t, in_=t, compare_op=ALU.is_ge, fill=0.0,
                                                    base=width - 1 - base, pattern=[[width, H]],
                                                    channel_multiplier=-1).then_inc(made, 1)
                        pool.wait_ge(made, 9)

                    @block.vector
                    def _(dve):
                        nc.vector.memset(onesb[:, :], 1.0)
                        nc.vector.memset(we1[:, :, 0:1], 0.0)
                        nc.vector.memset(wpz[:, :], 0.0)
                        nc.vector.memset(wcz[:, :, :], 0.0).then_inc(spread, 1)
                        dve.wait_ge(loaded, 16 * len(loads))
                        dve.wait_ge(spread, 1)
                        nc.vector.tensor_copy(wpz[:, CD:D], wp_[:, :])
                        nc.vector.tensor_copy(wcz[:, :, 0:CD], wc[:, :, :])
                        for k in range(KH):
                            m = nc.vector.tensor_scalar(be2b[:, k, :], onesb[:, :], be2[:, k:k + 1], None, ALU.mult)
                        m.then_inc(spread, 1)
                        dve.wait_ge(made, 9)
                        for j in range(2):
                            for k in range(KH):
                                m = nc.vector.tensor_tensor(avm[:, k, j * H:(j + 1) * H], hm_c[:, k, :],
                                                            comb[:, :, 0], ALU.mult)
                            m = nc.vector.tensor_tensor(apm[:, j * H:(j + 1) * H], hm_p[:, :],
                                                        comb[0:H * D4, :, 1], ALU.mult)
                        m.then_inc(v, 1)
                        dve.wait_ge(v, 1)
                        for j in range(2):
                            for k in range(KH):
                                m = nc.vector.tensor_scalar(avm[:, k, j * H:(j + 1) * H], avm[:, k, j * H:(j + 1) * H],
                                                            av[j][:, k:k + 1], None, ALU.mult)
                            m = nc.vector.tensor_scalar(apm[:, j * H:(j + 1) * H], apm[:, j * H:(j + 1) * H],
                                                        ap_[:, j:j + 1], None, ALU.mult)
                        m.then_inc(v, 1)
                        for s, n in enumerate(order + ["Wc"]):
                            dest = wT["attn"][:, :, 0:D] if n == "Wc" else targets[n][:, :, :]
                            dve.wait_ge(turned, s + 1)
                            nc.vector.tensor_copy(dest, ps_w[s % 2][:, :].rearrange("p (h o) -> p h o", h=KH)
                                                  ).then_inc(copied, 1)
                        s = len(order) + 1
                        dve.wait_ge(turned, s + 1)
                        nc.vector.tensor_copy(w_e1T[:, :], ps_w[s % 2][0:65, 0:D]).then_inc(copied, 1)
                        dve.wait_ge(fused, 1)
                        for k in range(KH):
                            nc.vector.tensor_copy(wT["fuse"][:, k, :], ps_f[k][:, :])
                        nc.vector.tensor_copy(rows_of["c2"][:, :], ps_c[:, :])
                        dve.wait_ge(vmade, 1)
                        nc.vector.tensor_copy(vrow[:, :], ps_v[:, :]).then_inc(v, 1)
                        dve.wait_ge(vturned, 1)
                        nc.vector.tensor_copy(wT["attn"][:, :, D:D + 2 * H], ps_vt[:, :, :]).then_inc(v, 1)
                        dve.wait_ge(v, 4)

                    @block.tensor
                    def _(pe):
                        pe.wait_ge(loaded, 16 * len(loads))
                        pe.wait_ge(spread, 2)
                        for s, n in enumerate(order + ["Wc"]):
                            if s >= 2:
                                pe.wait_ge(copied, s - 1)
                            tile = wcz if n == "Wc" else raw[n]
                            for k in range(KH):
                                for a in range(KH):
                                    m = nc.tensor.transpose(ps_w[s % 2][:, k * D + a * P:k * D + (a + 1) * P],
                                                            tile[:, a, k * P:(k + 1) * P], ident[:, :])
                            m.then_inc(turned, 1)
                        s = len(order) + 1
                        pe.wait_ge(copied, s - 1)
                        for a in range(KH):
                            m = nc.tensor.transpose(ps_w[s % 2][0:65, a * P:(a + 1) * P], we1[:, a, :], ident[:, :])
                        m.then_inc(turned, 1)
                        for k in range(KH):
                            for a in range(KH):
                                nc.tensor.matmul(ps_f[k][:, :], we2[:, a, k * P:(k + 1) * P], w_leT[:, a, :],
                                                 start=(a == 0), stop=(a == KH - 1))
                        for a in range(KH):
                            m = nc.tensor.matmul(ps_c[:, :], be2b[:, a, :], w_leT[:, a, :], start=(a == 0),
                                                 stop=(a == KH - 1))
                        m.then_inc(fused, 1)
                        pe.wait_ge(v, 2)
                        for a in range(KH):
                            nc.tensor.matmul(ps_v[:, :], avm[:, a, :], wcz[:, a, :], start=(a == 0), stop=False)
                        nc.tensor.matmul(ps_v[:, :], apm[:, :], wpz[:, :], start=False, stop=True).then_inc(vmade, 1)
                        pe.wait_ge(v, 3)
                        for k in range(KH):
                            m = nc.tensor.transpose(ps_vt[:, k, :], vrow[:, k * P:(k + 1) * P],
                                                    ident[0:2 * H, 0:2 * H])
                        m.then_inc(vturned, 1)

        def first_table():
            with ExitStack() as scope:
                sb, ps = scoped(scope, "ft")
                xt = [sb(f"xt{i}", [P, D]) for i in range(4)]
                xb = [sb(f"xb{i}", [P, D]) for i in range(4)]
                ps_x = [ps(f"ps_x{i}", [P, KH, P]) for i in range(4)]
                added, turned, moved, cleared = sems("ft", "added turned moved cleared")
                loaded = sems("ft", "ld0 ld1 ld2 ld3")
                stored = sems("ft", "st0 st1 st2 st3")
                with nc.Block() as block:
                    @block.sync
                    def _(sp):
                        def load(t, s):
                            r = rows(t)
                            if later(t, 4):
                                sp.wait_ge(added, t - 3)
                                sp.wait_ge(turned, t - 3)
                            sp.dma_start(xt[s][0:r, :], ins["x"][bass.ds(t * P, r), :]).then_inc(loaded[s], 16)

                        def store(t, s):
                            r = rows(t)
                            sp.wait_ge(added, t + 1)
                            sp.dma_start(t_x0[bass.ds(t * P, r), :], xb[s][0:r, :]).then_inc(stored[s], 16)

                        pipelined(sp, NT, 4, [(0, load), (3, store)])
                        for s in range(4):
                            n = len(range(s, NT, 4))
                            if n:
                                sp.wait_ge(stored[s], 16 * n)

                    @block.vector
                    def _(dve):
                        def add(t, s):
                            r = rows(t)
                            dve.wait_ge(loaded[s], ((t - s) // 4 + 1) * 16 if isinstance(t, int) else (t - s) * 4 + 16)
                            if later(t, 4):
                                dve.wait_ge(stored[s], (t - s) // 4 * 16 if isinstance(t, int) else (t - s) * 4)
                            nc.vector.tensor_tensor(xb[s][0:r, :], xt[s][0:r, :], rows_of["b_le"][0:r, :],
                                                    ALU.add).then_inc(added, 1)
                        pipelined(dve, NT, 4, [(0, add)])

                    @block.tensor
                    def _(pe):
                        def turn(t, s):
                            r = rows(t)
                            pe.wait_ge(loaded[s], ((t - s) // 4 + 1) * 16 if isinstance(t, int) else (t - s) * 4 + 16)
                            if later(t, 4):
                                pe.wait_ge(moved, t - 3)
                            for k in range(KH):
                                m = nc.tensor.transpose(ps_x[s][:, k, 0:r], xt[s][0:r, k * P:(k + 1) * P],
                                                        ident[0:r, 0:r])
                            m.then_inc(turned, 1)
                        pipelined(pe, NT, 4, [(0, turn)])

                    @block.scalar
                    def _(act):
                        def move(t, s):
                            r = rows(t)
                            act.wait_ge(turned, t + 1)
                            nc.scalar.activation(agg[:, :, bass.ds(t * P, r)], ps_x[s][:, :, 0:r],
                                                 ACT.Copy).then_inc(moved, 1)
                        pipelined(act, NT, 4, [(0, move)])
                        act.wait_ge(moved, NT)

                    @block.gpsimd
                    def _(pool):
                        nc.gpsimd.memset(agg[:, :, N:NW], 0.0).then_inc(cleared, 1)
                        nc.gpsimd.memset(den, 0.0).then_inc(cleared, 1)
                        pool.wait_ge(cleared, 2)

        def edge_phase(tag, kind, table, width):
            mlp, attn = kind == "mlp", kind == "attn"
            with ExitStack() as scope:
                sb, ps = scoped(scope, tag)
                G = [sb(f"G{s}", [P, TI, width]) for s in range(RING)]
                oh = [sb(f"oh{i}", [P, TI, W]) for i in range(2)]
                xoh = sb("xoh", [P, TI, W])
                xrel = sb("xrel", [P, TI])
                ps_s = [ps(f"ps_s{i}", [P, KH + 1, W]) for i in range(2)]
                ps_x = ps("ps_x", [P, KH + 1, W])
                if mlp or attn:
                    msg = [sb(f"msg{i}", [P, TI, D]) for i in range(2)]
                if mlp:
                    attr = [sb(f"attr{i}", [P, TI, 65]) for i in range(2)]
                    attrT = [sb(f"attrT{i}", [65, GE]) for i in range(2)]
                    hid = [sb(f"hid{i}", [P, KH, GE]) for i in range(2)]
                    gate = [sb(f"gate{i}", [P, TI]) for i in range(2)]
                    emb = sb("emb", [P, TI, D])
                    ps_a = ps("ps_a", [65, GE])
                    ps_h = ps("ps_h", [P, KH, GE])
                    ps_e = ps("ps_e", [P, TI, D])
                if attn:
                    dstb = [sb(f"dstb{i}", [W, GE], I32) for i in range(2)]
                    bound = [sb(f"bound{i}", [H, GE + 1]) for i in range(2)]
                    dwin = [sb(f"dwin{i}", [W, H]) for i in range(2)]
                    dwinx = sb("dwinx", [W, H])
                    ohT = [sb(f"ohT{i}", [W, GE]) for i in range(2)]
                    ohTx = sb("ohTx", [W, GE])
                    nbx = sb("nbx", [W, 1])
                    logit = sb("logit", [H, GE])
                    logit2 = sb("logit2", [H, GE])
                    run = [sb(f"run{i}", [H, GE]) for i in range(2)]
                    top = sb("top", [H, GE])
                    below = sb("below", [H, GE])
                    ee = [sb(f"ee{i}", [H, GE]) for i in range(2)]
                    eeo = [sb(f"eeo{i}", [P, TI, H + 1]) for i in range(2)]
                    shift = sb("shift", [H, 1])
                    resc = [sb(f"resc{i}", [H, 1]) for i in range(2)]
                    floor = sb("floor", [H, 1])
                    ps_l = [ps(f"ps_l{i}", [H, GE]) for i in range(2)]
                    ps_ee = [ps(f"ps_ee{i}", [P, TI * H + KH]) for i in range(2)]
                gathered = sems(tag, "gathered0 gathered1 gathered2 gathered3")
                (indexed, onehot, summed, merged, xonehot, xsummed, xmerged, xv, xv2) = sems(
                    tag, "indexed onehot summed merged xonehot xsummed xmerged xv xv2")
                if kind == "weighted":
                    unweighted, = sems(tag, "unweighted")
                if mlp:
                    (turned, attred, hidden, relued, embedded, biased, gated, gated1, premsg, messaged) = sems(
                        tag, "turned attred hidden relued embedded biased gated gated1 premsg messaged")
                    attr_in = sems(tag, "attr_in0 attr_in1")
                if attn:
                    (windowed, expanded, scored, leaked, leaked2, ran, topped, belowed, exped, spreadee, eecopied,
                     messaged, shifted, rescaled, rmul, xdone, onesset, xnb, xohT, xd) = sems(
                        tag, "windowed expanded scored leaked leaked2 ran topped belowed exped spreadee eecopied "
                             "messaged shifted rescaled rmul xdone onesset xnb xohT xd")
                    edge_in = sems(tag, "edge_in0 edge_in1")
                    xwin, = sems(tag, "xwin")

                def per_slot(t, s, n, each):
                    return ((t - s) // n + 1) * each if isinstance(t, int) else (t - s) * (each // n) + each

                def operand(t, s):
                    return msg[s % 2] if mlp or attn else G[s]

                with nc.Block() as block:
                    @block.gpsimd
                    def _(pool):
                        def gather(g, s):
                            pool.wait_ge(indexed, g + 1)
                            if later(g, RING):
                                if mlp or attn:
                                    pool.wait_ge(messaged if attn else premsg, (g - RING + 1))
                                else:
                                    pool.wait_ge(summed, g - RING + 1)
                            pool.nop(nofuse=True)
                            for i in range(TI):
                                nc.gpsimd.indirect_dma_start(
                                    out=G[s][:, i, :], out_offset=None, in_=table,
                                    in_offset=bass.IndirectOffsetOnAxis(ap=idx[s][:, i:i + 1], axis=0),
                                ).then_inc(gathered[s], 16)
                        pipelined(pool, NG, RING, [(0, gather)])

                    @block.sync
                    def _(sp):
                        if mlp:
                            def load(g, s):
                                b = s % 2
                                if later(g, 2):
                                    sp.wait_ge(turned, g - 1)
                                    sp.wait_ge(gated1, g - 1)
                                n = TAILP if isinstance(g, int) and g == NG - 1 else P
                                src = ins["edge_attr_65"][bass.ds(g * GE, n * TI), :]
                                sp.dma_start(attr[b][0:n, :, :], src.rearrange("(p i) c -> p i c", i=TI)
                                             ).then_inc(attr_in[b], 16)
                            pipelined(sp, NG, 4, [(0, load)])
                        if attn:
                            def load(g, s):
                                b = s % 2
                                if later(g, 2):
                                    sp.wait_ge(expanded, g - 1)
                                    sp.wait_ge(topped, g - 1)
                                n = TAILP * TI if isinstance(g, int) and g == NG - 1 else GE
                                sp.dma_start(dstb[b][:, 0:n],
                                             ins["dst"][bass.ds(g * GE, n)].unsqueeze(0).broadcast_to([W, n])
                                             ).then_inc(edge_in[b], 16)
                                sp.dma_start(bound[b][:, 0:GE],
                                             t_flag[bass.ds(g, 1), :].broadcast_to([H, GE])
                                             ).then_inc(edge_in[b], 16)
                                first = first_dst(sp, g)
                                sp.dma_start(dwin[b][:, :], t_dst[bass.ds(first, W), :]).then_inc(edge_in[b], 16)
                                lo, hi = extra_lo(sp, g), extra_hi(sp, g)
                                with between(sp, lo, hi) as q:
                                    sp.wait_ge(xd, q + 1)
                                    at = bounded(sp, first + (q - lo + 1) * W, N)
                                    sp.dma_start(dwinx[:, :], t_dst[bass.ds(at, W), :]).then_inc(xwin, 16)
                            pipelined(sp, NG, 4, [(0, load)])

                    @block.vector
                    def _(dve):
                        def index(g, s):
                            if later(g, RING):
                                dve.wait_ge(gathered[s], per_slot(g - RING, s, RING, 64))
                            nc.vector.tensor_copy(idx[s][:, :], srcT[:, bass.ds(g * TI, TI)]).then_inc(indexed, 1)

                        def window(g, s):
                            b = s % 2
                            if later(g, 2):
                                dve.wait_ge(summed, g - 1)
                            rel = relT[:, bass.ds(g * TI, TI)]
                            m = nc.vector.tensor_tensor(
                                oh[b][:, :, :], rel.unsqueeze(2).broadcast_to([P, TI, W]),
                                iotaw[:, :].unsqueeze(1).broadcast_to([P, TI, W]), ALU.is_equal)
                            if kind == "weighted":
                                m.then_inc(unweighted, 1)
                                dve.wait_ge(unweighted, g + 1)
                                m = nc.vector.tensor_tensor(
                                    oh[b][:, :, :], oh[b][:, :, :],
                                    ewT[:, bass.ds(g * TI, TI)].unsqueeze(2).broadcast_to([P, TI, W]), ALU.mult)
                            m.then_inc(onehot, 1)

                        def further(g, s):
                            lo, hi = extra_lo(dve, g), extra_hi(dve, g)
                            first = first_dst(dve, g)
                            with between(dve, lo, hi) as q:
                                k = q - lo + 1
                                dve.wait_ge(xmerged, q * (2 if attn else 1) + 1)
                                nc.vector.tensor_scalar(xrel[:, :], relT[:, bass.ds(g * TI, TI)],
                                                        starts[:, bass.ds(bounded(dve, k, MAXX - 1), 1)],
                                                        None, ALU.subtract).then_inc(xv, 1)
                                dve.wait_ge(xv, q + 1)
                                m = nc.vector.tensor_tensor(
                                    xoh[:, :, :], xrel[:, :].unsqueeze(2).broadcast_to([P, TI, W]),
                                    iotaw[:, :].unsqueeze(1).broadcast_to([P, TI, W]), ALU.is_equal)
                                if kind != "weighted":
                                    m.then_inc(xonehot, 1)
                                else:
                                    m.then_inc(xv2, 1)
                                    dve.wait_ge(xv2, q + 1)
                                    nc.vector.tensor_tensor(
                                        xoh[:, :, :], xoh[:, :, :],
                                        ewT[:, bass.ds(g * TI, TI)].unsqueeze(2).broadcast_to([P, TI, W]),
                                        ALU.mult).then_inc(xonehot, 1)
                                dve.wait_ge(xsummed, q + 1)
                                at = bounded(dve, first + k * W, N)
                                nc.vector.tensor_tensor(agg[:, :, bass.ds(at, W)], agg[:, :, bass.ds(at, W)],
                                                        ps_x[:, 0:KH, :], ALU.add).then_inc(xmerged, 1)
                                if attn:
                                    nc.vector.tensor_tensor(den[:, bass.ds(at, W)], den[:, bass.ds(at, W)],
                                                            ps_x[0:H + 1, KH, :], ALU.add).then_inc(xmerged, 1)

                        def merge(g, s):
                            b = s % 2
                            first, hi = first_dst(dve, g), extra_hi(dve, g)
                            dve.wait_ge(summed, g + 1)
                            x2 = 2 if attn else 1
                            if later(g, 1):
                                dve.wait_ge(merged, g * x2)
                            dve.wait_ge(xmerged, hi * x2 + 1)
                            if attn:
                                dve.wait_ge(spreadee, g + 1)
                                nc.vector.tensor_tensor(agg[:, :, bass.ds(first, 1)], agg[:, :, bass.ds(first, 1)],
                                                        ps_ee[b][:, TI * H:TI * H + KH].unsqueeze(2),
                                                        ALU.mult).then_inc(rmul, 1)
                                nc.vector.tensor_tensor(den[0:H, bass.ds(first, 1)], den[0:H, bass.ds(first, 1)],
                                                        resc[b][:, :], ALU.mult).then_inc(rmul, 1)
                                dve.wait_ge(rmul, g * 2 + 2)
                            nc.vector.tensor_tensor(agg[:, :, bass.ds(first, W)], agg[:, :, bass.ds(first, W)],
                                                    ps_s[b][:, 0:KH, :], ALU.add).then_inc(merged, 1)
                            if attn:
                                nc.vector.tensor_tensor(den[:, bass.ds(first, W)], den[:, bass.ds(first, W)],
                                                        ps_s[b][0:H + 1, KH, :], ALU.add).then_inc(merged, 1)

                        def mlp_gate(g, s):
                            b = s % 2
                            dve.wait_ge(attr_in[b], per_slot(g, b, 2, 16) if isinstance(g, int)
                                        else (g - b) * 8 + 16)
                            if later(g, 2):
                                dve.wait_ge(premsg, g - 1)
                            nc.vector.tensor_scalar(gate[b][:, :], attr[b][:, :, 0], 0.0, 1.0, ALU.max,
                                                    ALU.min).then_inc(gated1, 1)
                            dve.wait_ge(gated1, g + 1)
                            nc.vector.tensor_scalar(gate[b][:, :], gate[b][:, :], 0.01, None,
                                                    ALU.add).then_inc(gated, 1)

                        def mlp_message(g, s):
                            b = s % 2
                            dve.wait_ge(embedded, g + 1)
                            if later(g, 1):
                                dve.wait_ge(premsg, g)
                            nc.vector.tensor_tensor(emb[:, :, :], ps_e[:, :, :],
                                                    rows_of["c2"][:, :].unsqueeze(1).broadcast_to([P, TI, D]),
                                                    ALU.add).then_inc(biased, 1)
                            dve.wait_ge(biased, g + 1)
                            dve.wait_ge(gated, g + 1)
                            dve.wait_ge(gathered[s], per_slot(g, s, RING, 64))
                            if later(g, 2):
                                dve.wait_ge(summed, g - 1)
                            for i in range(TI):
                                m = nc.vector.scalar_tensor_tensor(
                                    out=msg[b][:, i, :], in0=emb[:, i, :], scalar=gate[b][:, i:i + 1],
                                    in1=G[s][:, i, :], op0=ALU.mult, op1=ALU.add)
                            m.then_inc(premsg, 1)

                        def attn_expand(g, s):
                            b = s % 2
                            dve.wait_ge(edge_in[b], per_slot(g, b, 2, 48) if isinstance(g, int)
                                        else (g - b) * 24 + 48)
                            if later(g, 2):
                                dve.wait_ge(expanded, g - 1)
                            nc.vector.tensor_scalar(ohT[b][:, :], dstb[b][:, :], nbase[:, bass.ds(g, 1)], None,
                                                    ALU.is_equal).then_inc(windowed, 1)
                            lo, hi = extra_lo(dve, g), extra_hi(dve, g)
                            with between(dve, lo, hi) as q:
                                k = q - lo + 1
                                dve.wait_ge(xd, q + 1)
                                nc.vector.tensor_tensor(
                                    nbx[:, :], nbase[:, bass.ds(g, 1)],
                                    starts[0:W, bass.ds(bounded(dve, k, MAXX - 1), 1)],
                                    ALU.add).then_inc(xnb, 1)
                                dve.wait_ge(xnb, q + 1)
                                nc.vector.tensor_scalar(ohTx[:, :], dstb[b][:, :], nbx[:, :], None,
                                                        ALU.is_equal).then_inc(xohT, 1)

                        def attn_scan(g, s):
                            b = s % 2
                            dve.wait_ge(scored, g + 1)
                            if later(g, 1):
                                dve.wait_ge(belowed, g)
                            nc.vector.tensor_copy(logit[:, :], ps_l[b][:, :]).then_inc(leaked, 1)
                            dve.wait_ge(leaked, g + 1)
                            nc.vector.scalar_tensor_tensor(out=logit2[:, :], in0=logit[:, :], scalar=0.2,
                                                           in1=logit[:, :], op0=ALU.mult,
                                                           op1=ALU.max).then_inc(leaked2, 1)
                            dve.wait_ge(leaked2, g + 1)
                            prev = run[1 - b][:, GE - 1:GE] if later(g, 1) else floor[:, :]
                            if later(g, 1):
                                dve.wait_ge(ran, g)
                            nc.vector.tensor_tensor_scan(run[b][:, :], bound[b][:, 0:GE], logit2[:, :], prev,
                                                         ALU.min, ALU.max).then_inc(ran, 1)
                            dve.wait_ge(ran, g + 1)
                            nc.vector.tensor_tensor_scan(top[:, ::-1], bound[b][:, GE:0:-1], run[b][:, ::-1], -BIG,
                                                         ALU.min, ALU.max).then_inc(topped, 1)
                            dve.wait_ge(topped, g + 1)
                            if later(g, 2):
                                dve.wait_ge(rescaled, g - 1)
                            if later(g, 1):
                                dve.wait_ge(exped, g)
                            nc.vector.tensor_scalar(shift[:, :], prev, top[:, 0:1], 0.0, ALU.subtract,
                                                    ALU.min)
                            nc.vector.tensor_tensor(below[:, :], logit2[:, :], top[:, :],
                                                    ALU.subtract).then_inc(belowed, 1)

                        def attn_message(g, s):
                            b = s % 2
                            dve.wait_ge(spreadee, g + 1)
                            dve.wait_ge(gathered[s], per_slot(g, s, RING, 64))
                            if later(g, 2):
                                dve.wait_ge(summed, g - 1)
                            nc.vector.tensor_copy(eeo[b][:, :, 0:H],
                                                  ps_ee[b][:, 0:TI * H].rearrange("p (i h) -> p i h", h=H)
                                                  ).then_inc(eecopied, 1)
                            dve.wait_ge(eecopied, g + 1)
                            for i in range(TI):
                                m = nc.vector.tensor_tensor(
                                    msg[b][:, i, :].rearrange("p (h d) -> p h d", h=H),
                                    G[s][:, i, 0:D].rearrange("p (h d) -> p h d", h=H),
                                    eeo[b][:, i, 0:H].unsqueeze(2).broadcast_to([P, H, DH]), ALU.mult)
                            m.then_inc(messaged, 1)

                        nc.vector.memset(xrel[:, :], 0.0).then_inc(xmerged, 1)
                        if attn:
                            nc.vector.memset(nbx[:, :], 0.0).then_inc(xd, 1)
                            nc.vector.memset(eeo[0][:, :, H:H + 1], 1.0)
                            nc.vector.memset(eeo[1][:, :, H:H + 1], 1.0)
                            nc.vector.memset(floor[:, :], -BIG)
                            nc.vector.memset(bound[0][:, GE:GE + 1], BIG)
                            nc.vector.memset(bound[1][:, GE:GE + 1], BIG).then_inc(onesset, 1)
                            dve.wait_ge(onesset, 1)
                        for g in range(min(3, NG)):
                            index(g, g % RING)

                        def index_ahead(g, s):
                            if isinstance(g, int) and g + 3 >= NG:
                                return
                            index(g + 3, (s + 3) % RING)

                        if mlp:
                            stages = [(0, index_ahead), (0, window), (0, further), (0, mlp_gate), (0, mlp_message),
                                      (1, merge)]
                            stages = [(0, index_ahead), (0, mlp_gate), (0, window), (0, mlp_message), (1, merge),
                                      (0, further)]
                        elif attn:
                            stages = [(0, index_ahead), (0, attn_expand), (2, merge), (0, window), (0, attn_scan),
                                      (1, attn_message), (1, further)]
                        else:
                            stages = [(0, index_ahead), (0, window), (0, further), (1, merge)]
                        pipelined(dve, NG, RING, stages)
                        dve.wait_ge(merged, NG * (2 if attn else 1))

                    @block.tensor
                    def _(pe):
                        def segment_sum(o, m, w, slot_ee):
                            for k in range(KH):
                                for i in range(TI):
                                    last = nc.tensor.matmul(o[:, k, :], m[:, i, k * P:(k + 1) * P], w[:, i, :],
                                                            start=(i == 0), stop=(i == TI - 1))
                            if attn:
                                for i in range(TI):
                                    last = nc.tensor.matmul(o[0:H + 1, KH, :], slot_ee[:, i, :], w[:, i, :],
                                                            start=(i == 0), stop=(i == TI - 1))
                            return last

                        def summing(g, s):
                            b = s % 2
                            lo, hi = extra_lo(pe, g), extra_hi(pe, g)
                            if mlp or attn:
                                pe.wait_ge(messaged, g + 1)
                            else:
                                pe.wait_ge(gathered[s], per_slot(g, s, RING, 64))
                            pe.wait_ge(onehot, g + 1)
                            slot_ee = eeo[b] if attn else None
                            pe.nop(nofuse=True)
                            with between(pe, lo, hi) as q:
                                pe.wait_ge(xonehot, q + 1)
                                segment_sum(ps_x, operand(g, s), xoh, slot_ee).then_inc(xsummed, 1)
                            if later(g, 2):
                                pe.wait_ge(merged, (g - 1) * (2 if attn else 1))
                            segment_sum(ps_s[b], operand(g, s), oh[b], slot_ee).then_inc(summed, 1)

                        def mlp_turn(g, s):
                            b = s % 2
                            pe.wait_ge(attr_in[b], per_slot(g, b, 2, 16) if isinstance(g, int) else (g - b) * 8 + 16)
                            if later(g, 1):
                                pe.wait_ge(attred, g)
                            for i in range(TI):
                                m = nc.tensor.transpose(ps_a[:, i * P:(i + 1) * P], attr[b][:, i, :], ident[:, :])
                            m.then_inc(turned, 1)

                        def mlp_hidden(g, s):
                            b = s % 2
                            pe.wait_ge(attred, g + 1)
                            if later(g, 1):
                                pe.wait_ge(relued, g)
                            for k in range(KH):
                                m = nc.tensor.matmul(ps_h[:, k, :], w_e1T[:, k * P:(k + 1) * P], attrT[b][:, :],
                                                     start=True, stop=True)
                            m.then_inc(hidden, 1)

                        def mlp_embed(g, s):
                            b = s % 2
                            pe.wait_ge(relued, g + 1)
                            if later(g, 1):
                                pe.wait_ge(biased, g)
                            for i in range(TI):
                                for k in range(KH):
                                    m = nc.tensor.matmul(ps_e[:, i, :], hid[b][:, k, i * P:(i + 1) * P],
                                                         wT["fuse"][:, k, :], start=(k == 0), stop=(k == KH - 1))
                            m.then_inc(embedded, 1)

                        def attn_score(g, s):
                            b = s % 2
                            pe.wait_ge(windowed, g + 1)
                            pe.wait_ge(gathered[s], per_slot(g, s, RING, 64))
                            if later(g, 2):
                                pe.wait_ge(leaked, g - 1)
                            pe.nop(nofuse=True)
                            nc.tensor.matmul(ps_l[b][:, :], dwin[b][:, :], ohT[b][:, :], start=True,
                                             stop=False).then_inc(expanded, 1)
                            lo, hi = extra_lo(pe, g), extra_hi(pe, g)
                            with between(pe, lo, hi) as q:
                                pe.wait_ge(xohT, q + 1)
                                pe.wait_ge(xwin, q * 16 + 16)
                                pe.nop(nofuse=True)
                                nc.tensor.matmul(ps_l[b][:, :], dwinx[:, :], ohTx[:, :], start=False,
                                                 stop=False).then_inc(xd, 1)
                            ov = ps_l[b][:, :].rearrange("h (p i) -> h i p", i=TI)
                            for i in range(TI):
                                m = nc.tensor.matmul(ov[:, i, :], G[s][:, i, D:D + H], ident[:, :], start=False,
                                                     stop=(i == TI - 1))
                            m.then_inc(scored, 1)

                        def attn_spread(g, s):
                            b = s % 2
                            pe.wait_ge(exped, g + 1)
                            if later(g, 2):
                                pe.wait_ge(merged, (g - 1) * 2)
                            pe.nop(nofuse=True)
                            ev = ee[b][:, :].rearrange("h (p i) -> h i p", i=TI)
                            for i in range(TI):
                                nc.tensor.transpose(ps_ee[b][:, i * H:(i + 1) * H], ev[:, i, :], ident[0:H, 0:H])
                            for k in range(KH):
                                m = nc.tensor.matmul(ps_ee[b][:, TI * H + k:TI * H + k + 1],
                                                     headmask[:, k * P:(k + 1) * P], resc[b][:, :], start=True,
                                                     stop=True)
                            m.then_inc(spreadee, 1)

                        if mlp:
                            stages = [(0, mlp_turn), (2, summing), (1, mlp_embed), (0, mlp_hidden)]
                            pipelined(pe, NG, RING, stages)
                        elif attn:
                            pipelined(pe, NG, RING, [(0, attn_score), (1, attn_spread), (1, summing)])
                        else:
                            pipelined(pe, NG, RING, [(0, summing)])

                    @block.scalar
                    def _(act):
                        if mlp:
                            def attr_move(g, s):
                                b = s % 2
                                act.wait_ge(turned, g + 1)
                                if later(g, 2):
                                    act.wait_ge(hidden, g - 1)
                                nc.scalar.activation(attrT[b][:, :], ps_a[:, :], ACT.Copy).then_inc(attred, 1)

                            def relu_hidden(g, s):
                                b = s % 2
                                act.wait_ge(hidden, g + 1)
                                if later(g, 2):
                                    act.wait_ge(embedded, g - 1)
                                for k in range(KH):
                                    m = nc.scalar.activation(hid[b][:, k, :], ps_h[:, k, :], ACT.Relu,
                                                             bias=cols_of["b_e1"][:, k:k + 1])
                                m.then_inc(relued, 1)

                            def relu_message(g, s):
                                b = s % 2
                                act.wait_ge(premsg, g + 1)
                                nc.scalar.activation(msg[b][:, :, :], msg[b][:, :, :], ACT.Relu).then_inc(messaged, 1)

                            pipelined(act, NG, RING, [(0, attr_move), (0, relu_hidden), (1, relu_message)])
                        if attn:
                            def expo(g, s):
                                b = s % 2
                                act.wait_ge(belowed, g + 1)
                                if later(g, 2):
                                    act.wait_ge(spreadee, g - 1)
                                    act.wait_ge(merged, (g - 1) * 2)
                                nc.scalar.activation(resc[b][:, :], shift[:, :], ACT.Exp).then_inc(rescaled, 1)
                                nc.scalar.activation(ee[b][:, :], below[:, :], ACT.Exp).then_inc(exped, 1)
                            pipelined(act, NG, RING, [(0, expo)])

        def node_phase(tag, kind, resid=None, rtab=None, to=None, second=None):
            mlp, attn, sage, last = (kind == k for k in ("mlp", "attn", "sage", "sagelast"))
            anysage = sage or last
            weight = wT["W_g1"] if mlp else None
            if anysage:
                weight = wT[{"n2": "Wl1", "n3": "Wl2", "n4": "Wl3"}[tag]]
            nxt = wT[{"n0": "attn", "n1": "Wr1", "n2": "Wr2", "n3": "Wr3", "n4": "W_root"}[tag]]
            nbias = {"n1": "bl1", "n2": "bl2", "n3": "bl3"}.get(tag)
            NXW = D + 2 * H if mlp else D
            B = 4
            with ExitStack() as scope:
                sb, ps = scoped(scope, tag)
                st = [sb(f"st{i}", [P, KH, P]) for i in range(B)]
                rd = [sb(f"rd{i}", [P, D]) for i in range(B)]
                rs = [sb(f"rs{i}", [P, D]) for i in range(B)] if last else rd
                y = [sb(f"y{i}", [P, D]) for i in range(B)]
                e = [sb(f"e{i}", [P, D]) for i in range(B)]
                u = [sb(f"u{i}", [P, D]) for i in range(B)]
                hT = [sb(f"hT{i}", [P, KH, P]) for i in range(B)]
                outt = [sb(f"outt{i}", [P, NXW]) for i in range(B)]
                fin = [sb(f"fin{i}", [P, D]) for i in range(B)]
                stats = [sb(f"stats{i}", [P, 6]) for i in range(B)]
                mv = [sb(f"mv{i}", [P, 2]) for i in range(B)]
                sd = [sb(f"sd{i}", [P, 1]) for i in range(B)]
                rstd = [sb(f"rstd{i}", [P, 1]) for i in range(B)]
                dst_ = sb("dst_", [H + 1, P])
                dtile = [sb(f"dtile{i}", [P, H + 1]) for i in range(2)]
                rden = [sb(f"rden{i}", [P, H]) for i in range(2)]
                mlpT = [sb(f"mlpT{i}", [P, KH, P]) for i in range(2)]
                ps_a = [ps(f"ps_a{i}", [P, D]) for i in range(2)]
                ps_t = [ps(f"ps_t{i}", [P, KH, P]) for i in range(2)]
                ps_n = [ps(f"ps_n{i}", [P, 512]) for i in range(2)]
                ps_d = ps("ps_d", [P, H + 1])
                ps_m = ps("ps_m", [P, KH, P])
                (staged, summed, c, finished, turned, moved, nexted, outed, dstaged, dturned, biased,
                 root, mid, midmoved, first) = sems(
                    tag, "staged summed c finished turned moved nexted outed dstaged dturned biased root mid midmoved "
                         "first")
                sdone, = sems(tag, "sdone")
                loaded = sems(tag, "ld0 ld1 ld2 ld3")
                stored = sems(tag, "st0 st1 st2 st3")
                LD = 2 if last else 1
                ST = 3 if mlp else (1 if last else 2)

                CH = {"mlp": 9, "attn": 7, "sage": 2, "sagelast": 6}[kind]
                CE = 1
                CR = {"mlp": 3, "attn": 6, "sage": 0, "sagelast": 5}[kind]
                CR1 = 8

                def slot_count(t, s, each):
                    return ((t - s) // B + 1) * each if isinstance(t, int) else (t - s) * (each // B) + each

                with nc.Block() as block:
                    @block.sync
                    def _(sp):
                        def load(t, s):
                            r = rows(t)
                            if later(t, B):
                                sp.wait_ge(finished, t - B + 1)
                            if anysage:
                                sp.dma_start(rd[s][0:r, :], rtab[bass.ds(t * P, r), :]).then_inc(loaded[s], 16)
                            if not sage:
                                sp.dma_start(rs[s][0:r, :], resid[bass.ds(t * P, r), :]).then_inc(loaded[s], 16)

                        def store(t, s):
                            r = rows(t)
                            sp.wait_ge(finished, t + 1)
                            sp.dma_start(to[bass.ds(t * P, r), :], fin[s][0:r, :]).then_inc(stored[s], 16)
                            if mlp:
                                sp.wait_ge(outed, t + 1)
                                sp.dma_start(t_hc[bass.ds(t * P, r), :], outt[s][0:r, 0:HCW]).then_inc(stored[s], 16)
                                sp.dma_start(t_dst[bass.ds(t * P, r), :], outt[s][0:r, HCW:]).then_inc(stored[s], 16)
                            elif not last:
                                sp.wait_ge(outed, t + 1)
                                sp.dma_start(second[bass.ds(t * P, r), :], outt[s][0:r, :]).then_inc(stored[s], 16)
                        if mlp:
                            sp.wait_ge(first, 1)
                            sp.dma_start(t_dst[N:N + 2 * W, :], fin[0][:, 0:H]).then_inc(sdone, 16)
                            sp.wait_ge(sdone, 16)
                        pipelined(sp, NT, B, [(0, load), (3, store)])
                        for s in range(B):
                            n = len(range(s, NT, B))
                            if n:
                                sp.wait_ge(stored[s], 16 * n * ST)

                    @block.scalar
                    def _(act):
                        def stage(t, s):
                            r = rows(t)
                            if later(t, B):
                                act.wait_ge(summed, t - B + 1)
                            nc.scalar.activation(st[s][:, :, 0:r], agg[:, :, bass.ds(t * P, r)],
                                                 ACT.Copy).then_inc(staged, 1)
                            if attn:
                                if later(t, 1):
                                    act.wait_ge(dturned, t)
                                nc.scalar.activation(dst_[:, 0:r], den[:, bass.ds(t * P, r)],
                                                     ACT.Copy).then_inc(dstaged, 1)

                        def exp_(t, s):
                            r = rows(t)
                            act.wait_ge(c, CH * t + CE)
                            nc.scalar.activation(e[s][0:r, :], y[s][0:r, :], ACT.Exp).then_inc(biased, 1)

                        def root1(t, s, n=0):
                            r = rows(t)
                            act.wait_ge(c, CH * t + (CR1 if n else CR))
                            m = nc.scalar.activation(sd[s][0:r, :], mv[s][0:r, 1:2], ACT.Sqrt, bias=epsc[0:r, :])
                            m.then_inc(root, 1)

                        def root2(t, s):
                            root1(t, s, 1)

                        def mid_(t, s):
                            r = rows(t)
                            act.wait_ge(mid, t + 1)
                            for k in range(KH):
                                m = nc.scalar.activation(mlpT[s % 2][:, k, 0:r], ps_m[:, k, 0:r], ACT.Relu,
                                                         bias=cols_of["ln_b"][:, k:k + 1],
                                                         scale=cols_of["ln_g"][:, k:k + 1])
                            m.then_inc(midmoved, 1)

                        def move(t, s):
                            r = rows(t)
                            act.wait_ge(turned, t + 1)
                            if later(t, B):
                                act.wait_ge(nexted, t - B + 1)
                            nc.scalar.activation(hT[s][:, :, 0:r], ps_t[s % 2][:, :, 0:r], ACT.Copy).then_inc(moved, 1)

                        def out_(t, s):
                            r = rows(t)
                            act.wait_ge(nexted, t + 1)
                            if last:
                                nc.scalar.activation(aux[:, :, bass.ds(t * P, r)],
                                                     ps_n[s % 2][:, 0:D].rearrange("p (k n) -> p k n", k=KH)[:, :, 0:r],
                                                     ACT.Copy).then_inc(outed, 1)
                                return
                            if later(t, B):
                                act.wait_ge(stored[s], slot_count(t - B, s, 16 * ST) if isinstance(t, int)
                                            else (t - s) * (4 * ST))
                            nc.scalar.activation(outt[s][0:r, :], ps_n[s % 2][0:r, 0:NXW], ACT.Copy).then_inc(outed, 1)

                        if mlp:
                            pipelined(act, NT, B, [(0, stage), (1, root1), (1, mid_), (1, root2), (1, move), (1, out_)])
                        elif attn:
                            pipelined(act, NT, B, [(0, stage), (1, root1), (1, move)])
                        elif sage:
                            pipelined(act, NT, B, [(0, stage), (1, exp_), (1, move)])
                        else:
                            pipelined(act, NT, B, [(0, stage), (1, exp_), (1, root1), (1, move), (1, out_)])
                        if last or mlp:
                            act.wait_ge(outed, NT)

                    @block.vector
                    def _(dve):
                        def norm(t, s, src, dest, base, nroot):
                            r = rows(t)
                            nc.vector.bn_stats(stats[s][0:r, :], src[0:r, :]).then_inc(c, 1)
                            dve.wait_ge(c, CH * t + base + 1)
                            dve.nop(nofuse=True)
                            nc.vector.bn_aggr(mv[s][0:r, :], stats[s][0:r, :]).then_inc(c, 1)
                            dve.wait_ge(root, nroot)
                            nc.vector.reciprocal(rstd[s][0:r, :], sd[s][0:r, :]).then_inc(c, 1)
                            dve.wait_ge(c, CH * t + base + 3)
                            return nc.vector.tensor_scalar(dest[0:r, :], src[0:r, :], mv[s][0:r, 0:1],
                                                           rstd[s][0:r, :], ALU.subtract, ALU.mult)

                        def fin_free(t, s):
                            if later(t, B):
                                dve.wait_ge(stored[s], slot_count(t - B, s, 16 * ST) if isinstance(t, int)
                                            else (t - s) * (4 * ST))

                        def front(t, s):
                            r = rows(t)
                            b = s % 2
                            dve.wait_ge(loaded[s], slot_count(t, s, 16 * LD))
                            if mlp:
                                dve.wait_ge(summed, t + 1)
                                nc.vector.tensor_tensor(y[s][0:r, :], ps_a[b][0:r, :], rows_of["b_g1"][0:r, :],
                                                        ALU.add).then_inc(c, 1)
                                dve.wait_ge(c, CH * t + 1)
                                norm(t, s, y[s], u[s], 1, t * 2 + 1).then_inc(c, 1)
                            elif attn:
                                dve.wait_ge(dturned, t + 1)
                                dve.wait_ge(summed, t + 1)
                                nc.vector.tensor_scalar(dtile[b][0:r, 0:H], ps_d[0:r, 0:H], 1e-30, None, ALU.max)
                                nc.vector.tensor_scalar(dtile[b][0:r, H:H + 1], ps_d[0:r, H:H + 1], 1.0, None,
                                                        ALU.max).then_inc(c, 1)
                                dve.wait_ge(c, CH * t + 1)
                                nc.vector.reciprocal(rden[b][0:r, :], dtile[b][0:r, 0:H])
                                nc.vector.reciprocal(invdeg[0:r, bass.ds(t, 1)], dtile[b][0:r, H:H + 1]
                                                     ).then_inc(c, 1)
                                dve.wait_ge(c, CH * t + 2)
                                nc.vector.tensor_tensor(
                                    u[s][0:r, :].rearrange("p (h d) -> p h d", h=H),
                                    ps_a[b][0:r, :].rearrange("p (h d) -> p h d", h=H),
                                    rden[b][0:r, :].unsqueeze(2).broadcast_to([r, H, DH]), ALU.mult
                                ).then_inc(c, 1)
                                dve.wait_ge(c, CH * t + 3)
                                nc.vector.scalar_tensor_tensor(out=y[s][0:r, :], in0=rs[s][0:r, :], scalar=2.0,
                                                               in1=u[s][0:r, :], op0=ALU.mult, op1=ALU.add
                                                               ).then_inc(c, 1)
                                dve.wait_ge(c, CH * t + 4)
                                fin_free(t, s)
                                norm(t, s, y[s], fin[s], 4, t + 1).then_inc(finished, 1)
                            else:
                                dve.wait_ge(summed, t + 1)
                                nc.vector.scalar_tensor_tensor(out=y[s][0:r, :], in0=ps_a[b][0:r, :],
                                                               scalar=invdeg[0:r, bass.ds(t, 1)],
                                                               in1=rd[s][0:r, :], op0=ALU.mult, op1=ALU.add
                                                               ).then_inc(c, 1)
                                dve.wait_ge(c, CH * t + 1)
                                nc.vector.tensor_scalar(u[s][0:r, :], y[s][0:r, :], 0.0, -1.0, ALU.max,
                                                        ALU.add).then_inc(c, 1)
                                dve.wait_ge(c, CH * t + 2)
                                dve.wait_ge(biased, t + 1)
                                if sage:
                                    fin_free(t, s)
                                    nc.vector.scalar_tensor_tensor(out=fin[s][0:r, :], in0=e[s][0:r, :], scalar=1.0,
                                                                   in1=u[s][0:r, :], op0=ALU.min, op1=ALU.add
                                                                   ).then_inc(finished, 1)
                                else:
                                    nc.vector.scalar_tensor_tensor(out=y[s][0:r, :], in0=e[s][0:r, :], scalar=1.0,
                                                                   in1=u[s][0:r, :], op0=ALU.min, op1=ALU.add
                                                                   ).then_inc(c, 1)
                                    dve.wait_ge(c, CH * t + 3)
                                    nc.vector.tensor_tensor(u[s][0:r, :], y[s][0:r, :], rs[s][0:r, :], ALU.add
                                                            ).then_inc(c, 1)
                                    dve.wait_ge(c, CH * t + 4)
                                    fin_free(t, s)
                                    nc.vector.bn_stats(stats[s][0:r, :], u[s][0:r, :]).then_inc(first, 1)
                                    dve.wait_ge(first, t + 1)
                                    dve.nop(nofuse=True)
                                    nc.vector.bn_aggr(mv[s][0:r, :], stats[s][0:r, :]).then_inc(c, 1)
                                    dve.wait_ge(root, t + 1)
                                    nc.vector.reciprocal(rstd[s][0:r, :], sd[s][0:r, :]).then_inc(c, 1)
                                    dve.wait_ge(c, CH * t + 6)
                                    nc.vector.tensor_scalar(fin[s][0:r, :], u[s][0:r, :], mv[s][0:r, 0:1],
                                                            rstd[s][0:r, :], ALU.subtract, ALU.mult
                                                            ).then_inc(finished, 1)

                        def back(t, s):
                            r = rows(t)
                            b = s % 2
                            dve.wait_ge(biased, t + 1)
                            nc.vector.tensor_tensor(y[s][0:r, :], ps_a[b][0:r, :], rows_of["b_g2"][0:r, :],
                                                    ALU.add).then_inc(c, 1)
                            dve.wait_ge(c, CH * t + 6)
                            nc.vector.tensor_tensor(y[s][0:r, :], y[s][0:r, :], rs[s][0:r, :], ALU.add
                                                    ).then_inc(first, 1)
                            dve.wait_ge(first, t + 2)
                            fin_free(t, s)
                            nc.vector.bn_stats(stats[s][0:r, :], y[s][0:r, :]).then_inc(c, 1)
                            dve.wait_ge(c, CH * t + 7)
                            dve.nop(nofuse=True)
                            nc.vector.bn_aggr(mv[s][0:r, :], stats[s][0:r, :]).then_inc(c, 1)
                            dve.wait_ge(root, t * 2 + 2)
                            nc.vector.reciprocal(rstd[s][0:r, :], sd[s][0:r, :]).then_inc(c, 1)
                            dve.wait_ge(c, CH * t + 9)
                            nc.vector.tensor_scalar(fin[s][0:r, :], y[s][0:r, :], mv[s][0:r, 0:1], rstd[s][0:r, :],
                                                    ALU.subtract, ALU.mult).then_inc(finished, 1)

                        def addbias(t, s):
                            r = rows(t)
                            dve.wait_ge(nexted, t + 1)
                            if later(t, B):
                                dve.wait_ge(stored[s], slot_count(t - B, s, 16 * ST) if isinstance(t, int)
                                            else (t - s) * (4 * ST))
                            nc.vector.tensor_tensor(outt[s][0:r, :], ps_n[s % 2][0:r, 0:D], rows_of[nbias][0:r, :],
                                                    ALU.add).then_inc(outed, 1)

                        if mlp:
                            nc.vector.memset(fin[0][:, :], 0.0).then_inc(first, 1)
                            dve.wait_ge(sdone, 16)
                            pipelined(dve, NT, B, [(0, front), (0, back)])
                        elif last:
                            pipelined(dve, NT, B, [(0, front)])
                        else:
                            pipelined(dve, NT, B, [(0, front), (1, addbias)])

                    @block.tensor
                    def _(pe):
                        def product(o, lhs, w, r, width, sem):
                            for k in range(KH):
                                m = nc.tensor.matmul(o[0:r, 0:width], lhs[:, k, 0:r], w[:, k, 0:width],
                                                     start=(k == 0), stop=(k == KH - 1))
                            m.then_inc(sem, 1)

                        def sum_(t, s):
                            r = rows(t)
                            b = s % 2
                            pe.wait_ge(staged, t + 1)
                            if later(t, 2):
                                pe.wait_ge(finished, t - 1)
                            if attn:
                                pe.wait_ge(dstaged, t + 1)
                                if later(t, 1):
                                    pe.wait_ge(c, CH * t)
                                pe.nop(nofuse=True)
                                nc.tensor.transpose(ps_d[0:r, :], dst_[:, 0:r], ident[0:H + 1, 0:H + 1]
                                                    ).then_inc(dturned, 1)
                                for k in range(KH):
                                    m = nc.tensor.transpose(ps_a[b][0:r, k * P:(k + 1) * P], st[s][:, k, 0:r],
                                                            ident[:, :])
                                m.then_inc(summed, 1)
                            else:
                                product(ps_a[b], st[s], weight, r, D, summed)

                        def middle(t, s):
                            r = rows(t)
                            b = s % 2
                            pe.wait_ge(c, CH * t + 5)
                            for k in range(KH):
                                m = nc.tensor.transpose(ps_m[:, k, 0:r], u[s][0:r, k * P:(k + 1) * P],
                                                        ident[0:r, 0:r])
                            m.then_inc(mid, 1)
                            pe.wait_ge(midmoved, t + 1)
                            product(ps_a[b], mlpT[b], wT["W_g2"], r, D, biased)

                        def turn(t, s):
                            r = rows(t)
                            pe.wait_ge(finished, t + 1)
                            if later(t, 2):
                                pe.wait_ge(moved, t - 1)
                            for k in range(KH):
                                m = nc.tensor.transpose(ps_t[s % 2][:, k, 0:r], fin[s][0:r, k * P:(k + 1) * P],
                                                        ident[0:r, 0:r])
                            m.then_inc(turned, 1)
                            pe.wait_ge(moved, t + 1)
                            if later(t, 2):
                                pe.wait_ge(outed, t - 1)
                            if last:
                                for a in range(KH):
                                    for k in range(KH):
                                        m = nc.tensor.matmul(ps_n[s % 2][:, a * P:a * P + r],
                                                             nxt[:, k, a * P:(a + 1) * P], hT[s][:, k, 0:r],
                                                             start=(k == 0), stop=(k == KH - 1))
                                m.then_inc(nexted, 1)
                            else:
                                product(ps_n[s % 2], hT[s], nxt, r, NXW, nexted)

                        if mlp:
                            pipelined(pe, NT, B, [(0, sum_), (0, middle), (0, turn)])
                        else:
                            pipelined(pe, NT, B, [(0, sum_), (1, turn)])

        def clear_agg(tag):
            done, = sems(tag, "cleared")
            with nc.Block() as block:
                @block.vector
                def _(dve):
                    nc.vector.memset(agg[:, 0, :], 0.0).then_inc(done, 1)
                    dve.wait_ge(done, 2)

                @block.gpsimd
                def _(pool):
                    nc.gpsimd.memset(agg[:, 1, :], 0.0).then_inc(done, 1)

        def last_phase(tag):
            CW = 512
            NC_ = -(-N // CW)
            with ExitStack() as scope:
                sb, ps = scoped(scope, tag)
                stats = sb("bstats", [P, KH, NC_, 6])
                mv = sb("bmv", [P, KH, 2])
                sd = sb("bsd", [P, KH])
                scl = sb("scl", [P, KH])
                off = sb("off", [P, KH])
                ps_o = [[ps(f"ps_o{i}{a}", [P, CW]) for a in range(KH)] for i in range(2)]
                (prod, placed, v, rooted, normed) = sems(tag, "prod placed v rooted normed")
                with nc.Block() as block:
                    @block.tensor
                    def _(pe):
                        for c in range(NC_):
                            n = min(CW, N - c * CW)
                            if c >= 2:
                                pe.wait_ge(placed, (c - 1) * KH)
                            for a in range(KH):
                                for k in range(KH):
                                    m = nc.tensor.matmul(ps_o[c % 2][a][:, 0:n], wT["W_rel"][:, k, a * P:(a + 1) * P],
                                                         agg[:, k, c * CW:c * CW + n], start=(k == 0),
                                                         stop=(k == KH - 1))
                            m.then_inc(prod, 1)

                    @block.vector
                    def _(dve):
                        for c in range(NC_):
                            n = min(CW, N - c * CW)
                            dve.wait_ge(prod, c + 1)
                            for a in range(KH):
                                nc.vector.scalar_tensor_tensor(
                                    out=agg[:, a, c * CW:c * CW + n], in0=ps_o[c % 2][a][:, 0:n],
                                    scalar=cols_of["b_rel"][:, a:a + 1], in1=aux[:, a, c * CW:c * CW + n],
                                    op0=ALU.add, op1=ALU.add).then_inc(placed, 1)
                            dve.wait_ge(placed, (c + 1) * KH)
                            for a in range(KH):
                                m = nc.vector.bn_stats(stats[:, a, c, :], agg[:, a, c * CW:c * CW + n])
                        m.then_inc(v, 1)
                        dve.wait_ge(v, 1)
                        for a in range(KH):
                            m = nc.vector.bn_aggr(mv[:, a, :], stats[:, a, :, :])
                        m.then_inc(v, 1)
                        dve.wait_ge(rooted, 1)
                        nc.vector.reciprocal(scl[:, :], sd[:, :]).then_inc(v, 1)
                        dve.wait_ge(v, 3)
                        nc.vector.tensor_tensor(scl[:, :], scl[:, :], cols_of["gamma"][:, :], ALU.mult).then_inc(v, 1)
                        dve.wait_ge(v, 4)
                        nc.vector.tensor_tensor(off[:, :], mv[:, :, 0], scl[:, :], ALU.mult).then_inc(v, 1)
                        dve.wait_ge(v, 5)
                        nc.vector.tensor_tensor(off[:, :], cols_of["beta"][:, :], off[:, :],
                                                ALU.subtract).then_inc(v, 1)
                        dve.wait_ge(v, 6)

                    @block.scalar
                    def _(act):
                        act.wait_ge(v, 2)
                        nc.scalar.activation(sd[:, :], mv[:, :, 1], ACT.Sqrt, bias=epsc[:, :]).then_inc(rooted, 1)
                B = 4
                st = [sb(f"fst{i}", [P, KH, P]) for i in range(B)]
                xr = [sb(f"fx{i}", [P, D]) for i in range(B)]
                y = [sb(f"fy{i}", [P, D]) for i in range(B)]
                u = [sb(f"fu{i}", [P, D]) for i in range(B)]
                fin = [sb(f"ffin{i}", [P, D]) for i in range(B)]
                st6 = [sb(f"fs{i}", [P, 6]) for i in range(B)]
                mv2 = [sb(f"fm{i}", [P, 2]) for i in range(B)]
                sd2 = [sb(f"fd{i}", [P, 1]) for i in range(B)]
                rstd = [sb(f"fr{i}", [P, 1]) for i in range(B)]
                ps_f = [ps(f"ps_f{i}", [P, D]) for i in range(2)]
                staged, turned, c, root, finished = sems(tag, "staged turned c root finished")
                loaded = sems(tag, "fl0 fl1 fl2 fl3")
                stored = sems(tag, "fs0 fs1 fs2 fs3")

                def slot_count(t, s, each):
                    return ((t - s) // B + 1) * each if isinstance(t, int) else (t - s) * (each // B) + each

                with nc.Block() as block:
                    @block.sync
                    def _(sp):
                        def load(t, s):
                            r = rows(t)
                            if later(t, B):
                                sp.wait_ge(finished, t - B + 1)
                            sp.dma_start(xr[s][0:r, :], t_x3[bass.ds(t * P, r), :]).then_inc(loaded[s], 16)

                        def store(t, s):
                            r = rows(t)
                            sp.wait_ge(finished, t + 1)
                            sp.dma_start(out[bass.ds(t * P, r), :], fin[s][0:r, :]).then_inc(stored[s], 16)
                        pipelined(sp, NT, B, [(0, load), (3, store)])
                        for s in range(B):
                            n = len(range(s, NT, B))
                            if n:
                                sp.wait_ge(stored[s], 16 * n)

                    @block.scalar
                    def _(act):
                        def stage(t, s):
                            r = rows(t)
                            if later(t, B):
                                act.wait_ge(turned, t - B + 1)
                            for a in range(KH):
                                m = nc.scalar.activation(st[s][:, a, 0:r], agg[:, a, bass.ds(t * P, r)], ACT.Relu,
                                                         bias=off[:, a:a + 1], scale=scl[:, a:a + 1])
                            m.then_inc(staged, 1)

                        def root1(t, s):
                            r = rows(t)
                            act.wait_ge(c, t * 5 + 4)
                            nc.scalar.activation(sd2[s][0:r, :], mv2[s][0:r, 1:2], ACT.Sqrt,
                                                 bias=epsc[0:r, :]).then_inc(root, 1)
                        pipelined(act, NT, B, [(0, stage), (1, root1)])

                    @block.tensor
                    def _(pe):
                        def turn(t, s):
                            r = rows(t)
                            pe.wait_ge(staged, t + 1)
                            if later(t, 2):
                                pe.wait_ge(finished, t - 1)
                            for a in range(KH):
                                m = nc.tensor.transpose(ps_f[s % 2][0:r, a * P:(a + 1) * P], st[s][:, a, 0:r],
                                                        ident[:, :])
                            m.then_inc(turned, 1)
                        pipelined(pe, NT, B, [(0, turn)])

                    @block.vector
                    def _(dve):
                        def chain(t, s):
                            r = rows(t)
                            dve.wait_ge(turned, t + 1)
                            dve.wait_ge(loaded[s], slot_count(t, s, 16))
                            nc.vector.tensor_tensor(y[s][0:r, :], ps_f[s % 2][0:r, :], xr[s][0:r, :],
                                                    ALU.add).then_inc(c, 1)
                            dve.wait_ge(c, t * 5 + 1)
                            nc.vector.scalar_tensor_tensor(out=u[s][0:r, :], in0=y[s][0:r, :], scalar=0.0,
                                                           in1=xr[s][0:r, :], op0=ALU.max, op1=ALU.add).then_inc(c, 1)
                            dve.wait_ge(c, t * 5 + 2)
                            nc.vector.bn_stats(st6[s][0:r, :], u[s][0:r, :]).then_inc(c, 1)
                            dve.wait_ge(c, t * 5 + 3)
                            dve.nop(nofuse=True)
                            nc.vector.bn_aggr(mv2[s][0:r, :], st6[s][0:r, :]).then_inc(c, 1)
                            dve.wait_ge(root, t + 1)
                            nc.vector.reciprocal(rstd[s][0:r, :], sd2[s][0:r, :]).then_inc(c, 1)
                            dve.wait_ge(c, t * 5 + 5)
                            if later(t, B):
                                dve.wait_ge(stored[s], slot_count(t - B, s, 16) if isinstance(t, int)
                                            else (t - s) * 4)
                            nc.vector.tensor_scalar(fin[s][0:r, :], u[s][0:r, :], mv2[s][0:r, 0:1],
                                                    rstd[s][0:r, :], ALU.subtract, ALU.mult).then_inc(finished, 1)
                        pipelined(dve, NT, B, [(0, chain)])

        def copy_out(table):
            done, = sems("co", "copied_out")
            with nc.Block() as block:
                @block.sync
                def _(sp):
                    sp.dma_start(out, table).then_inc(done, 16)
                    sp.wait_ge(done, 16)

        phase(edge_tables)
        phase(weights)
        phase(first_table)
        phase(edge_phase, "e0", "mlp", t_x0, D)
        phase(node_phase, "n0", "mlp", resid=ins["x"], to=t_x1)
        if depth == 1:
            return copy_out(t_x1)
        phase(clear_agg, "z1")
        phase(edge_phase, "e1", "attn", t_hc, HCW)
        phase(node_phase, "n1", "attn", resid=t_x1, to=t_x2, second=t_r[0])
        if depth == 2:
            return copy_out(t_x2)
        phase(clear_agg, "z2")
        phase(edge_phase, "e2", "sum", t_x2, D)
        phase(node_phase, "n2", "sage", rtab=t_r[0], to=t_h1, second=t_r[1])
        phase(clear_agg, "z3")
        phase(edge_phase, "e3", "sum", t_h1, D)
        phase(node_phase, "n3", "sage", rtab=t_r[1], to=t_h2, second=t_r[2])
        phase(clear_agg, "z4")
        phase(edge_phase, "e4", "sum", t_h2, D)
        phase(node_phase, "n4", "sagelast", resid=t_x2, rtab=t_r[2], to=t_x3)
        if depth == 3:
            return copy_out(t_x3)
        phase(clear_agg, "z5")
        phase(edge_phase, "e5", "weighted", t_x3, D)
        phase(last_phase, "n5")


DEPTH = 4


def kernel(**inputs):
    import numpy as _np
    import concourse.bacc as _bacc
    from concourse import mybir as _mybir
    from concourse.bass_utils import run_bass_kernel_spmd as _run

    nc = _bacc.Bacc("TRN2", target_bir_lowering=False, num_devices=1)
    arrays, args = {}, {}
    for name, value in inputs.items():
        a = _np.ascontiguousarray(value)
        arrays[f"in_{name}_dram"] = a
        args[name] = nc.dram_tensor(f"in_{name}_dram", a.shape, _mybir.dt.from_np(a.dtype), kind="ExternalInput").ap()
    shape = inputs["x"].shape
    out = nc.dram_tensor("out_0_dram", shape, _mybir.dt.float32, kind="ExternalOutput").ap()
    gnn_kernel(nc, args, out, DEPTH)
    r = _run(nc, [arrays], core_ids=[0])
    return r.results[0]["out_0_dram"]
```

```python
import concourse.bass as bass
from concourse import mybir
from contextlib import ExitStack, contextmanager

FP32 = mybir.dt.float32
I32 = mybir.dt.int32
ALU = mybir.AluOpType
ACT = mybir.ActivationFunctionType
AX = mybir.AxisListType

P = 128
D = 256
KH = D // P
GE = 512
TI = GE // P
W = 64
WSHIFT = 6
H = 4
DH = D // H
RING = 6
ACT_TI = 2
BIG = 1.7e38
EPS = 1e-5
NOWHERE = -1.0e4


def pipelined(eng, count, unroll, stages):
    lags = max(lag for lag, _ in stages)
    ahead = max(0, -min(lag for lag, _ in stages))

    def step(turn, u):
        for lag, f in stages:
            t = turn * unroll + u - lag
            if isinstance(t, int) and not 0 <= t < count:
                continue
            f(t, (u - lag) % unroll, turn + (u - lag) // unroll)

    head = -(-(lags + unroll) // unroll)
    loops = max(0, (count - 1 - ahead) // unroll - head)
    if loops < 2:
        head, loops = 0, 0
    for s in range(-ahead, head * unroll):
        step(s // unroll, s % unroll)
    if loops:
        with eng.Fori(0, loops) as it:
            for u in range(unroll):
                step(it + head, u)
    for s in range((head + loops) * unroll, count + lags):
        step(s // unroll, s % unroll)


def came(s, v, ring, unroll, each):
    return (v * (unroll // ring) + s // ring + 1) * each


@contextmanager
def between(eng, lo, hi):
    with eng.If(lo < hi):
        with eng.Fori(lo, hi) as q:
            yield q


def later(t, n):
    return not isinstance(t, int) or t >= n


def gnn_kernel(nc, ins, out, depth):
    N = ins["x"].shape[0]
    E = ins["src"].shape[0]
    NG = -(-E // GE)
    TAILP = (E - GE * (NG - 1)) // TI
    NT = -(-N // P)
    LASTR = N - P * (NT - 1)
    NW = N + W + P
    HCW = D + H
    NKW = -(-N // W) + 1
    MAXX = NKW + 1

    def rows(t):
        return LASTR if isinstance(t, int) and t == NT - 1 else P

    ctx = ExitStack()
    taken = []

    def sems(tag, names):
        got = [nc.alloc_semaphore(f"{tag}_{n}") for n in names.split()]
        taken.extend(got)
        return got

    def phase(build, *args, **kwargs):
        build(*args, **kwargs)
        nc.clear_and_free_semaphores(taken)
        taken.clear()
        nc.all_engine_barrier()

    def scoped(scope, tag):
        def sb(name, shape, dt=FP32):
            return scope.enter_context(nc.sbuf_tensor(f"{tag}_{name}", shape, dt))

        def ps(name, shape):
            free = 1
            for n in shape[1:]:
                free *= n
            whole = scope.enter_context(nc.psum_tensor(f"{tag}_{name}", [P, -(-free // 512) * 512], FP32))
            flat = whole[0:shape[0], 0:free]
            if len(shape) == 3:
                return flat.rearrange("p (a b) -> p a b", b=shape[2])
            return flat
        return sb, ps

    def dram(name, shape, dt=FP32):
        return nc.dram_tensor(name, shape, dt, kind="Internal").ap()

    with ctx:
        sb, _ = scoped(ctx, "all")
        t_x0 = dram("t_x0", (N, D))
        t_hc = dram("t_hc", (N, HCW))
        t_dst = dram("t_dst", (N + W * 2, H))
        t_x1 = dram("t_x1", (N, D))
        t_x2 = dram("t_x2", (N, D))
        t_h1 = dram("t_h1", (N, D))
        t_h2 = dram("t_h2", (N, D))
        t_x3 = dram("t_x3", (N, D))
        t_r = [dram(f"t_r{i}", (N, D)) for i in range(3)]
        t_flag = dram("t_flag", (NG, GE))

        agg = sb("agg", [P, KH, NW])
        aux = sb("aux", [P, KH, NW])
        den = aux[0:H + 1, 0, :]
        srcT = sb("srcT", [P, NG * TI], I32)
        relT = sb("relT", [P, NG * TI])
        ewT = sb("ewT", [P, NG * TI])
        nbase = sb("nbase", [W, NG])
        starts = sb("starts", [P, MAXX])
        ctrl = sb("ctrl", [1, 2 * NG + 1], I32)
        c_first, c_extra = 0, NG
        iotaw = sb("iotaw", [P, W])
        ident = sb("ident", [P, P])
        ones = sb("ones", [1, P])
        epsc = sb("epsc", [P, 1])
        idx = [sb(f"idx{s}", [P, TI], I32) for s in range(RING)]
        invdeg = sb("invdeg", [P, NT])
        wT = {}
        for n in "Wl1 Wr1 Wl2 Wr2 Wl3 Wr3 W_rel W_root".split():
            wT[n] = sb("T" + n, [P, KH, D])
        rows_of = {}
        for n in "bl1 bl2 bl3".split():
            rows_of[n] = sb("R" + n, [P, D])
        cols_of = {}
        for n in "b_e1 ln_g ln_b b_rel gamma beta".split():
            cols_of[n] = sb("C" + n, [P, KH])
        headmask = sb("headmask", [H, D])
        layer0 = ExitStack()
        sb, _ = scoped(layer0, "l0")
        for n in "W_g1 W_g2 fuse".split():
            wT[n] = sb("T" + n, [P, KH, D])
        wT["attn"] = sb("Tattn", [P, KH, D + 2 * H])
        w_e1T = sb("w_e1T", [65, D])
        for n in "b_le c2 b_g1 b_g2".split():
            rows_of[n] = sb("R" + n, [P, D])

        def extra_lo(eng, g):
            return eng.value_load(ctrl[0:1, bass.ds(g + c_extra, 1)], min_val=0, max_val=NG * NKW)

        def extra_hi(eng, g):
            return eng.value_load(ctrl[0:1, bass.ds(g + c_extra + 1, 1)], min_val=0, max_val=NG * NKW)

        def bounded(eng, value, most):
            return eng.snap(value.with_bounds(min_val=0, max_val=most))

        def first_dst(eng, g):
            return eng.value_load(ctrl[0:1, bass.ds(g + c_first, 1)], min_val=0, max_val=N - 1)

        def edge_tables():
            with ExitStack() as scope:
                sb, ps = scoped(scope, "et")
                blocks = [(a, min(P, NG - a)) for a in range(0, NG, P)]
                NB = len(blocks)
                d_i = sb("d_i", [P, NB, GE], I32)
                q_i = sb("q_i", [P, NB, GE], I32)
                s_i = sb("s_i", [P, NB, GE], I32)
                w_f = sb("w_f", [P, NB, GE])
                d_f = sb("d_f", [P, NB, GE])
                q_f = sb("q_f", [P, NB, GE])
                s_f = sb("s_f", [P, NB, GE])
                flag = sb("flag", [P, NB, GE])
                last = sb("last", [P, NB])
                frow = sb("frow", [1, NG])
                lrow = sb("lrow", [1, NG])
                span = sb("span", [1, NG])
                spani = sb("spani", [1, NG], I32)
                spanf = sb("spanf", [1, NG])
                xrow = sb("xrow", [1, NG])
                zrow = sb("zrow", [1, NG])
                pidx = sb("pidx", [P, 1])
                ps_t = [ps(f"ps_t{i}", [P, 4, P]) for i in range(3)]
                ps_r = ps("ps_r", [1, 2, NG])
                ps_b = ps("ps_b", [P, NG])
                (filled, loaded, cast, lasted, turned, copied, rowed, v, flagged, based, made, consts, filled2,
                 bmade) = sems("et", "filled loaded cast lasted turned copied rowed v flagged based made consts filled2 bmade")
                made_flags, = sems("et", "made_flags")
                n_loads = 0
                for a, n in blocks:
                    full = min(a + n, NG - 1) - a
                    n_loads += 3 * ((full > 0) + (full < n)) + (a == 0) + (full > (1 if a == 0 else 0)) + (full < n)
                with nc.Block() as block:
                    @block.gpsimd
                    def _(pool):
                        nc.gpsimd.memset(ident[:, :], 0.0).then_inc(made, 1)
                        nc.gpsimd.iota(iotaw[:, :], [[1, W]], base=0, channel_multiplier=0,
                                       allow_small_or_imprecise_dtypes=True).then_inc(made, 1)
                        nc.gpsimd.iota(starts[:, :], [[W, MAXX]], base=0, channel_multiplier=0,
                                       allow_small_or_imprecise_dtypes=True).then_inc(made, 1)
                        nc.gpsimd.iota(pidx[:, :], [[0, 1]], base=0, channel_multiplier=1,
                                       allow_small_or_imprecise_dtypes=True).then_inc(made, 1)
                        nc.gpsimd.memset(headmask[:, :], 1.0).then_inc(made, 1)
                        pool.wait_ge(made, 5)
                        nc.gpsimd.affine_select(out=ident[:, :], in_=ident[:, :], compare_op=ALU.not_equal, fill=1.0,
                                                base=0, pattern=[[-1, P]], channel_multiplier=1).then_inc(consts, 1)
                        nc.gpsimd.affine_select(out=headmask[:, :], in_=headmask[:, :], compare_op=ALU.is_ge,
                                                fill=0.0, base=0, pattern=[[1, D]],
                                                channel_multiplier=-DH).then_inc(made, 1)
                        pool.wait_ge(made, 6)
                        nc.gpsimd.affine_select(out=headmask[:, :], in_=headmask[:, :], compare_op=ALU.is_ge,
                                                fill=0.0, base=DH - 1, pattern=[[-1, D]],
                                                channel_multiplier=DH).then_inc(consts, 1)
                        pool.wait_ge(consts, 2)

                    def grouped(dram_vec, a, n):
                        return dram_vec[a * GE:(a + n) * GE].rearrange("(g e) -> g e", e=GE)

                    @block.sync
                    def _(sp):
                        sp.wait_ge(filled, 1)
                        for b, (a, n) in enumerate(blocks):
                            full = min(a + n, NG - 1) - a
                            for tile, vec in ((d_i, ins["dst"]), (s_i, ins["src"]), (w_f, ins["edge_weight"])):
                                if full:
                                    sp.dma_start(tile[0:full, b, :], grouped(vec, a, full)).then_inc(loaded, 16)
                                if full < n:
                                    sp.dma_start(tile[full:n, b, 0:TAILP * TI],
                                                 vec[(a + full) * GE:E].rearrange("(g e) -> g e", g=1)
                                                 ).then_inc(loaded, 16)
                            lo = 1 if a == 0 else 0
                            if a == 0:
                                sp.dma_start(q_i[0:1, b, 1:GE],
                                             ins["dst"][0:GE - 1].rearrange("(g e) -> g e", g=1)).then_inc(loaded, 16)
                            if full > lo:
                                sp.dma_start(q_i[lo:full, b, :],
                                             ins["dst"][(a + lo) * GE - 1:(a + full) * GE - 1].rearrange(
                                                 "(g e) -> g e", e=GE)).then_inc(loaded, 16)
                            if full < n:
                                sp.dma_start(q_i[full:n, b, 0:TAILP * TI + 1],
                                             ins["dst"][(a + full) * GE - 1:E].rearrange("(g e) -> g e", g=1)
                                             ).then_inc(loaded, 16)
                        for b, (a, n) in enumerate(blocks):
                            sp.wait_ge(flagged, b + 1)
                            sp.dma_start(t_flag[a:a + n, :], flag[0:n, b, :]).then_inc(made_flags, 16)
                        sp.wait_ge(made_flags, 16 * NB)

                    @block.vector
                    def _(dve):
                        nc.vector.memset(d_i[:, :, :], int(NOWHERE))
                        nc.vector.memset(q_i[:, :, :], -1)
                        nc.vector.memset(s_i[:, :, :], 0)
                        nc.vector.memset(w_f[:, :, :], 0.0).then_inc(filled, 1)
                        nc.vector.memset(ones[:, :], 1.0)
                        nc.vector.memset(epsc[:, :], EPS)
                        nc.vector.memset(zrow[:, :], 0.0).then_inc(filled2, 1)
                        dve.wait_ge(loaded, 16 * n_loads)
                        nc.vector.tensor_copy(d_f[:, :, :], d_i[:, :, :]).then_inc(cast, 1)
                        nc.vector.tensor_copy(q_f[:, :, :], q_i[:, :, :]).then_inc(cast, 1)
                        nc.vector.tensor_copy(s_f[:, :, :], s_i[:, :, :]).then_inc(cast, 1)
                        dve.wait_ge(cast, 2)
                        nc.vector.tensor_reduce(last[:, :], d_f[:, :, :], AX.X, ALU.max).then_inc(lasted, 1)
                        nc.vector.tensor_tensor(flag[:, :, :], d_f[:, :, :], q_f[:, :, :],
                                                ALU.not_equal).then_inc(v, 1)
                        dve.wait_ge(v, 1)
                        for b in range(NB):
                            nc.vector.tensor_scalar(flag[:, b, :], flag[:, b, :], -2 * BIG, BIG, ALU.mult,
                                                    ALU.add).then_inc(flagged, 1)
                        dve.wait_ge(rowed, 1)
                        nc.vector.tensor_copy(frow[:, :], ps_r[0:1, 0, :]).then_inc(based, 1)
                        nc.vector.tensor_copy(lrow[:, :], ps_r[0:1, 1, :]).then_inc(v, 1)
                        dve.wait_ge(based, 1)
                        dve.wait_ge(v, 2)
                        nc.vector.tensor_copy(ctrl[0:1, 0:NG], frow[:, :])
                        nc.vector.tensor_tensor(span[:, :], lrow[:, :], frow[:, :], ALU.subtract).then_inc(v, 1)
                        dve.wait_ge(v, 3)
                        nc.vector.tensor_copy(spani[:, :], span[:, :]).then_inc(v, 1)
                        dve.wait_ge(v, 4)
                        nc.vector.tensor_scalar(spani[:, :], spani[:, :], WSHIFT, None,
                                                ALU.arith_shift_right).then_inc(v, 1)
                        dve.wait_ge(v, 5)
                        nc.vector.tensor_copy(spanf[:, :], spani[:, :]).then_inc(v, 1)
                        dve.wait_ge(v, 6)
                        dve.wait_ge(filled2, 1)
                        nc.vector.tensor_tensor_scan(xrow[:, :], spanf[:, :], zrow[:, :], 0.0, ALU.add,
                                                     ALU.add).then_inc(v, 1)
                        nc.vector.memset(ctrl[0:1, NG:NG + 1], 0)
                        dve.wait_ge(v, 7)
                        nc.vector.tensor_copy(ctrl[0:1, NG + 1:2 * NG + 1], xrow[:, :])
                        n_done = 0
                        for b, (a, n) in enumerate(blocks):
                            for k, dest in enumerate((relT, srcT, ewT)):
                                n_done += 1
                                dve.wait_ge(turned, n_done)
                                nc.vector.tensor_copy(
                                    dest[:, a * TI:(a + n) * TI].rearrange("p (g i) -> p i g", i=TI),
                                    ps_t[k][:, :, 0:n]).then_inc(copied, 1)
                        dve.wait_ge(bmade, 1)
                        dve.wait_ge(copied, 3 * NB)
                        rv = relT[:, :].rearrange("p (g i) -> p g i", i=TI)
                        nc.vector.tensor_tensor(rv, rv, ps_b[:, :].unsqueeze(2).broadcast_to([P, NG, TI]),
                                                ALU.subtract).then_inc(v, 1)
                        dve.wait_ge(consts, 2)
                        nc.vector.tensor_scalar(nbase[:, :], ps_b[0:W, :], pidx[0:W, :], None, ALU.add).then_inc(v, 1)
                        dve.wait_ge(v, 9)

                    @block.tensor
                    def _(pe):
                        pe.wait_ge(consts, 1)
                        pe.wait_ge(lasted, 1)
                        for b, (a, n) in enumerate(blocks):
                            nc.tensor.transpose(ps_r[0:1, 0, a:a + n], d_f[0:n, b, 0:1], ident[0:n, 0:n])
                            m = nc.tensor.transpose(ps_r[0:1, 1, a:a + n], last[0:n, b:b + 1], ident[0:n, 0:n])
                        m.then_inc(rowed, 1)
                        pe.wait_ge(cast, 3)
                        for b, (a, n) in enumerate(blocks):
                            if b:
                                pe.wait_ge(copied, 3 * b)
                            for k, tile in enumerate((d_f, s_f, w_f)):
                                tv = tile[0:n, b, :].rearrange("g (p i) -> g i p", i=TI)
                                for i in range(TI):
                                    m = nc.tensor.transpose(ps_t[k][:, i, 0:n], tv[:, i, :], ident[0:n, 0:n])
                                m.then_inc(turned, 1)
                        pe.wait_ge(based, 1)
                        pe.wait_ge(filled2, 1)
                        nc.tensor.matmul(ps_b[:, :], ones[0:1, :], frow[0:1, :], start=True, stop=True).then_inc(bmade, 1)

        def weights():
            with ExitStack() as scope:
                sb, ps = scoped(scope, "wt")
                names = dict(W_g1="L0_gnn_W_g1", W_g2="L0_gnn_W_g2", Wl1="L2_gnn_Wl1", Wr1="L2_gnn_Wr1",
                             Wl2="L2_gnn_Wl2", Wr2="L2_gnn_Wr2", Wl3="L2_gnn_Wl3", Wr3="L2_gnn_Wr3",
                             W_rel="L3_gnn_W_rel", W_root="L3_gnn_W_root", W_le="L0_gnn_W_le")
                raw = {n: sb("w" + n, [P, KH, D]) for n in names}
                w_leT = sb("w_leT", [P, KH, D])
                targets = {**{n: wT[n] for n in names if n != "W_le"}, "W_le": w_leT}
                we2 = sb("we2", [P, KH, D])
                we1 = sb("we1", [P, KH, 65])
                CD = ins["L1_gnn_Wc"].shape[1]
                POS = D - CD
                D4 = DH // 4
                wc = sb("wc", [P, KH, CD])
                wp_ = sb("wp", [H * D4, POS])
                av = [sb(f"av{j}", [P, KH]) for j in range(2)]
                ap_ = sb("ap", [H * D4, 2])
                avm = sb("avm", [P, KH, 2 * H])
                apm = sb("apm", [H * D4, 2 * H])
                hm_c = sb("hm_c", [P, KH, H])
                hm_p = sb("hm_p", [H * D4, H])
                comb = sb("comb", [P, H, 2])
                be2 = sb("be2", [P, KH])
                be2b = sb("be2b", [P, KH, P])
                vrow = sb("vrow", [2 * H, D])
                wpz = sb("wpz", [H * D4, D])
                wcz = sb("wcz", [P, KH, D])
                onesb = sb("onesb", [P, P])
                ps_w = [ps(f"ps_w{i}", [P, 512]) for i in range(2)]
                ps_f = [ps(f"ps_f{i}", [P, 256]) for i in range(2)]
                ps_c = ps("ps_c", [P, 256])
                ps_v = ps("ps_v", [2 * H, D])
                ps_vt = ps("ps_vt", [P, KH, 2 * H])
                loads = []
                for n, k in names.items():
                    loads.append((raw[n][:, :, :], ins[k].rearrange("(h p) c -> p h c", p=P)))
                loads.append((we2[:, :, :], ins["L0_gnn_W_e2"].rearrange("(h p) c -> p h c", p=P)))
                loads.append((we1[:, :, 1:65], ins["L0_gnn_W_e1"].rearrange("(h p) c -> p h c", p=P)))
                loads.append((wc[:, :, :], ins["L1_gnn_Wc"].rearrange("(h p) c -> p h c", p=P)))
                loads.append((wp_[:, :], ins["L1_gnn_Wp"]))
                for j, n in enumerate(("attn_src", "attn_dst")):
                    loads.append((av[j][:, :], ins["L1_gnn_" + n].rearrange("o (a b) d -> (b d) (o a)", a=KH)))
                for j, n in enumerate(("pos_attn_src", "pos_attn_dst")):
                    loads.append((ap_[:, j:j + 1], ins["L1_gnn_" + n].rearrange("o a (d z) -> (o a d) z", z=1)))
                loads.append((comb[:, :, :], ins["L1_gnn_att_comb"].unsqueeze(0).broadcast_to([P, H, 2])))
                loads.append((be2[:, :], ins["L0_gnn_b_e2"].rearrange("(h p) -> p h", p=P)))
                for n, k in dict(b_le="L0_gnn_b_le", b_g1="L0_gnn_b_g1", b_g2="L0_gnn_b_g2", bl1="L2_gnn_bl1",
                                 bl2="L2_gnn_bl2", bl3="L2_gnn_bl3").items():
                    loads.append((rows_of[n][:, :], ins[k].unsqueeze(0).broadcast_to([P, D])))
                for n, k in dict(b_e1="L0_gnn_b_e1", ln_g="L0_gnn_ln_g", ln_b="L0_gnn_ln_b", b_rel="L3_gnn_b_rel",
                                 gamma="L3_gnn_gamma", beta="L3_gnn_beta").items():
                    loads.append((cols_of[n][:, :], ins[k].rearrange("(h p) -> p h", p=P)))
                (loaded, turned, copied, fused, v, vmade, vturned, made, c2made, spread) = sems(
                    "wt", "loaded turned copied fused v vmade vturned made c2made spread")
                order = ["W_le"] + [n for n in names if n != "W_le"]
                with nc.Block() as block:
                    @block.sync
                    def _(sp):
                        with nc.allow_non_contiguous_dma(reason="a few vectors by feature, once"):
                            for o, i in loads:
                                sp.dma_start(o, i).then_inc(loaded, 16)
                        sp.wait_ge(loaded, 16 * len(loads))

                    @block.gpsimd
                    def _(pool):
                        for k, (t, width) in enumerate(((hm_c[:, 0, :], DH), (hm_c[:, 1, :], DH), (hm_p[:, :], D4))):
                            base = P if k == 1 else 0
                            nc.gpsimd.memset(t, 1.0).then_inc(made, 1)
                            pool.wait_ge(made, 3 * k + 1)
                            nc.gpsimd.affine_select(out=t, in_=t, compare_op=ALU.is_ge, fill=0.0, base=base,
                                                    pattern=[[-width, H]], channel_multiplier=1).then_inc(made, 1)
                            pool.wait_ge(made, 3 * k + 2)
                            nc.gpsimd.affine_select(out=t, in_=t, compare_op=ALU.is_ge, fill=0.0,
                                                    base=width - 1 - base, pattern=[[width, H]],
                                                    channel_multiplier=-1).then_inc(made, 1)
                        pool.wait_ge(made, 9)

                    @block.vector
                    def _(dve):
                        nc.vector.memset(onesb[:, :], 1.0)
                        nc.vector.memset(we1[:, :, 0:1], 0.0)
                        nc.vector.memset(wpz[:, :], 0.0)
                        nc.vector.memset(wcz[:, :, :], 0.0).then_inc(spread, 1)
                        dve.wait_ge(loaded, 16 * len(loads))
                        dve.wait_ge(spread, 1)
                        nc.vector.tensor_copy(wpz[:, CD:D], wp_[:, :])
                        nc.vector.tensor_copy(wcz[:, :, 0:CD], wc[:, :, :])
                        for k in range(KH):
                            m = nc.vector.tensor_scalar(be2b[:, k, :], onesb[:, :], be2[:, k:k + 1], None, ALU.mult)
                        m.then_inc(spread, 1)
                        dve.wait_ge(made, 9)
                        for j in range(2):
                            for k in range(KH):
                                m = nc.vector.tensor_tensor(avm[:, k, j * H:(j + 1) * H], hm_c[:, k, :],
                                                            comb[:, :, 0], ALU.mult)
                            m = nc.vector.tensor_tensor(apm[:, j * H:(j + 1) * H], hm_p[:, :],
                                                        comb[0:H * D4, :, 1], ALU.mult)
                        m.then_inc(v, 1)
                        dve.wait_ge(v, 1)
                        for j in range(2):
                            for k in range(KH):
                                m = nc.vector.tensor_scalar(avm[:, k, j * H:(j + 1) * H], avm[:, k, j * H:(j + 1) * H],
                                                            av[j][:, k:k + 1], None, ALU.mult)
                            m = nc.vector.tensor_scalar(apm[:, j * H:(j + 1) * H], apm[:, j * H:(j + 1) * H],
                                                        ap_[:, j:j + 1], None, ALU.mult)
                        m.then_inc(v, 1)
                        for s, n in enumerate(order + ["Wc"]):
                            dest = wT["attn"][:, :, 0:D] if n == "Wc" else targets[n][:, :, :]
                            dve.wait_ge(turned, s + 1)
                            nc.vector.tensor_copy(dest, ps_w[s % 2][:, :].rearrange("p (h o) -> p h o", h=KH)
                                                  ).then_inc(copied, 1)
                        s = len(order) + 1
                        dve.wait_ge(turned, s + 1)
                        nc.vector.tensor_copy(w_e1T[:, :], ps_w[s % 2][0:65, 0:D]).then_inc(copied, 1)
                        dve.wait_ge(fused, 1)
                        for k in range(KH):
                            nc.vector.tensor_copy(wT["fuse"][:, k, :], ps_f[k][:, :])
                        nc.vector.tensor_copy(rows_of["c2"][:, :], ps_c[:, :])
                        dve.wait_ge(vmade, 1)
                        nc.vector.tensor_copy(vrow[:, :], ps_v[:, :]).then_inc(v, 1)
                        dve.wait_ge(vturned, 1)
                        nc.vector.tensor_copy(wT["attn"][:, :, D:D + 2 * H], ps_vt[:, :, :]).then_inc(v, 1)
                        dve.wait_ge(v, 4)

                    @block.tensor
                    def _(pe):
                        pe.wait_ge(loaded, 16 * len(loads))
                        pe.wait_ge(spread, 2)
                        for s, n in enumerate(order + ["Wc"]):
                            if s >= 2:
                                pe.wait_ge(copied, s - 1)
                            tile = wcz if n == "Wc" else raw[n]
                            for k in range(KH):
                                for a in range(KH):
                                    m = nc.tensor.transpose(ps_w[s % 2][:, k * D + a * P:k * D + (a + 1) * P],
                                                            tile[:, a, k * P:(k + 1) * P], ident[:, :])
                            m.then_inc(turned, 1)
                        s = len(order) + 1
                        pe.wait_ge(copied, s - 1)
                        for a in range(KH):
                            m = nc.tensor.transpose(ps_w[s % 2][0:65, a * P:(a + 1) * P], we1[:, a, :], ident[:, :])
                        m.then_inc(turned, 1)
                        for k in range(KH):
                            for a in range(KH):
                                nc.tensor.matmul(ps_f[k][:, :], we2[:, a, k * P:(k + 1) * P], w_leT[:, a, :],
                                                 start=(a == 0), stop=(a == KH - 1))
                        for a in range(KH):
                            m = nc.tensor.matmul(ps_c[:, :], be2b[:, a, :], w_leT[:, a, :], start=(a == 0),
                                                 stop=(a == KH - 1))
                        m.then_inc(fused, 1)
                        pe.wait_ge(v, 2)
                        for a in range(KH):
                            nc.tensor.matmul(ps_v[:, :], avm[:, a, :], wcz[:, a, :], start=(a == 0), stop=False)
                        nc.tensor.matmul(ps_v[:, :], apm[:, :], wpz[:, :], start=False, stop=True).then_inc(vmade, 1)
                        pe.wait_ge(v, 3)
                        for k in range(KH):
                            m = nc.tensor.transpose(ps_vt[:, k, :], vrow[:, k * P:(k + 1) * P],
                                                    ident[0:2 * H, 0:2 * H])
                        m.then_inc(vturned, 1)

        def first_table():
            with ExitStack() as scope:
                sb, ps = scoped(scope, "ft")
                xt = [sb(f"xt{i}", [P, D]) for i in range(4)]
                xb = [sb(f"xb{i}", [P, D]) for i in range(4)]
                ps_x = [ps(f"ps_x{i}", [P, KH, P]) for i in range(4)]
                added, turned, moved, cleared = sems("ft", "added turned moved cleared")
                loaded = sems("ft", "ld0 ld1 ld2 ld3")
                stored = sems("ft", "st0 st1 st2 st3")
                with nc.Block() as block:
                    @block.sync
                    def _(sp):
                        def load(t, s, v):
                            r = rows(t)
                            if later(t, 4):
                                sp.wait_ge(added, t - 3)
                                sp.wait_ge(turned, t - 3)
                            sp.dma_start(xt[s][0:r, :], ins["x"][bass.ds(t * P, r), :]).then_inc(loaded[s], 16)

                        def store(t, s, v):
                            r = rows(t)
                            sp.wait_ge(added, t + 1)
                            sp.dma_start(t_x0[bass.ds(t * P, r), :], xb[s][0:r, :]).then_inc(stored[s], 16)

                        pipelined(sp, NT, 4, [(0, load), (3, store)])
                        for s in range(4):
                            n = len(range(s, NT, 4))
                            if n:
                                sp.wait_ge(stored[s], 16 * n)

                    @block.vector
                    def _(dve):
                        def add(t, s, v):
                            r = rows(t)
                            dve.wait_ge(loaded[s], (v + 1) * 16)
                            if later(t, 4):
                                dve.wait_ge(stored[s], v * 16)
                            nc.vector.tensor_tensor(xb[s][0:r, :], xt[s][0:r, :], rows_of["b_le"][0:r, :],
                                                    ALU.add).then_inc(added, 1)
                        pipelined(dve, NT, 4, [(0, add)])

                    @block.tensor
                    def _(pe):
                        def turn(t, s, v):
                            r = rows(t)
                            pe.wait_ge(loaded[s], (v + 1) * 16)
                            if later(t, 4):
                                pe.wait_ge(moved, t - 3)
                            for k in range(KH):
                                m = nc.tensor.transpose(ps_x[s][:, k, 0:r], xt[s][0:r, k * P:(k + 1) * P],
                                                        ident[0:r, 0:r])
                            m.then_inc(turned, 1)
                        pipelined(pe, NT, 4, [(0, turn)])

                    @block.scalar
                    def _(act):
                        def move(t, s, v):
                            r = rows(t)
                            act.wait_ge(turned, t + 1)
                            nc.scalar.activation(agg[:, :, bass.ds(t * P, r)], ps_x[s][:, :, 0:r],
                                                 ACT.Copy).then_inc(moved, 1)
                        pipelined(act, NT, 4, [(0, move)])
                        act.wait_ge(moved, NT)

                    @block.gpsimd
                    def _(pool):
                        nc.gpsimd.memset(agg[:, :, N:NW], 0.0).then_inc(cleared, 1)
                        nc.gpsimd.memset(den, 0.0).then_inc(cleared, 1)
                        pool.wait_ge(cleared, 2)

        def edge_phase(tag, kind, table, width):
            mlp, attn = kind == "mlp", kind == "attn"
            with ExitStack() as scope:
                sb, ps = scoped(scope, tag)
                G = [sb(f"G{s}", [P, TI, width]) for s in range(RING)]
                oh = [sb(f"oh{i}", [P, TI, W]) for i in range(2)]
                xoh = sb("xoh", [P, TI, W])
                xrel = sb("xrel", [P, TI])
                ps_s = [ps(f"ps_s{i}", [P, KH + 1, W]) for i in range(2)]
                ps_x = ps("ps_x", [P, KH + 1, W])
                if mlp or attn:
                    msg = [sb(f"msg{i}", [P, TI, D]) for i in range(2)]
                if mlp:
                    attr = [sb(f"attr{i}", [P, TI, 65]) for i in range(2)]
                    attrT = [sb(f"attrT{i}", [65, GE]) for i in range(2)]
                    hid = [sb(f"hid{i}", [P, KH, GE]) for i in range(2)]
                    gate = [sb(f"gate{i}", [P, TI]) for i in range(2)]
                    emb = sb("emb", [P, TI, D])
                    ps_a = ps("ps_a", [65, GE])
                    ps_h = ps("ps_h", [P, KH, GE])
                    ps_e = ps("ps_e", [P, TI, D])
                if attn:
                    dstb = [sb(f"dstb{i}", [W, GE], I32) for i in range(3)]
                    bound = [sb(f"bound{i}", [H, GE + 1]) for i in range(3)]
                    dwin = [sb(f"dwin{i}", [W, H]) for i in range(3)]
                    dwinx = sb("dwinx", [W, H])
                    ohT = [sb(f"ohT{i}", [W, GE]) for i in range(2)]
                    ohTx = sb("ohTx", [W, GE])
                    nbx = sb("nbx", [W, 1])
                    leaky = [sb(f"leaky{i}", [H, GE]) for i in range(2)]
                    run = [sb(f"run{i}", [H, GE]) for i in range(2)]
                    top = sb("top", [H, GE])
                    ee = [sb(f"ee{i}", [H, GE]) for i in range(2)]
                    eeo = [sb(f"eeo{i}", [P, TI, H + 1]) for i in range(2)]
                    shift = sb("shift", [H, 1])
                    resc = [sb(f"resc{i}", [H, 1]) for i in range(3)]
                    floor = sb("floor", [H, 1])
                    ps_l = [ps(f"ps_l{i}", [H, GE]) for i in range(2)]
                    ps_ee = [ps(f"ps_ee{i}", [P, TI * H + KH]) for i in range(2)]
                gathered = sems(tag, " ".join(f"gathered{s}" for s in range(RING)))
                (indexed, onehot, summed, merged, xonehot, xsummed, xmerged, xv, xv2) = sems(
                    tag, "indexed onehot summed merged xonehot xsummed xmerged xv xv2")
                if kind == "weighted":
                    unweighted, = sems(tag, "unweighted")
                if mlp:
                    (turned, attred, hidden, relued, embedded, biased, gated, gated1, premsg, messaged) = sems(
                        tag, "turned attred hidden relued embedded biased gated gated1 premsg messaged")
                    attr_in = sems(tag, "attr_in0 attr_in1")
                if attn:
                    (windowed, expanded, scored, scaled, leaked, messaged_a, ran, topped, belowed, exped, spreadee, eecopied,
                     messaged, shifted, rescaled, rmul, xdone, onesset, xnb, xohT, xd) = sems(
                        tag, "windowed expanded scored scaled leaked messaged_a ran topped belowed exped spreadee eecopied "
                             "messaged shifted rescaled rmul xdone onesset xnb xohT xd")
                    edge_in = sems(tag, "edge_in0 edge_in1 edge_in2")
                    xwin, = sems(tag, "xwin")

                def operand(g, s):
                    return msg[s % 2] if mlp or attn else G[s]

                with nc.Block() as block:
                    @block.gpsimd
                    def _(pool):
                        def gather(g, s, v):
                            pool.wait_ge(indexed, g + 1)
                            if later(g, RING):
                                if mlp or attn:
                                    pool.wait_ge(messaged if attn else premsg, (g - RING + 1))
                                    if attn:
                                        pool.wait_ge(messaged_a, (g - RING + 1))
                                else:
                                    pool.wait_ge(summed, g - RING + 1)
                            pool.nop(nofuse=True)
                            for i in range(TI):
                                nc.gpsimd.indirect_dma_start(
                                    out=G[s][:, i, :], out_offset=None, in_=table,
                                    in_offset=bass.IndirectOffsetOnAxis(ap=idx[s][:, i:i + 1], axis=0),
                                ).then_inc(gathered[s], 16)
                        pipelined(pool, NG, RING, [(0, gather)])

                    @block.sync
                    def _(sp):
                        if mlp:
                            def load(g, s, v):
                                b = s % 2
                                if later(g, 2):
                                    sp.wait_ge(turned, g - 1)
                                    sp.wait_ge(gated1, g - 1)
                                n = TAILP if isinstance(g, int) and g == NG - 1 else P
                                src = ins["edge_attr_65"][bass.ds(g * GE, n * TI), :]
                                sp.dma_start(attr[b][0:n, :, :], src.rearrange("(p i) c -> p i c", i=TI)
                                             ).then_inc(attr_in[b], 16)
                            pipelined(sp, NG, RING, [(0, load)])
                        if attn:
                            def load(g, s, v):
                                b = s % 3
                                if later(g, 3):
                                    sp.wait_ge(expanded, g - 2)
                                    sp.wait_ge(topped, g - 2)
                                n = TAILP * TI if isinstance(g, int) and g == NG - 1 else GE
                                sp.dma_start(dstb[b][:, 0:n],
                                             ins["dst"][bass.ds(g * GE, n)].unsqueeze(0).broadcast_to([W, n])
                                             ).then_inc(edge_in[b], 16)
                                sp.dma_start(bound[b][:, 0:GE],
                                             t_flag[bass.ds(g, 1), :].broadcast_to([H, GE])
                                             ).then_inc(edge_in[b], 16)
                                first = first_dst(sp, g)
                                sp.dma_start(dwin[b][:, :], t_dst[bass.ds(first, W), :]).then_inc(edge_in[b], 16)
                                lo, hi = extra_lo(sp, g), extra_hi(sp, g)
                                with between(sp, lo, hi) as q:
                                    sp.wait_ge(xd, q + 1)
                                    at = bounded(sp, first + (q - lo + 1) * W, N)
                                    sp.dma_start(dwinx[:, :], t_dst[bass.ds(at, W), :]).then_inc(xwin, 16)
                            pipelined(sp, NG, RING, [(0, load)])

                    @block.vector
                    def _(dve):
                        def index(g, s, v):
                            if later(g, RING):
                                dve.wait_ge(gathered[s], v * 64)
                            nc.vector.tensor_copy(idx[s][:, :], srcT[:, bass.ds(g * TI, TI)]).then_inc(indexed, 1)

                        def window(g, s, v):
                            b = s % 2
                            if later(g, 2):
                                dve.wait_ge(summed, g - 1)
                            rel = relT[:, bass.ds(g * TI, TI)]
                            m = nc.vector.tensor_tensor(
                                oh[b][:, :, :], rel.unsqueeze(2).broadcast_to([P, TI, W]),
                                iotaw[:, :].unsqueeze(1).broadcast_to([P, TI, W]), ALU.is_equal)
                            if kind == "weighted":
                                m.then_inc(unweighted, 1)
                                dve.wait_ge(unweighted, g + 1)
                                m = nc.vector.tensor_tensor(
                                    oh[b][:, :, :], oh[b][:, :, :],
                                    ewT[:, bass.ds(g * TI, TI)].unsqueeze(2).broadcast_to([P, TI, W]), ALU.mult)
                            m.then_inc(onehot, 1)

                        def further(g, s, v):
                            lo, hi = extra_lo(dve, g), extra_hi(dve, g)
                            first = first_dst(dve, g)
                            with between(dve, lo, hi) as q:
                                k = q - lo + 1
                                dve.wait_ge(xmerged, q * (2 if attn else 1) + 1)
                                nc.vector.tensor_scalar(xrel[:, :], relT[:, bass.ds(g * TI, TI)],
                                                        starts[:, bass.ds(bounded(dve, k, MAXX - 1), 1)],
                                                        None, ALU.subtract).then_inc(xv, 1)
                                dve.wait_ge(xv, q + 1)
                                m = nc.vector.tensor_tensor(
                                    xoh[:, :, :], xrel[:, :].unsqueeze(2).broadcast_to([P, TI, W]),
                                    iotaw[:, :].unsqueeze(1).broadcast_to([P, TI, W]), ALU.is_equal)
                                if kind != "weighted":
                                    m.then_inc(xonehot, 1)
                                else:
                                    m.then_inc(xv2, 1)
                                    dve.wait_ge(xv2, q + 1)
                                    nc.vector.tensor_tensor(
                                        xoh[:, :, :], xoh[:, :, :],
                                        ewT[:, bass.ds(g * TI, TI)].unsqueeze(2).broadcast_to([P, TI, W]),
                                        ALU.mult).then_inc(xonehot, 1)
                                dve.wait_ge(xsummed, q + 1)
                                at = bounded(dve, first + k * W, N)
                                nc.vector.tensor_tensor(agg[:, :, bass.ds(at, W)], agg[:, :, bass.ds(at, W)],
                                                        ps_x[:, 0:KH, :], ALU.add).then_inc(xmerged, 1)
                                if attn:
                                    nc.vector.tensor_tensor(den[:, bass.ds(at, W)], den[:, bass.ds(at, W)],
                                                            ps_x[0:H + 1, KH, :], ALU.add).then_inc(xmerged, 1)

                        def merge(g, s, v):
                            b = s % 2
                            first, hi = first_dst(dve, g), extra_hi(dve, g)
                            dve.wait_ge(summed, g + 1)
                            x2 = 2 if attn else 1
                            if later(g, 1):
                                dve.wait_ge(merged, g * x2)
                            dve.wait_ge(xmerged, hi * x2 + 1)
                            if attn:
                                dve.wait_ge(spreadee, g + 1)
                                nc.vector.tensor_tensor(agg[:, :, bass.ds(first, 1)], agg[:, :, bass.ds(first, 1)],
                                                        ps_ee[b][:, TI * H:TI * H + KH].unsqueeze(2),
                                                        ALU.mult).then_inc(rmul, 1)
                                nc.vector.tensor_tensor(den[0:H, bass.ds(first, 1)], den[0:H, bass.ds(first, 1)],
                                                        resc[s % 3][:, :], ALU.mult).then_inc(rmul, 1)
                                dve.wait_ge(rmul, g * 2 + 2)
                            nc.vector.tensor_tensor(agg[:, :, bass.ds(first, W)], agg[:, :, bass.ds(first, W)],
                                                    ps_s[b][:, 0:KH, :], ALU.add).then_inc(merged, 1)
                            if attn:
                                nc.vector.tensor_tensor(den[:, bass.ds(first, W)], den[:, bass.ds(first, W)],
                                                        ps_s[b][0:H + 1, KH, :], ALU.add).then_inc(merged, 1)

                        def mlp_gate(g, s, v):
                            b = s % 2
                            dve.wait_ge(attr_in[b], came(s, v, 2, RING, 16))
                            if later(g, 2):
                                dve.wait_ge(premsg, g - 1)
                            nc.vector.tensor_scalar(gate[b][:, :], attr[b][:, :, 0], 0.0, 1.0, ALU.max,
                                                    ALU.min).then_inc(gated1, 1)
                            dve.wait_ge(gated1, g + 1)
                            nc.vector.tensor_scalar(gate[b][:, :], gate[b][:, :], 0.01, None,
                                                    ALU.add).then_inc(gated, 1)

                        def mlp_message(g, s, v):
                            b = s % 2
                            dve.wait_ge(embedded, g + 1)
                            if later(g, 1):
                                dve.wait_ge(premsg, g)
                            nc.vector.tensor_tensor(emb[:, :, :], ps_e[:, :, :],
                                                    rows_of["c2"][:, :].unsqueeze(1).broadcast_to([P, TI, D]),
                                                    ALU.add).then_inc(biased, 1)
                            dve.wait_ge(biased, g + 1)
                            dve.wait_ge(gated, g + 1)
                            dve.wait_ge(gathered[s], came(s, v, RING, RING, 64))
                            if later(g, 2):
                                dve.wait_ge(summed, g - 1)
                            for i in range(TI):
                                m = nc.vector.scalar_tensor_tensor(
                                    out=msg[b][:, i, :], in0=emb[:, i, :], scalar=gate[b][:, i:i + 1],
                                    in1=G[s][:, i, :], op0=ALU.mult, op1=ALU.add)
                            m.then_inc(premsg, 1)

                        def attn_expand(g, s, v):
                            b = s % 2
                            dve.wait_ge(edge_in[s % 3], came(s, v, 3, RING, 48))
                            if later(g, 2):
                                dve.wait_ge(expanded, g - 1)
                            nc.vector.tensor_scalar(ohT[b][:, :], dstb[s % 3][:, :], nbase[:, bass.ds(g, 1)], None,
                                                    ALU.is_equal).then_inc(windowed, 1)
                            lo, hi = extra_lo(dve, g), extra_hi(dve, g)
                            with between(dve, lo, hi) as q:
                                k = q - lo + 1
                                dve.wait_ge(xd, q + 1)
                                nc.vector.tensor_tensor(
                                    nbx[:, :], nbase[:, bass.ds(g, 1)],
                                    starts[0:W, bass.ds(bounded(dve, k, MAXX - 1), 1)],
                                    ALU.add).then_inc(xnb, 1)
                                dve.wait_ge(xnb, q + 1)
                                nc.vector.tensor_scalar(ohTx[:, :], dstb[s % 3][:, :], nbx[:, :], None,
                                                        ALU.is_equal).then_inc(xohT, 1)

                        def attn_scan(g, s, v):
                            b = s % 2
                            d = s % 3
                            dve.wait_ge(scaled, g + 1)
                            nc.vector.tensor_tensor(leaky[b][:, :], leaky[b][:, :], ps_l[b][:, :],
                                                    ALU.max).then_inc(leaked, 1)
                            dve.wait_ge(leaked, g + 1)
                            if later(g, 1):
                                dve.wait_ge(ran, g)
                            prev = run[1 - b][:, GE - 1:GE] if later(g, 1) else floor[:, :]
                            nc.vector.tensor_tensor_scan(run[b][:, :], bound[d][:, 0:GE], leaky[b][:, :], prev,
                                                         ALU.min, ALU.max).then_inc(ran, 1)
                            dve.wait_ge(ran, g + 1)
                            nc.vector.tensor_tensor_scan(top[:, ::-1], bound[d][:, GE:0:-1], run[b][:, ::-1], -BIG,
                                                         ALU.min, ALU.max).then_inc(topped, 1)
                            dve.wait_ge(topped, g + 1)
                            if later(g, 1):
                                dve.wait_ge(rescaled, g)
                            nc.vector.tensor_scalar(shift[:, :], prev, top[:, 0:1], 0.0, ALU.subtract,
                                                    ALU.min)
                            nc.vector.tensor_tensor(leaky[b][:, :], leaky[b][:, :], top[:, :],
                                                    ALU.subtract).then_inc(belowed, 1)

                        def attn_message(g, s, v):
                            b = s % 2
                            dve.wait_ge(eecopied, g + 1)
                            dve.wait_ge(gathered[s], came(s, v, RING, RING, 64))
                            if later(g, 2):
                                dve.wait_ge(summed, g - 1)
                            n = TI - ACT_TI
                            nc.vector.tensor_tensor(
                                msg[b][:, 0:n, :].rearrange("p i (h d) -> p i h d", h=H),
                                G[s][:, 0:n, 0:D].rearrange("p i (h d) -> p i h d", h=H),
                                eeo[b][:, 0:n, 0:H].unsqueeze(3).broadcast_to([P, n, H, DH]), ALU.mult).then_inc(messaged, 1)

                        nc.vector.memset(xrel[:, :], 0.0).then_inc(xmerged, 1)
                        if attn:
                            nc.vector.memset(nbx[:, :], 0.0).then_inc(xd, 1)
                            nc.vector.memset(eeo[0][:, :, H:H + 1], 1.0)
                            nc.vector.memset(eeo[1][:, :, H:H + 1], 1.0)
                            nc.vector.memset(floor[:, :], -BIG)
                            nc.vector.memset(bound[0][:, GE:GE + 1], BIG)
                            nc.vector.memset(bound[1][:, GE:GE + 1], BIG)
                            nc.vector.memset(bound[2][:, GE:GE + 1], BIG).then_inc(onesset, 1)
                            dve.wait_ge(onesset, 1)
                        if mlp:
                            stages = [(1 - RING, index), (0, mlp_gate), (3, further), (3, merge), (1, window),
                                      (1, mlp_message)]
                        elif attn:
                            stages = [(1 - RING, index), (0, attn_expand), (1, attn_scan), (3, further),
                                      (3, merge), (2, window), (2, attn_message)]
                        else:
                            stages = [(1 - RING, index), (0, window), (0, further), (1, merge)]
                        pipelined(dve, NG, RING, stages)
                        dve.wait_ge(merged, NG * (2 if attn else 1))

                    @block.tensor
                    def _(pe):
                        def segment_sum(o, m, w, slot_ee):
                            for k in range(KH):
                                for i in range(TI):
                                    last = nc.tensor.matmul(o[:, k, :], m[:, i, k * P:(k + 1) * P], w[:, i, :],
                                                            start=(i == 0), stop=(i == TI - 1))
                            if attn:
                                for i in range(TI):
                                    last = nc.tensor.matmul(o[0:H + 1, KH, :], slot_ee[:, i, :], w[:, i, :],
                                                            start=(i == 0), stop=(i == TI - 1))
                            return last

                        def summing(g, s, v):
                            b = s % 2
                            lo, hi = extra_lo(pe, g), extra_hi(pe, g)
                            if mlp or attn:
                                pe.wait_ge(messaged, g + 1)
                                if attn:
                                    pe.wait_ge(messaged_a, g + 1)
                            else:
                                pe.wait_ge(gathered[s], came(s, v, RING, RING, 64))
                            pe.wait_ge(onehot, g + 1)
                            slot_ee = eeo[b] if attn else None
                            pe.nop(nofuse=True)
                            with between(pe, lo, hi) as q:
                                pe.wait_ge(xonehot, q + 1)
                                segment_sum(ps_x, operand(g, s), xoh, slot_ee).then_inc(xsummed, 1)
                            if later(g, 2):
                                pe.wait_ge(merged, (g - 1) * (2 if attn else 1))
                            segment_sum(ps_s[b], operand(g, s), oh[b], slot_ee).then_inc(summed, 1)

                        def mlp_turn(g, s, v):
                            b = s % 2
                            pe.wait_ge(attr_in[b], came(s, v, 2, RING, 16))
                            if later(g, 1):
                                pe.wait_ge(attred, g)
                            for i in range(TI):
                                m = nc.tensor.transpose(ps_a[:, i * P:(i + 1) * P], attr[b][:, i, :], ident[:, :])
                            m.then_inc(turned, 1)

                        def mlp_hidden(g, s, v):
                            b = s % 2
                            pe.wait_ge(attred, g + 1)
                            if later(g, 1):
                                pe.wait_ge(relued, g * KH)
                            for k in range(KH):
                                nc.tensor.matmul(ps_h[:, k, :], w_e1T[:, k * P:(k + 1) * P], attrT[b][:, :],
                                                 start=True, stop=True).then_inc(hidden, 1)

                        def mlp_embed(g, s, v):
                            b = s % 2
                            pe.wait_ge(relued, (g + 1) * KH)
                            if later(g, 1):
                                pe.wait_ge(biased, g)
                            for i in range(TI):
                                for k in range(KH):
                                    m = nc.tensor.matmul(ps_e[:, i, :], hid[b][:, k, i * P:(i + 1) * P],
                                                         wT["fuse"][:, k, :], start=(k == 0), stop=(k == KH - 1))
                            m.then_inc(embedded, 1)

                        def attn_score(g, s, v):
                            b = s % 2
                            pe.wait_ge(windowed, g + 1)
                            pe.wait_ge(gathered[s], came(s, v, RING, RING, 64))
                            if later(g, 2):
                                pe.wait_ge(leaked, g - 1)
                            pe.nop(nofuse=True)
                            nc.tensor.matmul(ps_l[b][:, :], dwin[s % 3][:, :], ohT[b][:, :], start=True,
                                             stop=False).then_inc(expanded, 1)
                            lo, hi = extra_lo(pe, g), extra_hi(pe, g)
                            with between(pe, lo, hi) as q:
                                pe.wait_ge(xohT, q + 1)
                                pe.wait_ge(xwin, q * 16 + 16)
                                pe.nop(nofuse=True)
                                nc.tensor.matmul(ps_l[b][:, :], dwinx[:, :], ohTx[:, :], start=False,
                                                 stop=False).then_inc(xd, 1)
                            ov = ps_l[b][:, :].rearrange("h (p i) -> h i p", i=TI)
                            for i in range(TI):
                                m = nc.tensor.matmul(ov[:, i, :], G[s][:, i, D:D + H], ident[:, :], start=False,
                                                     stop=(i == TI - 1))
                            m.then_inc(scored, 1)

                        def attn_spread(g, s, v):
                            b = s % 2
                            pe.wait_ge(exped, g + 1)
                            if later(g, 2):
                                pe.wait_ge(merged, (g - 1) * 2)
                            pe.nop(nofuse=True)
                            ev = ee[b][:, :].rearrange("h (p i) -> h i p", i=TI)
                            for i in range(TI):
                                nc.tensor.transpose(ps_ee[b][:, i * H:(i + 1) * H], ev[:, i, :], ident[0:H, 0:H])
                            for k in range(KH):
                                m = nc.tensor.matmul(ps_ee[b][:, TI * H + k:TI * H + k + 1],
                                                     headmask[:, k * P:(k + 1) * P], resc[s % 3][:, :], start=True,
                                                     stop=True)
                            m.then_inc(spreadee, 1)

                        if mlp:
                            stages = [(0, mlp_turn), (3, summing), (1, mlp_embed), (0, mlp_hidden)]
                            pipelined(pe, NG, RING, stages)
                        elif attn:
                            pipelined(pe, NG, RING, [(0, attn_score), (2, attn_spread), (3, summing)])
                        else:
                            pipelined(pe, NG, RING, [(0, summing)])

                    @block.scalar
                    def _(act):
                        if mlp:
                            def attr_move(g, s, v):
                                b = s % 2
                                act.wait_ge(turned, g + 1)
                                if later(g, 2):
                                    act.wait_ge(hidden, (g - 1) * KH)
                                nc.scalar.activation(attrT[b][:, :], ps_a[:, :], ACT.Copy).then_inc(attred, 1)

                            def relu_hidden(g, s, v):
                                b = s % 2
                                if later(g, 2):
                                    act.wait_ge(embedded, g - 1)
                                for k in range(KH):
                                    act.wait_ge(hidden, g * KH + k + 1)
                                    nc.scalar.activation(hid[b][:, k, :], ps_h[:, k, :], ACT.Relu,
                                                         bias=cols_of["b_e1"][:, k:k + 1]).then_inc(relued, 1)

                            def relu_message(g, s, v):
                                b = s % 2
                                act.wait_ge(premsg, g + 1)
                                nc.scalar.activation(msg[b][:, :, :], msg[b][:, :, :], ACT.Relu).then_inc(messaged, 1)

                            pipelined(act, NG, RING, [(0, attr_move), (2, relu_message), (0, relu_hidden)])
                        if attn:
                            def scale(g, s, v):
                                b = s % 2
                                act.wait_ge(scored, g + 1)
                                if later(g, 2):
                                    act.wait_ge(exped, g - 1)
                                nc.scalar.activation(leaky[b][:, :], ps_l[b][:, :], ACT.Copy,
                                                     scale=0.2).then_inc(scaled, 1)

                            def expo(g, s, v):
                                b = s % 2
                                act.wait_ge(belowed, g + 1)
                                if later(g, 3):
                                    act.wait_ge(merged, (g - 2) * 2)
                                if later(g, 2):
                                    act.wait_ge(spreadee, g - 1)
                                nc.scalar.activation(resc[s % 3][:, :], shift[:, :], ACT.Exp).then_inc(rescaled, 1)
                                nc.scalar.activation(ee[b][:, :], leaky[b][:, :], ACT.Exp).then_inc(exped, 1)

                            def message(g, s, v):
                                b = s % 2
                                act.wait_ge(spreadee, g + 1)
                                act.wait_ge(gathered[s], came(s, v, RING, RING, 64))
                                if later(g, 2):
                                    act.wait_ge(summed, g - 1)
                                else:
                                    act.wait_ge(onesset, 1)
                                nc.scalar.activation(eeo[b][:, :, 0:H],
                                                     ps_ee[b][:, 0:TI * H].rearrange("p (i h) -> p i h", h=H),
                                                     ACT.Copy).then_inc(eecopied, 1)
                                act.wait_ge(eecopied, g + 1)
                                for i in range(TI - ACT_TI, TI):
                                    for h in range(H):
                                        m = nc.scalar.activation(msg[b][:, i, h * DH:(h + 1) * DH],
                                                                 G[s][:, i, h * DH:(h + 1) * DH], ACT.Copy,
                                                                 scale=eeo[b][:, i, h:h + 1])
                                m.then_inc(messaged_a, 1)
                            pipelined(act, NG, RING, [(0, scale), (1, expo), (2, message)])

        def node_phase(tag, kind, resid=None, rtab=None, to=None, second=None):
            mlp, attn, sage, last = (kind == k for k in ("mlp", "attn", "sage", "sagelast"))
            anysage = sage or last
            weight = wT["W_g1"] if mlp else None
            if anysage:
                weight = wT[{"n2": "Wl1", "n3": "Wl2", "n4": "Wl3"}[tag]]
            nxt = wT[{"n0": "attn", "n1": "Wr1", "n2": "Wr2", "n3": "Wr3", "n4": "W_root"}[tag]]
            nbias = {"n1": "bl1", "n2": "bl2", "n3": "bl3"}.get(tag)
            NXW = D + 2 * H if mlp else D
            B = 4
            with ExitStack() as scope:
                sb, ps = scoped(scope, tag)
                st = [sb(f"st{i}", [P, KH, P]) for i in range(B)]
                rd = [sb(f"rd{i}", [P, D]) for i in range(B)]
                rs = [sb(f"rs{i}", [P, D]) for i in range(B)] if last else rd
                y = [sb(f"y{i}", [P, D]) for i in range(B)]
                e = [sb(f"e{i}", [P, D]) for i in range(B)]
                u = [sb(f"u{i}", [P, D]) for i in range(B)]
                hT = [sb(f"hT{i}", [P, KH, P]) for i in range(B)]
                outt = [sb(f"outt{i}", [P, NXW]) for i in range(B)]
                fin = [sb(f"fin{i}", [P, D]) for i in range(B)]
                stats = [sb(f"stats{i}", [P, 6]) for i in range(B)]
                mv = [sb(f"mv{i}", [P, 2]) for i in range(B)]
                sd = [sb(f"sd{i}", [P, 1]) for i in range(B)]
                rstd = [sb(f"rstd{i}", [P, 1]) for i in range(B)]
                dst_ = sb("dst_", [H + 1, P])
                dtile = [sb(f"dtile{i}", [P, H + 1]) for i in range(2)]
                rden = [sb(f"rden{i}", [P, H]) for i in range(2)]
                mlpT = [sb(f"mlpT{i}", [P, KH, P]) for i in range(2)]
                ps_a = [ps(f"ps_a{i}", [P, D]) for i in range(2)]
                ps_t = [ps(f"ps_t{i}", [P, KH, P]) for i in range(2)]
                ps_n = [ps(f"ps_n{i}", [P, 512]) for i in range(2)]
                ps_d = ps("ps_d", [P, H + 1])
                ps_m = ps("ps_m", [P, KH, P])
                (staged, summed, c, finished, turned, moved, nexted, outed, dstaged, dturned, biased,
                 root, mid, midmoved, first) = sems(
                    tag, "staged summed c finished turned moved nexted outed dstaged dturned biased root mid midmoved "
                         "first")
                sdone, = sems(tag, "sdone")
                loaded = sems(tag, "ld0 ld1 ld2 ld3")
                stored = sems(tag, "st0 st1 st2 st3")
                LD = 2 if last else 1
                ST = 3 if mlp else (1 if last else 2)

                CH = {"mlp": 9, "attn": 7, "sage": 2, "sagelast": 6}[kind]
                CE = 1
                CR = {"mlp": 3, "attn": 6, "sage": 0, "sagelast": 5}[kind]
                CR1 = 8

                with nc.Block() as block:
                    @block.sync
                    def _(sp):
                        def load(t, s, v):
                            r = rows(t)
                            if later(t, B):
                                sp.wait_ge(finished, t - B + 1)
                            if anysage:
                                sp.dma_start(rd[s][0:r, :], rtab[bass.ds(t * P, r), :]).then_inc(loaded[s], 16)
                            if not sage:
                                sp.dma_start(rs[s][0:r, :], resid[bass.ds(t * P, r), :]).then_inc(loaded[s], 16)

                        def store(t, s, v):
                            r = rows(t)
                            sp.wait_ge(finished, t + 1)
                            sp.dma_start(to[bass.ds(t * P, r), :], fin[s][0:r, :]).then_inc(stored[s], 16)
                            if mlp:
                                sp.wait_ge(outed, t + 1)
                                sp.dma_start(t_hc[bass.ds(t * P, r), :], outt[s][0:r, 0:HCW]).then_inc(stored[s], 16)
                                sp.dma_start(t_dst[bass.ds(t * P, r), :], outt[s][0:r, HCW:]).then_inc(stored[s], 16)
                            elif not last:
                                sp.wait_ge(outed, t + 1)
                                sp.dma_start(second[bass.ds(t * P, r), :], outt[s][0:r, :]).then_inc(stored[s], 16)
                        if mlp:
                            sp.wait_ge(first, 1)
                            sp.dma_start(t_dst[N:N + 2 * W, :], fin[0][:, 0:H]).then_inc(sdone, 16)
                            sp.wait_ge(sdone, 16)
                        pipelined(sp, NT, B, [(0, load), (3, store)])
                        for s in range(B):
                            n = len(range(s, NT, B))
                            if n:
                                sp.wait_ge(stored[s], 16 * n * ST)

                    @block.scalar
                    def _(act):
                        def stage(t, s, v):
                            r = rows(t)
                            if later(t, B):
                                act.wait_ge(summed, t - B + 1)
                            nc.scalar.activation(st[s][:, :, 0:r], agg[:, :, bass.ds(t * P, r)],
                                                 ACT.Copy).then_inc(staged, 1)
                            if attn:
                                if later(t, 1):
                                    act.wait_ge(dturned, t)
                                nc.scalar.activation(dst_[:, 0:r], den[:, bass.ds(t * P, r)],
                                                     ACT.Copy).then_inc(dstaged, 1)

                        def exp_(t, s, v):
                            r = rows(t)
                            act.wait_ge(c, CH * t + CE)
                            nc.scalar.activation(e[s][0:r, :], y[s][0:r, :], ACT.Exp).then_inc(biased, 1)

                        def root1(t, s, v, n=0):
                            r = rows(t)
                            act.wait_ge(c, CH * t + (CR1 if n else CR))
                            m = nc.scalar.activation(sd[s][0:r, :], mv[s][0:r, 1:2], ACT.Sqrt, bias=epsc[0:r, :])
                            m.then_inc(root, 1)

                        def root2(t, s, v):
                            root1(t, s, v, 1)

                        def mid_(t, s, v):
                            r = rows(t)
                            act.wait_ge(mid, t + 1)
                            for k in range(KH):
                                m = nc.scalar.activation(mlpT[s % 2][:, k, 0:r], ps_m[:, k, 0:r], ACT.Relu,
                                                         bias=cols_of["ln_b"][:, k:k + 1],
                                                         scale=cols_of["ln_g"][:, k:k + 1])
                            m.then_inc(midmoved, 1)

                        def move(t, s, v):
                            r = rows(t)
                            act.wait_ge(turned, t + 1)
                            if later(t, B):
                                act.wait_ge(nexted, t - B + 1)
                            nc.scalar.activation(hT[s][:, :, 0:r], ps_t[s % 2][:, :, 0:r], ACT.Copy).then_inc(moved, 1)

                        def out_(t, s, v):
                            r = rows(t)
                            act.wait_ge(nexted, t + 1)
                            if last:
                                nc.scalar.activation(aux[:, :, bass.ds(t * P, r)],
                                                     ps_n[s % 2][:, 0:D].rearrange("p (k n) -> p k n", k=KH)[:, :, 0:r],
                                                     ACT.Copy).then_inc(outed, 1)
                                return
                            if later(t, B):
                                act.wait_ge(stored[s], v * 16 * ST)
                            nc.scalar.activation(outt[s][0:r, :], ps_n[s % 2][0:r, 0:NXW], ACT.Copy).then_inc(outed, 1)

                        if mlp:
                            pipelined(act, NT, B, [(0, stage), (1, root1), (1, mid_), (1, root2), (1, move), (1, out_)])
                        elif attn:
                            pipelined(act, NT, B, [(0, stage), (1, root1), (1, move)])
                        elif sage:
                            pipelined(act, NT, B, [(0, stage), (1, exp_), (1, move)])
                        else:
                            pipelined(act, NT, B, [(0, stage), (1, exp_), (1, root1), (1, move), (1, out_)])
                        if last or mlp:
                            act.wait_ge(outed, NT)

                    @block.vector
                    def _(dve):
                        def norm(t, s, src, dest, base, nroot):
                            r = rows(t)
                            nc.vector.bn_stats(stats[s][0:r, :], src[0:r, :]).then_inc(c, 1)
                            dve.wait_ge(c, CH * t + base + 1)
                            dve.nop(nofuse=True)
                            nc.vector.bn_aggr(mv[s][0:r, :], stats[s][0:r, :]).then_inc(c, 1)
                            dve.wait_ge(root, nroot)
                            nc.vector.reciprocal(rstd[s][0:r, :], sd[s][0:r, :]).then_inc(c, 1)
                            dve.wait_ge(c, CH * t + base + 3)
                            return nc.vector.tensor_scalar(dest[0:r, :], src[0:r, :], mv[s][0:r, 0:1],
                                                           rstd[s][0:r, :], ALU.subtract, ALU.mult)

                        def fin_free(t, s, v):
                            if later(t, B):
                                dve.wait_ge(stored[s], v * 16 * ST)

                        def front(t, s, v):
                            r = rows(t)
                            b = s % 2
                            dve.wait_ge(loaded[s], (v + 1) * 16 * LD)
                            if mlp:
                                dve.wait_ge(summed, t + 1)
                                nc.vector.tensor_tensor(y[s][0:r, :], ps_a[b][0:r, :], rows_of["b_g1"][0:r, :],
                                                        ALU.add).then_inc(c, 1)
                                dve.wait_ge(c, CH * t + 1)
                                norm(t, s, y[s], u[s], 1, t * 2 + 1).then_inc(c, 1)
                            elif attn:
                                dve.wait_ge(dturned, t + 1)
                                dve.wait_ge(summed, t + 1)
                                nc.vector.tensor_scalar(dtile[b][0:r, 0:H], ps_d[0:r, 0:H], 1e-30, None, ALU.max)
                                nc.vector.tensor_scalar(dtile[b][0:r, H:H + 1], ps_d[0:r, H:H + 1], 1.0, None,
                                                        ALU.max).then_inc(c, 1)
                                dve.wait_ge(c, CH * t + 1)
                                nc.vector.reciprocal(rden[b][0:r, :], dtile[b][0:r, 0:H])
                                nc.vector.reciprocal(invdeg[0:r, bass.ds(t, 1)], dtile[b][0:r, H:H + 1]
                                                     ).then_inc(c, 1)
                                dve.wait_ge(c, CH * t + 2)
                                nc.vector.tensor_tensor(
                                    u[s][0:r, :].rearrange("p (h d) -> p h d", h=H),
                                    ps_a[b][0:r, :].rearrange("p (h d) -> p h d", h=H),
                                    rden[b][0:r, :].unsqueeze(2).broadcast_to([r, H, DH]), ALU.mult
                                ).then_inc(c, 1)
                                dve.wait_ge(c, CH * t + 3)
                                nc.vector.scalar_tensor_tensor(out=y[s][0:r, :], in0=rs[s][0:r, :], scalar=2.0,
                                                               in1=u[s][0:r, :], op0=ALU.mult, op1=ALU.add
                                                               ).then_inc(c, 1)
                                dve.wait_ge(c, CH * t + 4)
                                fin_free(t, s, v)
                                norm(t, s, y[s], fin[s], 4, t + 1).then_inc(finished, 1)
                            else:
                                dve.wait_ge(summed, t + 1)
                                nc.vector.scalar_tensor_tensor(out=y[s][0:r, :], in0=ps_a[b][0:r, :],
                                                               scalar=invdeg[0:r, bass.ds(t, 1)],
                                                               in1=rd[s][0:r, :], op0=ALU.mult, op1=ALU.add
                                                               ).then_inc(c, 1)
                                dve.wait_ge(c, CH * t + 1)
                                nc.vector.tensor_scalar(u[s][0:r, :], y[s][0:r, :], 0.0, -1.0, ALU.max,
                                                        ALU.add).then_inc(c, 1)
                                dve.wait_ge(c, CH * t + 2)
                                dve.wait_ge(biased, t + 1)
                                if sage:
                                    fin_free(t, s, v)
                                    nc.vector.scalar_tensor_tensor(out=fin[s][0:r, :], in0=e[s][0:r, :], scalar=1.0,
                                                                   in1=u[s][0:r, :], op0=ALU.min, op1=ALU.add
                                                                   ).then_inc(finished, 1)
                                else:
                                    nc.vector.scalar_tensor_tensor(out=y[s][0:r, :], in0=e[s][0:r, :], scalar=1.0,
                                                                   in1=u[s][0:r, :], op0=ALU.min, op1=ALU.add
                                                                   ).then_inc(c, 1)
                                    dve.wait_ge(c, CH * t + 3)
                                    nc.vector.tensor_tensor(u[s][0:r, :], y[s][0:r, :], rs[s][0:r, :], ALU.add
                                                            ).then_inc(c, 1)
                                    dve.wait_ge(c, CH * t + 4)
                                    fin_free(t, s, v)
                                    nc.vector.bn_stats(stats[s][0:r, :], u[s][0:r, :]).then_inc(first, 1)
                                    dve.wait_ge(first, t + 1)
                                    dve.nop(nofuse=True)
                                    nc.vector.bn_aggr(mv[s][0:r, :], stats[s][0:r, :]).then_inc(c, 1)
                                    dve.wait_ge(root, t + 1)
                                    nc.vector.reciprocal(rstd[s][0:r, :], sd[s][0:r, :]).then_inc(c, 1)
                                    dve.wait_ge(c, CH * t + 6)
                                    nc.vector.tensor_scalar(fin[s][0:r, :], u[s][0:r, :], mv[s][0:r, 0:1],
                                                            rstd[s][0:r, :], ALU.subtract, ALU.mult
                                                            ).then_inc(finished, 1)

                        def back(t, s, v):
                            r = rows(t)
                            b = s % 2
                            dve.wait_ge(biased, t + 1)
                            nc.vector.tensor_tensor(y[s][0:r, :], ps_a[b][0:r, :], rows_of["b_g2"][0:r, :],
                                                    ALU.add).then_inc(c, 1)
                            dve.wait_ge(c, CH * t + 6)
                            nc.vector.tensor_tensor(y[s][0:r, :], y[s][0:r, :], rs[s][0:r, :], ALU.add
                                                    ).then_inc(first, 1)
                            dve.wait_ge(first, t + 2)
                            fin_free(t, s, v)
                            nc.vector.bn_stats(stats[s][0:r, :], y[s][0:r, :]).then_inc(c, 1)
                            dve.wait_ge(c, CH * t + 7)
                            dve.nop(nofuse=True)
                            nc.vector.bn_aggr(mv[s][0:r, :], stats[s][0:r, :]).then_inc(c, 1)
                            dve.wait_ge(root, t * 2 + 2)
                            nc.vector.reciprocal(rstd[s][0:r, :], sd[s][0:r, :]).then_inc(c, 1)
                            dve.wait_ge(c, CH * t + 9)
                            nc.vector.tensor_scalar(fin[s][0:r, :], y[s][0:r, :], mv[s][0:r, 0:1], rstd[s][0:r, :],
                                                    ALU.subtract, ALU.mult).then_inc(finished, 1)

                        def addbias(t, s, v):
                            r = rows(t)
                            dve.wait_ge(nexted, t + 1)
                            if later(t, B):
                                dve.wait_ge(stored[s], v * 16 * ST)
                            nc.vector.tensor_tensor(outt[s][0:r, :], ps_n[s % 2][0:r, 0:D], rows_of[nbias][0:r, :],
                                                    ALU.add).then_inc(outed, 1)

                        if mlp:
                            nc.vector.memset(fin[0][:, :], 0.0).then_inc(first, 1)
                            dve.wait_ge(sdone, 16)
                            pipelined(dve, NT, B, [(0, front), (0, back)])
                        elif last:
                            pipelined(dve, NT, B, [(0, front)])
                        else:
                            pipelined(dve, NT, B, [(0, front), (1, addbias)])

                    @block.tensor
                    def _(pe):
                        def product(o, lhs, w, r, width, sem):
                            for k in range(KH):
                                m = nc.tensor.matmul(o[0:r, 0:width], lhs[:, k, 0:r], w[:, k, 0:width],
                                                     start=(k == 0), stop=(k == KH - 1))
                            m.then_inc(sem, 1)

                        def sum_(t, s, v):
                            r = rows(t)
                            b = s % 2
                            pe.wait_ge(staged, t + 1)
                            if later(t, 2):
                                pe.wait_ge(finished, t - 1)
                            if attn:
                                pe.wait_ge(dstaged, t + 1)
                                if later(t, 1):
                                    pe.wait_ge(c, CH * t)
                                pe.nop(nofuse=True)
                                nc.tensor.transpose(ps_d[0:r, :], dst_[:, 0:r], ident[0:H + 1, 0:H + 1]
                                                    ).then_inc(dturned, 1)
                                for k in range(KH):
                                    m = nc.tensor.transpose(ps_a[b][0:r, k * P:(k + 1) * P], st[s][:, k, 0:r],
                                                            ident[:, :])
                                m.then_inc(summed, 1)
                            else:
                                product(ps_a[b], st[s], weight, r, D, summed)

                        def middle(t, s, v):
                            r = rows(t)
                            b = s % 2
                            pe.wait_ge(c, CH * t + 5)
                            for k in range(KH):
                                m = nc.tensor.transpose(ps_m[:, k, 0:r], u[s][0:r, k * P:(k + 1) * P],
                                                        ident[0:r, 0:r])
                            m.then_inc(mid, 1)
                            pe.wait_ge(midmoved, t + 1)
                            product(ps_a[b], mlpT[b], wT["W_g2"], r, D, biased)

                        def turn(t, s, v):
                            r = rows(t)
                            pe.wait_ge(finished, t + 1)
                            if later(t, 2):
                                pe.wait_ge(moved, t - 1)
                            for k in range(KH):
                                m = nc.tensor.transpose(ps_t[s % 2][:, k, 0:r], fin[s][0:r, k * P:(k + 1) * P],
                                                        ident[0:r, 0:r])
                            m.then_inc(turned, 1)
                            pe.wait_ge(moved, t + 1)
                            if later(t, 2):
                                pe.wait_ge(outed, t - 1)
                            if last:
                                for a in range(KH):
                                    for k in range(KH):
                                        m = nc.tensor.matmul(ps_n[s % 2][:, a * P:a * P + r],
                                                             nxt[:, k, a * P:(a + 1) * P], hT[s][:, k, 0:r],
                                                             start=(k == 0), stop=(k == KH - 1))
                                m.then_inc(nexted, 1)
                            else:
                                product(ps_n[s % 2], hT[s], nxt, r, NXW, nexted)

                        if mlp:
                            pipelined(pe, NT, B, [(0, sum_), (0, middle), (0, turn)])
                        else:
                            pipelined(pe, NT, B, [(0, sum_), (1, turn)])

        def clear_agg(tag):
            done, = sems(tag, "cleared")
            with nc.Block() as block:
                @block.vector
                def _(dve):
                    nc.vector.memset(agg[:, 0, :], 0.0).then_inc(done, 1)
                    dve.wait_ge(done, 2)

                @block.gpsimd
                def _(pool):
                    nc.gpsimd.memset(agg[:, 1, :], 0.0).then_inc(done, 1)

        def last_phase(tag):
            CW = 512
            NC_ = -(-N // CW)
            with ExitStack() as scope:
                sb, ps = scoped(scope, tag)
                stats = sb("bstats", [P, KH, NC_, 6])
                mv = sb("bmv", [P, KH, 2])
                sd = sb("bsd", [P, KH])
                scl = sb("scl", [P, KH])
                off = sb("off", [P, KH])
                ps_o = [[ps(f"ps_o{i}{a}", [P, CW]) for a in range(KH)] for i in range(2)]
                (prod, placed, v, rooted, normed) = sems(tag, "prod placed v rooted normed")
                with nc.Block() as block:
                    @block.tensor
                    def _(pe):
                        for c in range(NC_):
                            n = min(CW, N - c * CW)
                            if c >= 2:
                                pe.wait_ge(placed, (c - 1) * KH)
                            for a in range(KH):
                                for k in range(KH):
                                    m = nc.tensor.matmul(ps_o[c % 2][a][:, 0:n], wT["W_rel"][:, k, a * P:(a + 1) * P],
                                                         agg[:, k, c * CW:c * CW + n], start=(k == 0),
                                                         stop=(k == KH - 1))
                            m.then_inc(prod, 1)

                    @block.vector
                    def _(dve):
                        for c in range(NC_):
                            n = min(CW, N - c * CW)
                            dve.wait_ge(prod, c + 1)
                            for a in range(KH):
                                nc.vector.scalar_tensor_tensor(
                                    out=agg[:, a, c * CW:c * CW + n], in0=ps_o[c % 2][a][:, 0:n],
                                    scalar=cols_of["b_rel"][:, a:a + 1], in1=aux[:, a, c * CW:c * CW + n],
                                    op0=ALU.add, op1=ALU.add).then_inc(placed, 1)
                            dve.wait_ge(placed, (c + 1) * KH)
                            for a in range(KH):
                                m = nc.vector.bn_stats(stats[:, a, c, :], agg[:, a, c * CW:c * CW + n])
                        m.then_inc(v, 1)
                        dve.wait_ge(v, 1)
                        for a in range(KH):
                            m = nc.vector.bn_aggr(mv[:, a, :], stats[:, a, :, :])
                        m.then_inc(v, 1)
                        dve.wait_ge(rooted, 1)
                        nc.vector.reciprocal(scl[:, :], sd[:, :]).then_inc(v, 1)
                        dve.wait_ge(v, 3)
                        nc.vector.tensor_tensor(scl[:, :], scl[:, :], cols_of["gamma"][:, :], ALU.mult).then_inc(v, 1)
                        dve.wait_ge(v, 4)
                        nc.vector.tensor_tensor(off[:, :], mv[:, :, 0], scl[:, :], ALU.mult).then_inc(v, 1)
                        dve.wait_ge(v, 5)
                        nc.vector.tensor_tensor(off[:, :], cols_of["beta"][:, :], off[:, :],
                                                ALU.subtract).then_inc(v, 1)
                        dve.wait_ge(v, 6)

                    @block.scalar
                    def _(act):
                        act.wait_ge(v, 2)
                        nc.scalar.activation(sd[:, :], mv[:, :, 1], ACT.Sqrt, bias=epsc[:, :]).then_inc(rooted, 1)
                B = 4
                st = [sb(f"fst{i}", [P, KH, P]) for i in range(B)]
                xr = [sb(f"fx{i}", [P, D]) for i in range(B)]
                y = [sb(f"fy{i}", [P, D]) for i in range(B)]
                u = [sb(f"fu{i}", [P, D]) for i in range(B)]
                fin = [sb(f"ffin{i}", [P, D]) for i in range(B)]
                st6 = [sb(f"fs{i}", [P, 6]) for i in range(B)]
                mv2 = [sb(f"fm{i}", [P, 2]) for i in range(B)]
                sd2 = [sb(f"fd{i}", [P, 1]) for i in range(B)]
                rstd = [sb(f"fr{i}", [P, 1]) for i in range(B)]
                ps_f = [ps(f"ps_f{i}", [P, D]) for i in range(2)]
                staged, turned, c, root, finished = sems(tag, "staged turned c root finished")
                loaded = sems(tag, "fl0 fl1 fl2 fl3")
                stored = sems(tag, "fs0 fs1 fs2 fs3")

                with nc.Block() as block:
                    @block.sync
                    def _(sp):
                        def load(t, s, v):
                            r = rows(t)
                            if later(t, B):
                                sp.wait_ge(finished, t - B + 1)
                            sp.dma_start(xr[s][0:r, :], t_x3[bass.ds(t * P, r), :]).then_inc(loaded[s], 16)

                        def store(t, s, v):
                            r = rows(t)
                            sp.wait_ge(finished, t + 1)
                            sp.dma_start(out[bass.ds(t * P, r), :], fin[s][0:r, :]).then_inc(stored[s], 16)
                        pipelined(sp, NT, B, [(0, load), (3, store)])
                        for s in range(B):
                            n = len(range(s, NT, B))
                            if n:
                                sp.wait_ge(stored[s], 16 * n)

                    @block.scalar
                    def _(act):
                        def stage(t, s, v):
                            r = rows(t)
                            if later(t, B):
                                act.wait_ge(turned, t - B + 1)
                            for a in range(KH):
                                m = nc.scalar.activation(st[s][:, a, 0:r], agg[:, a, bass.ds(t * P, r)], ACT.Relu,
                                                         bias=off[:, a:a + 1], scale=scl[:, a:a + 1])
                            m.then_inc(staged, 1)

                        def root1(t, s, v):
                            r = rows(t)
                            act.wait_ge(c, t * 5 + 4)
                            nc.scalar.activation(sd2[s][0:r, :], mv2[s][0:r, 1:2], ACT.Sqrt,
                                                 bias=epsc[0:r, :]).then_inc(root, 1)
                        pipelined(act, NT, B, [(0, stage), (1, root1)])

                    @block.tensor
                    def _(pe):
                        def turn(t, s, v):
                            r = rows(t)
                            pe.wait_ge(staged, t + 1)
                            if later(t, 2):
                                pe.wait_ge(finished, t - 1)
                            for a in range(KH):
                                m = nc.tensor.transpose(ps_f[s % 2][0:r, a * P:(a + 1) * P], st[s][:, a, 0:r],
                                                        ident[:, :])
                            m.then_inc(turned, 1)
                        pipelined(pe, NT, B, [(0, turn)])

                    @block.vector
                    def _(dve):
                        def chain(t, s, v):
                            r = rows(t)
                            dve.wait_ge(turned, t + 1)
                            dve.wait_ge(loaded[s], (v + 1) * 16)
                            nc.vector.tensor_tensor(y[s][0:r, :], ps_f[s % 2][0:r, :], xr[s][0:r, :],
                                                    ALU.add).then_inc(c, 1)
                            dve.wait_ge(c, t * 5 + 1)
                            nc.vector.scalar_tensor_tensor(out=u[s][0:r, :], in0=y[s][0:r, :], scalar=0.0,
                                                           in1=xr[s][0:r, :], op0=ALU.max, op1=ALU.add).then_inc(c, 1)
                            dve.wait_ge(c, t * 5 + 2)
                            nc.vector.bn_stats(st6[s][0:r, :], u[s][0:r, :]).then_inc(c, 1)
                            dve.wait_ge(c, t * 5 + 3)
                            dve.nop(nofuse=True)
                            nc.vector.bn_aggr(mv2[s][0:r, :], st6[s][0:r, :]).then_inc(c, 1)
                            dve.wait_ge(root, t + 1)
                            nc.vector.reciprocal(rstd[s][0:r, :], sd2[s][0:r, :]).then_inc(c, 1)
                            dve.wait_ge(c, t * 5 + 5)
                            if later(t, B):
                                dve.wait_ge(stored[s], v * 16)
                            nc.vector.tensor_scalar(fin[s][0:r, :], u[s][0:r, :], mv2[s][0:r, 0:1],
                                                    rstd[s][0:r, :], ALU.subtract, ALU.mult).then_inc(finished, 1)
                        pipelined(dve, NT, B, [(0, chain)])

        def copy_out(table):
            done, = sems("co", "copied_out")
            with nc.Block() as block:
                @block.sync
                def _(sp):
                    sp.dma_start(out, table).then_inc(done, 16)
                    sp.wait_ge(done, 16)

        phase(edge_tables)
        phase(weights)
        phase(first_table)
        phase(edge_phase, "e0", "mlp", t_x0, D)
        phase(node_phase, "n0", "mlp", resid=ins["x"], to=t_x1)
        layer0.close()
        if depth == 1:
            return copy_out(t_x1)
        phase(clear_agg, "z1")
        phase(edge_phase, "e1", "attn", t_hc, HCW)
        phase(node_phase, "n1", "attn", resid=t_x1, to=t_x2, second=t_r[0])
        if depth == 2:
            return copy_out(t_x2)
        phase(clear_agg, "z2")
        phase(edge_phase, "e2", "sum", t_x2, D)
        phase(node_phase, "n2", "sage", rtab=t_r[0], to=t_h1, second=t_r[1])
        phase(clear_agg, "z3")
        phase(edge_phase, "e3", "sum", t_h1, D)
        phase(node_phase, "n3", "sage", rtab=t_r[1], to=t_h2, second=t_r[2])
        phase(clear_agg, "z4")
        phase(edge_phase, "e4", "sum", t_h2, D)
        phase(node_phase, "n4", "sagelast", resid=t_x2, rtab=t_r[2], to=t_x3)
        if depth == 3:
            return copy_out(t_x3)
        phase(clear_agg, "z5")
        phase(edge_phase, "e5", "weighted", t_x3, D)
        phase(last_phase, "n5")


DEPTH = 4


def kernel(**inputs):
    import numpy as _np
    import concourse.bacc as _bacc
    from concourse import mybir as _mybir
    from concourse.bass_utils import run_bass_kernel_spmd as _run

    nc = _bacc.Bacc("TRN2", target_bir_lowering=False, num_devices=1)
    arrays, args = {}, {}
    for name, value in inputs.items():
        a = _np.ascontiguousarray(value)
        arrays[f"in_{name}_dram"] = a
        args[name] = nc.dram_tensor(f"in_{name}_dram", a.shape, _mybir.dt.from_np(a.dtype), kind="ExternalInput").ap()
    shape = inputs["x"].shape
    out = nc.dram_tensor("out_0_dram", shape, _mybir.dt.float32, kind="ExternalOutput").ap()
    gnn_kernel(nc, args, out, DEPTH)
    r = _run(nc, [arrays], core_ids=[0])
    return r.results[0]["out_0_dram"]
```

```python
import concourse.bass as bass
from concourse import mybir
from contextlib import ExitStack, contextmanager

FP32 = mybir.dt.float32
I32 = mybir.dt.int32
BF16 = mybir.dt.bfloat16
PARTS = 3
ALU = mybir.AluOpType
ACT = mybir.ActivationFunctionType
AX = mybir.AxisListType

P = 128
D = 256
KH = D // P
GE = 512
TI = GE // P
W = 40
H = 4
DH = D // H
RING = 6
ACT_TI = 2
BIG = 1.7e38
EPS = 1e-5
NOWHERE = -1.0e4


def pipelined(eng, count, unroll, stages):
    lags = max(lag for lag, _ in stages)
    ahead = max(0, -min(lag for lag, _ in stages))

    def step(turn, u):
        for lag, f in stages:
            t = turn * unroll + u - lag
            if isinstance(t, int) and not 0 <= t < count:
                continue
            f(t, (u - lag) % unroll, turn + (u - lag) // unroll)

    head = -(-(lags + unroll) // unroll)
    loops = max(0, (count - 1 - ahead) // unroll - head)
    if loops < 2:
        head, loops = 0, 0
    for s in range(-ahead, head * unroll):
        step(s // unroll, s % unroll)
    if loops:
        with eng.Fori(0, loops) as it:
            for u in range(unroll):
                step(it + head, u)
    for s in range((head + loops) * unroll, count + lags):
        step(s // unroll, s % unroll)


def came(s, v, ring, unroll, each):
    return (v * (unroll // ring) + s // ring + 1) * each


@contextmanager
def between(eng, lo, hi):
    with eng.If(lo < hi):
        with eng.Fori(lo, hi) as q:
            yield q


def later(t, n):
    return not isinstance(t, int) or t >= n


def gnn_kernel(nc, ins, out, depth):
    N = ins["x"].shape[0]
    E = ins["src"].shape[0]
    NG = -(-E // GE)
    TAILP = (E - GE * (NG - 1)) // TI
    NT = -(-N // P)
    LASTR = N - P * (NT - 1)
    NW = N + W + P
    HCW = D + H
    NKW = -(-N // W) + 1
    MAXX = NKW + 1

    def rows(t):
        return LASTR if isinstance(t, int) and t == NT - 1 else P

    ctx = ExitStack()
    taken = []

    def sems(tag, names):
        got = [nc.alloc_semaphore(f"{tag}_{n}") for n in names.split()]
        taken.extend(got)
        return got

    def phase(build, *args, **kwargs):
        build(*args, **kwargs)
        nc.clear_and_free_semaphores(taken)
        taken.clear()
        nc.all_engine_barrier()

    def scoped(scope, tag):
        def sb(name, shape, dt=FP32):
            return scope.enter_context(nc.sbuf_tensor(f"{tag}_{name}", shape, dt))

        def ps(name, shape):
            free = 1
            for n in shape[1:]:
                free *= n
            whole = scope.enter_context(nc.psum_tensor(f"{tag}_{name}", [P, -(-free // 512) * 512], FP32))
            flat = whole[0:shape[0], 0:free]
            if len(shape) == 3:
                return flat.rearrange("p (a b) -> p a b", b=shape[2])
            return flat
        return sb, ps

    def dram(name, shape, dt=FP32):
        return nc.dram_tensor(name, shape, dt, kind="Internal").ap()

    with ctx:
        sb, _ = scoped(ctx, "all")
        t_x0 = dram("t_x0", (N, D))
        t_hc = dram("t_hc", (N, HCW))
        t_dst = dram("t_dst", (N + P, PARTS * H), BF16)
        t_x1 = dram("t_x1", (N, D))
        t_x2 = dram("t_x2", (N, D))
        t_h1 = dram("t_h1", (N, D))
        t_h2 = dram("t_h2", (N, D))
        t_x3 = dram("t_x3", (N, D))
        t_r = [dram(f"t_r{i}", (N, D)) for i in range(3)]
        t_flag = dram("t_flag", (NG, GE))

        agg = sb("agg", [P, KH, NW])
        aux = sb("aux", [P, KH, NW])
        den = aux[0:H + 1, 0, :]
        srcT = sb("srcT", [P, NG * TI], I32)
        relT = sb("relT", [P, NG * TI])
        ewT = sb("ewT", [P, NG * TI])
        nbase = sb("nbase", [W, NG])
        starts = sb("starts", [P, MAXX])
        ctrl = sb("ctrl", [1, 2 * NG + 1], I32)
        c_first, c_extra = 0, NG
        iotaw = sb("iotaw", [P, W])
        ident = sb("ident", [P, P])
        ones = sb("ones", [1, P])
        epsc = sb("epsc", [P, 1])
        idx = [sb(f"idx{s}", [P, TI], I32) for s in range(RING)]
        invdeg = sb("invdeg", [P, NT])
        wT = {}
        for n in "Wl1 Wr1 Wl2 Wr2 Wl3 Wr3 W_rel W_root".split():
            wT[n] = sb("T" + n, [P, KH, D])
        rows_of = {}
        for n in "bl1 bl2 bl3".split():
            rows_of[n] = sb("R" + n, [P, D])
        cols_of = {}
        for n in "b_e1 ln_g ln_b b_rel gamma beta".split():
            cols_of[n] = sb("C" + n, [P, KH])
        headmask = sb("headmask", [H, D])
        halfmask = sb("halfmask", [H, P])
        layer0 = ExitStack()
        sb, _ = scoped(layer0, "l0")
        for n in "W_g1 W_g2 fuse".split():
            wT[n] = sb("T" + n, [P, KH, D])
        wT["attn"] = sb("Tattn", [P, KH, D + 2 * H])
        w_e1T = sb("w_e1T", [65, D])
        for n in "b_le c2 b_g1 b_g2".split():
            rows_of[n] = sb("R" + n, [P, D])

        def extra_lo(eng, g):
            return eng.value_load(ctrl[0:1, bass.ds(g + c_extra, 1)], min_val=0, max_val=NG * NKW)

        def extra_hi(eng, g):
            return eng.value_load(ctrl[0:1, bass.ds(g + c_extra + 1, 1)], min_val=0, max_val=NG * NKW)

        far = [False]

        def either(eng, write):
            total = eng.value_load(ctrl[0:1, 2 * NG:2 * NG + 1], min_val=0, max_val=NG * NKW)
            with eng.If(total < 1):
                far[0] = False
                write()
            with eng.If(total > 0):
                far[0] = True
                write()

        def bounded(eng, value, most):
            return eng.snap(value.with_bounds(min_val=0, max_val=most))

        def first_dst(eng, g):
            return eng.value_load(ctrl[0:1, bass.ds(g + c_first, 1)], min_val=0, max_val=N - 1)

        def edge_tables():
            with ExitStack() as scope:
                sb, ps = scoped(scope, "et")
                blocks = [(a, min(P, NG - a)) for a in range(0, NG, P)]
                NB = len(blocks)
                d_i = sb("d_i", [P, NB, GE], I32)
                q_i = sb("q_i", [P, NB, GE], I32)
                s_i = sb("s_i", [P, NB, GE], I32)
                w_f = sb("w_f", [P, NB, GE])
                d_f = sb("d_f", [P, NB, GE])
                q_f = sb("q_f", [P, NB, GE])
                s_f = sb("s_f", [P, NB, GE])
                flag = sb("flag", [P, NB, GE])
                last = sb("last", [P, NB])
                frow = sb("frow", [1, NG])
                lrow = sb("lrow", [1, NG])
                span = sb("span", [1, NG])
                spani = sb("spani", [1, NG], I32)
                spanf = sb("spanf", [1, NG])
                xrow = sb("xrow", [1, NG])
                zrow = sb("zrow", [1, NG])
                pidx = sb("pidx", [P, 1])
                ps_t = [ps(f"ps_t{i}", [P, 4, P]) for i in range(3)]
                ps_r = ps("ps_r", [1, 2, NG])
                ps_b = ps("ps_b", [P, NG])
                (filled, loaded, cast, lasted, turned, copied, rowed, v, flagged, based, made, consts, filled2,
                 bmade) = sems("et", "filled loaded cast lasted turned copied rowed v flagged based made consts filled2 bmade")
                made_flags, spanned = sems("et", "made_flags spanned")
                n_loads = 0
                for a, n in blocks:
                    full = min(a + n, NG - 1) - a
                    n_loads += 3 * ((full > 0) + (full < n)) + (a == 0) + (full > (1 if a == 0 else 0)) + (full < n)
                with nc.Block() as block:
                    @block.gpsimd
                    def _(pool):
                        nc.gpsimd.memset(ident[:, :], 0.0).then_inc(made, 1)
                        nc.gpsimd.iota(iotaw[:, :], [[1, W]], base=0, channel_multiplier=0,
                                       allow_small_or_imprecise_dtypes=True).then_inc(made, 1)
                        nc.gpsimd.iota(starts[:, :], [[W, MAXX]], base=0, channel_multiplier=0,
                                       allow_small_or_imprecise_dtypes=True).then_inc(made, 1)
                        nc.gpsimd.iota(pidx[:, :], [[0, 1]], base=0, channel_multiplier=1,
                                       allow_small_or_imprecise_dtypes=True).then_inc(made, 1)
                        nc.gpsimd.memset(headmask[:, :], 1.0).then_inc(made, 1)
                        pool.wait_ge(made, 5)
                        nc.gpsimd.affine_select(out=ident[:, :], in_=ident[:, :], compare_op=ALU.not_equal, fill=1.0,
                                                base=0, pattern=[[-1, P]], channel_multiplier=1).then_inc(consts, 1)
                        nc.gpsimd.affine_select(out=headmask[:, :], in_=headmask[:, :], compare_op=ALU.is_ge,
                                                fill=0.0, base=0, pattern=[[1, D]],
                                                channel_multiplier=-DH).then_inc(made, 1)
                        pool.wait_ge(made, 6)
                        nc.gpsimd.affine_select(out=headmask[:, :], in_=headmask[:, :], compare_op=ALU.is_ge,
                                                fill=0.0, base=DH - 1, pattern=[[-1, D]],
                                                channel_multiplier=DH).then_inc(consts, 1)
                        pool.wait_ge(consts, 2)
                        nc.gpsimd.tensor_tensor(halfmask[:, :], headmask[:, 0:P], headmask[:, P:D],
                                                ALU.add).then_inc(consts, 1)
                        pool.wait_ge(consts, 3)

                    def grouped(dram_vec, a, n):
                        return dram_vec[a * GE:(a + n) * GE].rearrange("(g e) -> g e", e=GE)

                    @block.sync
                    def _(sp):
                        sp.wait_ge(filled, 1)
                        for b, (a, n) in enumerate(blocks):
                            full = min(a + n, NG - 1) - a
                            for tile, vec in ((d_i, ins["dst"]), (s_i, ins["src"]), (w_f, ins["edge_weight"])):
                                if full:
                                    sp.dma_start(tile[0:full, b, :], grouped(vec, a, full)).then_inc(loaded, 16)
                                if full < n:
                                    sp.dma_start(tile[full:n, b, 0:TAILP * TI],
                                                 vec[(a + full) * GE:E].rearrange("(g e) -> g e", g=1)
                                                 ).then_inc(loaded, 16)
                            lo = 1 if a == 0 else 0
                            if a == 0:
                                sp.dma_start(q_i[0:1, b, 1:GE],
                                             ins["dst"][0:GE - 1].rearrange("(g e) -> g e", g=1)).then_inc(loaded, 16)
                            if full > lo:
                                sp.dma_start(q_i[lo:full, b, :],
                                             ins["dst"][(a + lo) * GE - 1:(a + full) * GE - 1].rearrange(
                                                 "(g e) -> g e", e=GE)).then_inc(loaded, 16)
                            if full < n:
                                sp.dma_start(q_i[full:n, b, 0:TAILP * TI + 1],
                                             ins["dst"][(a + full) * GE - 1:E].rearrange("(g e) -> g e", g=1)
                                             ).then_inc(loaded, 16)
                        for b, (a, n) in enumerate(blocks):
                            sp.wait_ge(flagged, b + 1)
                            sp.dma_start(t_flag[a:a + n, :], flag[0:n, b, :]).then_inc(made_flags, 16)
                        sp.wait_ge(made_flags, 16 * NB)

                    @block.vector
                    def _(dve):
                        nc.vector.memset(d_i[:, :, :], int(NOWHERE))
                        nc.vector.memset(q_i[:, :, :], -1)
                        nc.vector.memset(s_i[:, :, :], 0)
                        nc.vector.memset(w_f[:, :, :], 0.0).then_inc(filled, 1)
                        nc.vector.memset(ones[:, :], 1.0)
                        nc.vector.memset(epsc[:, :], EPS)
                        nc.vector.memset(zrow[:, :], 0.0).then_inc(filled2, 1)
                        dve.wait_ge(loaded, 16 * n_loads)
                        nc.vector.tensor_copy(d_f[:, :, :], d_i[:, :, :]).then_inc(cast, 1)
                        nc.vector.tensor_copy(q_f[:, :, :], q_i[:, :, :]).then_inc(cast, 1)
                        nc.vector.tensor_copy(s_f[:, :, :], s_i[:, :, :]).then_inc(cast, 1)
                        dve.wait_ge(cast, 2)
                        nc.vector.tensor_reduce(last[:, :], d_f[:, :, :], AX.X, ALU.max).then_inc(lasted, 1)
                        nc.vector.tensor_tensor(flag[:, :, :], d_f[:, :, :], q_f[:, :, :],
                                                ALU.not_equal).then_inc(v, 1)
                        dve.wait_ge(v, 1)
                        for b in range(NB):
                            nc.vector.tensor_scalar(flag[:, b, :], flag[:, b, :], -2 * BIG, BIG, ALU.mult,
                                                    ALU.add).then_inc(flagged, 1)
                        dve.wait_ge(rowed, 1)
                        nc.vector.tensor_copy(frow[:, :], ps_r[0:1, 0, :]).then_inc(based, 1)
                        nc.vector.tensor_copy(lrow[:, :], ps_r[0:1, 1, :]).then_inc(v, 1)
                        dve.wait_ge(based, 1)
                        dve.wait_ge(v, 2)
                        nc.vector.tensor_copy(ctrl[0:1, 0:NG], frow[:, :])
                        nc.vector.tensor_tensor(span[:, :], lrow[:, :], frow[:, :], ALU.subtract).then_inc(v, 1)
                        dve.wait_ge(v, 3)
                        nc.vector.tensor_scalar(span[:, :], span[:, :], 0.5, 1024.0 / W, ALU.add,
                                                ALU.mult).then_inc(spanned, 1)
                        dve.wait_ge(spanned, 1)
                        nc.vector.tensor_copy(spani[:, :], span[:, :]).then_inc(v, 1)
                        dve.wait_ge(v, 4)
                        nc.vector.tensor_scalar(spani[:, :], spani[:, :], 10, None,
                                                ALU.arith_shift_right).then_inc(v, 1)
                        dve.wait_ge(v, 5)
                        nc.vector.tensor_copy(spanf[:, :], spani[:, :]).then_inc(v, 1)
                        dve.wait_ge(v, 6)
                        dve.wait_ge(filled2, 1)
                        nc.vector.tensor_tensor_scan(xrow[:, :], spanf[:, :], zrow[:, :], 0.0, ALU.add,
                                                     ALU.add).then_inc(v, 1)
                        nc.vector.memset(ctrl[0:1, NG:NG + 1], 0)
                        dve.wait_ge(v, 7)
                        nc.vector.tensor_copy(ctrl[0:1, NG + 1:2 * NG + 1], xrow[:, :])
                        n_done = 0
                        for b, (a, n) in enumerate(blocks):
                            for k, dest in enumerate((relT, srcT, ewT)):
                                n_done += 1
                                dve.wait_ge(turned, n_done)
                                nc.vector.tensor_copy(
                                    dest[:, a * TI:(a + n) * TI].rearrange("p (g i) -> p i g", i=TI),
                                    ps_t[k][:, :, 0:n]).then_inc(copied, 1)
                        dve.wait_ge(bmade, 1)
                        dve.wait_ge(copied, 3 * NB)
                        rv = relT[:, :].rearrange("p (g i) -> p g i", i=TI)
                        nc.vector.tensor_tensor(rv, rv, ps_b[:, :].unsqueeze(2).broadcast_to([P, NG, TI]),
                                                ALU.subtract).then_inc(v, 1)
                        dve.wait_ge(consts, 2)
                        nc.vector.tensor_scalar(nbase[:, :], ps_b[0:W, :], pidx[0:W, :], None, ALU.add).then_inc(v, 1)
                        dve.wait_ge(v, 9)

                    @block.tensor
                    def _(pe):
                        pe.wait_ge(consts, 1)
                        pe.wait_ge(lasted, 1)
                        for b, (a, n) in enumerate(blocks):
                            nc.tensor.transpose(ps_r[0:1, 0, a:a + n], d_f[0:n, b, 0:1], ident[0:n, 0:n])
                            m = nc.tensor.transpose(ps_r[0:1, 1, a:a + n], last[0:n, b:b + 1], ident[0:n, 0:n])
                        m.then_inc(rowed, 1)
                        pe.wait_ge(cast, 3)
                        for b, (a, n) in enumerate(blocks):
                            if b:
                                pe.wait_ge(copied, 3 * b)
                            for k, tile in enumerate((d_f, s_f, w_f)):
                                tv = tile[0:n, b, :].rearrange("g (p i) -> g i p", i=TI)
                                for i in range(TI):
                                    m = nc.tensor.transpose(ps_t[k][:, i, 0:n], tv[:, i, :], ident[0:n, 0:n])
                                m.then_inc(turned, 1)
                        pe.wait_ge(based, 1)
                        pe.wait_ge(filled2, 1)
                        nc.tensor.matmul(ps_b[:, :], ones[0:1, :], frow[0:1, :], start=True, stop=True).then_inc(bmade, 1)

        def weights():
            with ExitStack() as scope:
                sb, ps = scoped(scope, "wt")
                names = dict(W_g1="L0_gnn_W_g1", W_g2="L0_gnn_W_g2", Wl1="L2_gnn_Wl1", Wr1="L2_gnn_Wr1",
                             Wl2="L2_gnn_Wl2", Wr2="L2_gnn_Wr2", Wl3="L2_gnn_Wl3", Wr3="L2_gnn_Wr3",
                             W_rel="L3_gnn_W_rel", W_root="L3_gnn_W_root", W_le="L0_gnn_W_le")
                raw = {n: sb("w" + n, [P, KH, D]) for n in names}
                w_leT = sb("w_leT", [P, KH, D])
                targets = {**{n: wT[n] for n in names if n != "W_le"}, "W_le": w_leT}
                we2 = sb("we2", [P, KH, D])
                we1 = sb("we1", [P, KH, 65])
                CD = ins["L1_gnn_Wc"].shape[1]
                POS = D - CD
                D4 = DH // 4
                wc = sb("wc", [P, KH, CD])
                wp_ = sb("wp", [H * D4, POS])
                av = [sb(f"av{j}", [P, KH]) for j in range(2)]
                ap_ = sb("ap", [H * D4, 2])
                avm = sb("avm", [P, KH, 2 * H])
                apm = sb("apm", [H * D4, 2 * H])
                hm_c = sb("hm_c", [P, KH, H])
                hm_p = sb("hm_p", [H * D4, H])
                comb = sb("comb", [P, H, 2])
                be2 = sb("be2", [P, KH])
                be2b = sb("be2b", [P, KH, P])
                vrow = sb("vrow", [2 * H, D])
                wpz = sb("wpz", [H * D4, D])
                wcz = sb("wcz", [P, KH, D])
                onesb = sb("onesb", [P, P])
                ps_w = [ps(f"ps_w{i}", [P, 512]) for i in range(2)]
                ps_f = [ps(f"ps_f{i}", [P, 256]) for i in range(2)]
                ps_c = ps("ps_c", [P, 256])
                ps_v = ps("ps_v", [2 * H, D])
                ps_vt = ps("ps_vt", [P, KH, 2 * H])
                loads = []
                for n, k in names.items():
                    loads.append((raw[n][:, :, :], ins[k].rearrange("(h p) c -> p h c", p=P)))
                loads.append((we2[:, :, :], ins["L0_gnn_W_e2"].rearrange("(h p) c -> p h c", p=P)))
                loads.append((we1[:, :, 1:65], ins["L0_gnn_W_e1"].rearrange("(h p) c -> p h c", p=P)))
                loads.append((wc[:, :, :], ins["L1_gnn_Wc"].rearrange("(h p) c -> p h c", p=P)))
                loads.append((wp_[:, :], ins["L1_gnn_Wp"]))
                for j, n in enumerate(("attn_src", "attn_dst")):
                    loads.append((av[j][:, :], ins["L1_gnn_" + n].rearrange("o (a b) d -> (b d) (o a)", a=KH)))
                for j, n in enumerate(("pos_attn_src", "pos_attn_dst")):
                    loads.append((ap_[:, j:j + 1], ins["L1_gnn_" + n].rearrange("o a (d z) -> (o a d) z", z=1)))
                loads.append((comb[:, :, :], ins["L1_gnn_att_comb"].unsqueeze(0).broadcast_to([P, H, 2])))
                loads.append((be2[:, :], ins["L0_gnn_b_e2"].rearrange("(h p) -> p h", p=P)))
                for n, k in dict(b_le="L0_gnn_b_le", b_g1="L0_gnn_b_g1", b_g2="L0_gnn_b_g2", bl1="L2_gnn_bl1",
                                 bl2="L2_gnn_bl2", bl3="L2_gnn_bl3").items():
                    loads.append((rows_of[n][:, :], ins[k].unsqueeze(0).broadcast_to([P, D])))
                for n, k in dict(b_e1="L0_gnn_b_e1", ln_g="L0_gnn_ln_g", ln_b="L0_gnn_ln_b", b_rel="L3_gnn_b_rel",
                                 gamma="L3_gnn_gamma", beta="L3_gnn_beta").items():
                    loads.append((cols_of[n][:, :], ins[k].rearrange("(h p) -> p h", p=P)))
                (loaded, turned, copied, fused, v, vmade, vturned, made, c2made, spread) = sems(
                    "wt", "loaded turned copied fused v vmade vturned made c2made spread")
                order = ["W_le"] + [n for n in names if n != "W_le"]
                with nc.Block() as block:
                    @block.sync
                    def _(sp):
                        with nc.allow_non_contiguous_dma(reason="a few vectors by feature, once"):
                            for o, i in loads:
                                sp.dma_start(o, i).then_inc(loaded, 16)
                        sp.wait_ge(loaded, 16 * len(loads))

                    @block.gpsimd
                    def _(pool):
                        for k, (t, width) in enumerate(((hm_c[:, 0, :], DH), (hm_c[:, 1, :], DH), (hm_p[:, :], D4))):
                            base = P if k == 1 else 0
                            nc.gpsimd.memset(t, 1.0).then_inc(made, 1)
                            pool.wait_ge(made, 3 * k + 1)
                            nc.gpsimd.affine_select(out=t, in_=t, compare_op=ALU.is_ge, fill=0.0, base=base,
                                                    pattern=[[-width, H]], channel_multiplier=1).then_inc(made, 1)
                            pool.wait_ge(made, 3 * k + 2)
                            nc.gpsimd.affine_select(out=t, in_=t, compare_op=ALU.is_ge, fill=0.0,
                                                    base=width - 1 - base, pattern=[[width, H]],
                                                    channel_multiplier=-1).then_inc(made, 1)
                        pool.wait_ge(made, 9)

                    @block.vector
                    def _(dve):
                        nc.vector.memset(onesb[:, :], 1.0)
                        nc.vector.memset(we1[:, :, 0:1], 0.0)
                        nc.vector.memset(wpz[:, :], 0.0)
                        nc.vector.memset(wcz[:, :, :], 0.0).then_inc(spread, 1)
                        dve.wait_ge(loaded, 16 * len(loads))
                        dve.wait_ge(spread, 1)
                        nc.vector.tensor_copy(wpz[:, CD:D], wp_[:, :])
                        nc.vector.tensor_copy(wcz[:, :, 0:CD], wc[:, :, :])
                        for k in range(KH):
                            m = nc.vector.tensor_scalar(be2b[:, k, :], onesb[:, :], be2[:, k:k + 1], None, ALU.mult)
                        m.then_inc(spread, 1)
                        dve.wait_ge(made, 9)
                        for j in range(2):
                            for k in range(KH):
                                m = nc.vector.tensor_tensor(avm[:, k, j * H:(j + 1) * H], hm_c[:, k, :],
                                                            comb[:, :, 0], ALU.mult)
                            m = nc.vector.tensor_tensor(apm[:, j * H:(j + 1) * H], hm_p[:, :],
                                                        comb[0:H * D4, :, 1], ALU.mult)
                        m.then_inc(v, 1)
                        dve.wait_ge(v, 1)
                        for j in range(2):
                            for k in range(KH):
                                m = nc.vector.tensor_scalar(avm[:, k, j * H:(j + 1) * H], avm[:, k, j * H:(j + 1) * H],
                                                            av[j][:, k:k + 1], None, ALU.mult)
                            m = nc.vector.tensor_scalar(apm[:, j * H:(j + 1) * H], apm[:, j * H:(j + 1) * H],
                                                        ap_[:, j:j + 1], None, ALU.mult)
                        m.then_inc(v, 1)
                        for s, n in enumerate(order + ["Wc"]):
                            dest = wT["attn"][:, :, 0:D] if n == "Wc" else targets[n][:, :, :]
                            dve.wait_ge(turned, s + 1)
                            nc.vector.tensor_copy(dest, ps_w[s % 2][:, :].rearrange("p (h o) -> p h o", h=KH)
                                                  ).then_inc(copied, 1)
                        s = len(order) + 1
                        dve.wait_ge(turned, s + 1)
                        nc.vector.tensor_copy(w_e1T[:, :], ps_w[s % 2][0:65, 0:D]).then_inc(copied, 1)
                        dve.wait_ge(fused, 1)
                        for k in range(KH):
                            nc.vector.tensor_copy(wT["fuse"][:, k, :], ps_f[k][:, :])
                        nc.vector.tensor_copy(rows_of["c2"][:, :], ps_c[:, :])
                        dve.wait_ge(vmade, 1)
                        nc.vector.tensor_copy(vrow[:, :], ps_v[:, :]).then_inc(v, 1)
                        dve.wait_ge(vturned, 1)
                        nc.vector.tensor_copy(wT["attn"][:, :, D:D + 2 * H], ps_vt[:, :, :]).then_inc(v, 1)
                        dve.wait_ge(v, 4)

                    @block.tensor
                    def _(pe):
                        pe.wait_ge(loaded, 16 * len(loads))
                        pe.wait_ge(spread, 2)
                        for s, n in enumerate(order + ["Wc"]):
                            if s >= 2:
                                pe.wait_ge(copied, s - 1)
                            tile = wcz if n == "Wc" else raw[n]
                            for k in range(KH):
                                for a in range(KH):
                                    m = nc.tensor.transpose(ps_w[s % 2][:, k * D + a * P:k * D + (a + 1) * P],
                                                            tile[:, a, k * P:(k + 1) * P], ident[:, :])
                            m.then_inc(turned, 1)
                        s = len(order) + 1
                        pe.wait_ge(copied, s - 1)
                        for a in range(KH):
                            m = nc.tensor.transpose(ps_w[s % 2][0:65, a * P:(a + 1) * P], we1[:, a, :], ident[:, :])
                        m.then_inc(turned, 1)
                        for k in range(KH):
                            for a in range(KH):
                                nc.tensor.matmul(ps_f[k][:, :], we2[:, a, k * P:(k + 1) * P], w_leT[:, a, :],
                                                 start=(a == 0), stop=(a == KH - 1))
                        for a in range(KH):
                            m = nc.tensor.matmul(ps_c[:, :], be2b[:, a, :], w_leT[:, a, :], start=(a == 0),
                                                 stop=(a == KH - 1))
                        m.then_inc(fused, 1)
                        pe.wait_ge(v, 2)
                        for a in range(KH):
                            nc.tensor.matmul(ps_v[:, :], avm[:, a, :], wcz[:, a, :], start=(a == 0), stop=False)
                        nc.tensor.matmul(ps_v[:, :], apm[:, :], wpz[:, :], start=False, stop=True).then_inc(vmade, 1)
                        pe.wait_ge(v, 3)
                        for k in range(KH):
                            m = nc.tensor.transpose(ps_vt[:, k, :], vrow[:, k * P:(k + 1) * P],
                                                    ident[0:2 * H, 0:2 * H])
                        m.then_inc(vturned, 1)

        def first_table():
            with ExitStack() as scope:
                sb, ps = scoped(scope, "ft")
                xt = [sb(f"xt{i}", [P, D]) for i in range(4)]
                xb = [sb(f"xb{i}", [P, D]) for i in range(4)]
                ps_x = [ps(f"ps_x{i}", [P, KH, P]) for i in range(4)]
                added, turned, moved, cleared = sems("ft", "added turned moved cleared")
                loaded = sems("ft", "ld0 ld1 ld2 ld3")
                stored = sems("ft", "st0 st1 st2 st3")
                with nc.Block() as block:
                    @block.sync
                    def _(sp):
                        def load(t, s, v):
                            r = rows(t)
                            if later(t, 4):
                                sp.wait_ge(added, t - 3)
                                sp.wait_ge(turned, t - 3)
                            sp.dma_start(xt[s][0:r, :], ins["x"][bass.ds(t * P, r), :]).then_inc(loaded[s], 16)

                        def store(t, s, v):
                            r = rows(t)
                            sp.wait_ge(added, t + 1)
                            sp.dma_start(t_x0[bass.ds(t * P, r), :], xb[s][0:r, :]).then_inc(stored[s], 16)

                        pipelined(sp, NT, 4, [(0, load), (3, store)])
                        for s in range(4):
                            n = len(range(s, NT, 4))
                            if n:
                                sp.wait_ge(stored[s], 16 * n)

                    @block.vector
                    def _(dve):
                        def add(t, s, v):
                            r = rows(t)
                            dve.wait_ge(loaded[s], (v + 1) * 16)
                            if later(t, 4):
                                dve.wait_ge(stored[s], v * 16)
                            nc.vector.tensor_tensor(xb[s][0:r, :], xt[s][0:r, :], rows_of["b_le"][0:r, :],
                                                    ALU.add).then_inc(added, 1)
                        pipelined(dve, NT, 4, [(0, add)])

                    @block.tensor
                    def _(pe):
                        def turn(t, s, v):
                            r = rows(t)
                            pe.wait_ge(loaded[s], (v + 1) * 16)
                            if later(t, 4):
                                pe.wait_ge(moved, t - 3)
                            for k in range(KH):
                                m = nc.tensor.transpose(ps_x[s][:, k, 0:r], xt[s][0:r, k * P:(k + 1) * P],
                                                        ident[0:r, 0:r])
                            m.then_inc(turned, 1)
                        pipelined(pe, NT, 4, [(0, turn)])

                    @block.scalar
                    def _(act):
                        def move(t, s, v):
                            r = rows(t)
                            act.wait_ge(turned, t + 1)
                            nc.scalar.activation(agg[:, :, bass.ds(t * P, r)], ps_x[s][:, :, 0:r],
                                                 ACT.Copy).then_inc(moved, 1)
                        pipelined(act, NT, 4, [(0, move)])
                        act.wait_ge(moved, NT)

                    @block.gpsimd
                    def _(pool):
                        nc.gpsimd.memset(agg[:, :, N:NW], 0.0).then_inc(cleared, 1)
                        nc.gpsimd.memset(den, 0.0).then_inc(cleared, 1)
                        pool.wait_ge(cleared, 2)

        def edge_phase(tag, kind, table, width):
            mlp, attn = kind == "mlp", kind == "attn"
            with ExitStack() as scope:
                sb, ps = scoped(scope, tag)
                G = [sb(f"G{s}", [P, TI, width]) for s in range(RING)]
                oh = [sb(f"oh{i}", [P, TI, W]) for i in range(2)]
                xoh = sb("xoh", [P, TI, W])
                xrel = sb("xrel", [P, TI])
                ps_s = [ps(f"ps_s{i}", [P, KH + 1, W]) for i in range(2)]
                ps_x = ps("ps_x", [P, KH + 1, W])
                if mlp or attn:
                    msg = [sb(f"msg{i}", [P, TI, D]) for i in range(2)]
                if mlp:
                    attr = [sb(f"attr{i}", [P, TI, 65]) for i in range(2)]
                    attrT = [sb(f"attrT{i}", [65, GE]) for i in range(2)]
                    hid = [sb(f"hid{i}", [P, KH, GE]) for i in range(2)]
                    gate = [sb(f"gate{i}", [P, TI]) for i in range(2)]
                    emb = sb("emb", [P, TI, D])
                    ps_a = ps("ps_a", [65, GE])
                    ps_h = ps("ps_h", [P, KH, GE])
                    ps_e = ps("ps_e", [P, TI, D])
                if attn:
                    dstb = [sb(f"dstb{i}", [W, GE], I32) for i in range(RING)]
                    bound = [sb(f"bound{i}", [H, GE + 1]) for i in range(RING)]
                    dwin = [sb(f"dwin{i}", [W, PARTS * H], BF16) for i in range(RING)]
                    dwinx = sb("dwinx", [W, PARTS * H], BF16)
                    ohT = [sb(f"ohT{i}", [W, GE], BF16) for i in range(2)]
                    ohTx = sb("ohTx", [W, GE], BF16)
                    nbx = sb("nbx", [W, 1])
                    nothing = sb("nothing", [W, TI * PARTS * H], BF16)
                    dsum = sb("dsum", [P, TI, H])
                    esc = [sb(f"esc{i}", [P, TI, H]) for i in range(3)]
                    leaky = [sb(f"leaky{i}", [P, TI, H]) for i in range(3)]
                    bel = [sb(f"bel{i}", [P, TI, H]) for i in range(2)]
                    run = [sb(f"run{i}", [H, GE]) for i in range(2)]
                    top = [sb(f"top{i}", [H, GE]) for i in range(2)]
                    eeo = [sb(f"eeo{i}", [P, TI, H + 1]) for i in range(2)]
                    shift = sb("shift", [H, 1 + KH])
                    ownhalf = sb("ownhalf", [H, 1 + KH])
                    resc = [sb(f"resc{i}", [H, 1 + KH]) for i in range(RING)]
                    rescf = [sb(f"rescf{i}", [P, KH]) for i in range(RING)]
                    floor = sb("floor", [H, 1])
                    ps_d = ps("ps_d", [P, TI, PARTS * H])
                    ps_l = [ps(f"ps_l{i}", [H, GE]) for i in range(2)]
                    ps_top = [ps(f"ps_top{i}", [P, TI * H + KH]) for i in range(2)]
                gathered = sems(tag, " ".join(f"gathered{s}" for s in range(RING)))
                (indexed, onehot, summed, merged, xonehot, xsummed, xmerged, xv, xv2) = sems(
                    tag, "indexed onehot summed merged xonehot xsummed xmerged xv xv2")
                if kind == "weighted":
                    unweighted, = sems(tag, "unweighted")
                if mlp:
                    (turned, attred, hidden, relued, embedded, biased, gated, gated1, premsg, messaged) = sems(
                        tag, "turned attred hidden relued embedded biased gated gated1 premsg messaged")
                    attr_in = sems(tag, "attr_in0 attr_in1")
                if attn:
                    (windowed, expanded, dadded, added, leaked, sturned, ran, topped, rescaled, spread,
                     belowed, eemade, messaged, messaged_a, rmul, shifted, onesset, xnb, xohT, xd) = sems(
                        tag, "windowed expanded dadded added leaked sturned ran topped rescaled spread "
                             "belowed eemade messaged messaged_a rmul shifted onesset xnb xohT xd")
                    edge_in = sems(tag, " ".join(f"edge_in{s}" for s in range(RING)))
                    xwin, = sems(tag, "xwin")

                def operand(g, s):
                    return msg[s % 2] if mlp or attn else G[s]

                with nc.Block() as block:
                    @block.gpsimd
                    def _(pool):
                        def gather(g, s, v):
                            pool.wait_ge(indexed, g + 1)
                            if later(g, RING):
                                if mlp or attn:
                                    pool.wait_ge(messaged if attn else premsg, (g - RING + 1))
                                    if attn:
                                        pool.wait_ge(messaged_a, (g - RING + 1))
                                else:
                                    pool.wait_ge(summed, g - RING + 1)
                            pool.nop(nofuse=True)
                            for i in range(TI):
                                nc.gpsimd.indirect_dma_start(
                                    out=G[s][:, i, :], out_offset=None, in_=table,
                                    in_offset=bass.IndirectOffsetOnAxis(ap=idx[s][:, i:i + 1], axis=0),
                                ).then_inc(gathered[s], 16)
                        pipelined(pool, NG, RING, [(0, gather)])

                    @block.sync
                    def _(sp):
                        if mlp:
                            def load(g, s, v):
                                b = s % 2
                                if later(g, 2):
                                    sp.wait_ge(turned, g - 1)
                                    sp.wait_ge(gated1, g - 1)
                                n = TAILP if isinstance(g, int) and g == NG - 1 else P
                                src = ins["edge_attr_65"][bass.ds(g * GE, n * TI), :]
                                sp.dma_start(attr[b][0:n, :, :], src.rearrange("(p i) c -> p i c", i=TI)
                                             ).then_inc(attr_in[b], 16)
                            pipelined(sp, NG, RING, [(0, load)])
                        if attn:
                            def load(g, s, v):
                                if later(g, RING):
                                    sp.wait_ge(expanded, g - RING + 1)
                                    sp.wait_ge(topped, g - RING + 1)
                                n = TAILP * TI if isinstance(g, int) and g == NG - 1 else GE
                                sp.dma_start(dstb[s][:, 0:n],
                                             ins["dst"][bass.ds(g * GE, n)].unsqueeze(0).broadcast_to([W, n])
                                             ).then_inc(edge_in[s], 16)
                                sp.dma_start(bound[s][:, 0:GE],
                                             t_flag[bass.ds(g, 1), :].broadcast_to([H, GE])
                                             ).then_inc(edge_in[s], 16)
                                first = first_dst(sp, g)
                                sp.dma_start(dwin[s][:, :], t_dst[bass.ds(first, W), :]).then_inc(edge_in[s], 16)
                                if not far[0]:
                                    return
                                lo, hi = extra_lo(sp, g), extra_hi(sp, g)
                                with between(sp, lo, hi) as q:
                                    sp.wait_ge(xd, q + 1)
                                    at = bounded(sp, first + (q - lo + 1) * W, N)
                                    sp.dma_start(dwinx[:, :], t_dst[bass.ds(at, W), :]).then_inc(xwin, 16)
                            either(sp, lambda: pipelined(sp, NG, RING, [(0, load)]))

                    @block.vector
                    def _(dve):
                        def index(g, s, v):
                            if later(g, RING):
                                dve.wait_ge(gathered[s], v * 64)
                            nc.vector.tensor_copy(idx[s][:, :], srcT[:, bass.ds(g * TI, TI)]).then_inc(indexed, 1)

                        def window(g, s, v):
                            b = s % 2
                            if later(g, 2):
                                dve.wait_ge(summed, g - 1)
                            rel = relT[:, bass.ds(g * TI, TI)]
                            m = nc.vector.tensor_tensor(
                                oh[b][:, :, :], rel.unsqueeze(2).broadcast_to([P, TI, W]),
                                iotaw[:, :].unsqueeze(1).broadcast_to([P, TI, W]), ALU.is_equal)
                            if kind == "weighted":
                                m.then_inc(unweighted, 1)
                                dve.wait_ge(unweighted, g + 1)
                                m = nc.vector.tensor_tensor(
                                    oh[b][:, :, :], oh[b][:, :, :],
                                    ewT[:, bass.ds(g * TI, TI)].unsqueeze(2).broadcast_to([P, TI, W]), ALU.mult)
                            m.then_inc(onehot, 1)

                        def further(g, s, v):
                            if not far[0]:
                                return
                            lo, hi = extra_lo(dve, g), extra_hi(dve, g)
                            first = first_dst(dve, g)
                            with between(dve, lo, hi) as q:
                                k = q - lo + 1
                                dve.wait_ge(xmerged, q * (2 if attn else 1) + 1)
                                nc.vector.tensor_scalar(xrel[:, :], relT[:, bass.ds(g * TI, TI)],
                                                        starts[:, bass.ds(bounded(dve, k, MAXX - 1), 1)],
                                                        None, ALU.subtract).then_inc(xv, 1)
                                dve.wait_ge(xv, q + 1)
                                m = nc.vector.tensor_tensor(
                                    xoh[:, :, :], xrel[:, :].unsqueeze(2).broadcast_to([P, TI, W]),
                                    iotaw[:, :].unsqueeze(1).broadcast_to([P, TI, W]), ALU.is_equal)
                                if kind != "weighted":
                                    m.then_inc(xonehot, 1)
                                else:
                                    m.then_inc(xv2, 1)
                                    dve.wait_ge(xv2, q + 1)
                                    nc.vector.tensor_tensor(
                                        xoh[:, :, :], xoh[:, :, :],
                                        ewT[:, bass.ds(g * TI, TI)].unsqueeze(2).broadcast_to([P, TI, W]),
                                        ALU.mult).then_inc(xonehot, 1)
                                dve.wait_ge(xsummed, q + 1)
                                at = bounded(dve, first + k * W, N)
                                nc.vector.tensor_tensor(agg[:, :, bass.ds(at, W)], agg[:, :, bass.ds(at, W)],
                                                        ps_x[:, 0:KH, :], ALU.add).then_inc(xmerged, 1)
                                if attn:
                                    nc.vector.tensor_tensor(den[:, bass.ds(at, W)], den[:, bass.ds(at, W)],
                                                            ps_x[0:H + 1, KH, :], ALU.add).then_inc(xmerged, 1)

                        def merge(g, s, v):
                            b = s % 2
                            first = first_dst(dve, g)
                            if far[0]:
                                hi = extra_hi(dve, g)
                            dve.wait_ge(summed, g + 1)
                            x2 = 2 if attn else 1
                            if later(g, 1):
                                dve.wait_ge(merged, g * x2)
                            if far[0]:
                                dve.wait_ge(xmerged, hi * x2 + 1)
                            if attn:
                                dve.wait_ge(eemade, g * 2 + 2)
                                nc.vector.tensor_tensor(agg[:, :, bass.ds(first, 1)], agg[:, :, bass.ds(first, 1)],
                                                        rescf[s][:, :].unsqueeze(2),
                                                        ALU.mult).then_inc(rmul, 1)
                                nc.vector.tensor_tensor(den[0:H, bass.ds(first, 1)], den[0:H, bass.ds(first, 1)],
                                                        resc[s][:, 0:1], ALU.mult).then_inc(rmul, 1)
                                dve.wait_ge(rmul, g * 2 + 2)
                            nc.vector.tensor_tensor(agg[:, :, bass.ds(first, W)], agg[:, :, bass.ds(first, W)],
                                                    ps_s[b][:, 0:KH, :], ALU.add).then_inc(merged, 1)
                            if attn:
                                nc.vector.tensor_tensor(den[:, bass.ds(first, W)], den[:, bass.ds(first, W)],
                                                        ps_s[b][0:H + 1, KH, :], ALU.add).then_inc(merged, 1)

                        def mlp_gate(g, s, v):
                            b = s % 2
                            dve.wait_ge(attr_in[b], came(s, v, 2, RING, 16))
                            if later(g, 2):
                                dve.wait_ge(premsg, g - 1)
                            nc.vector.tensor_scalar(gate[b][:, :], attr[b][:, :, 0], 0.0, 1.0, ALU.max,
                                                    ALU.min).then_inc(gated1, 1)
                            dve.wait_ge(gated1, g + 1)
                            nc.vector.tensor_scalar(gate[b][:, :], gate[b][:, :], 0.01, None,
                                                    ALU.add).then_inc(gated, 1)

                        def mlp_message(g, s, v):
                            b = s % 2
                            dve.wait_ge(embedded, g + 1)
                            if later(g, 1):
                                dve.wait_ge(premsg, g)
                            nc.vector.tensor_tensor(emb[:, :, :], ps_e[:, :, :],
                                                    rows_of["c2"][:, :].unsqueeze(1).broadcast_to([P, TI, D]),
                                                    ALU.add).then_inc(biased, 1)
                            dve.wait_ge(biased, g + 1)
                            dve.wait_ge(gated, g + 1)
                            dve.wait_ge(gathered[s], came(s, v, RING, RING, 64))
                            if later(g, 2):
                                dve.wait_ge(summed, g - 1)
                            for i in range(TI):
                                m = nc.vector.scalar_tensor_tensor(
                                    out=msg[b][:, i, :], in0=emb[:, i, :], scalar=gate[b][:, i:i + 1],
                                    in1=G[s][:, i, :], op0=ALU.mult, op1=ALU.add)
                            m.then_inc(premsg, 1)

                        def attn_expand(g, s, v):
                            b = s % 2
                            dve.wait_ge(edge_in[s], came(s, v, RING, RING, 48))
                            if later(g, 2):
                                dve.wait_ge(expanded, g - 1)
                            nc.vector.tensor_scalar(ohT[b][:, :], dstb[s][:, :], nbase[:, bass.ds(g, 1)], None,
                                                    ALU.is_equal).then_inc(windowed, 1)
                            if not far[0]:
                                return
                            lo, hi = extra_lo(dve, g), extra_hi(dve, g)
                            with between(dve, lo, hi) as q:
                                k = q - lo + 1
                                dve.wait_ge(xd, q + 1)
                                nc.vector.tensor_tensor(
                                    nbx[:, :], nbase[:, bass.ds(g, 1)],
                                    starts[0:W, bass.ds(bounded(dve, k, MAXX - 1), 1)],
                                    ALU.add).then_inc(xnb, 1)
                                dve.wait_ge(xnb, q + 1)
                                nc.vector.tensor_scalar(ohTx[:, :], dstb[s][:, :], nbx[:, :], None,
                                                        ALU.is_equal).then_inc(xohT, 1)

                        def attn_leaky(g, s, v):
                            dve.wait_ge(expanded, g + 1)
                            nc.vector.tensor_reduce(dsum[:, :, :],
                                                    ps_d[:, :, :].rearrange("p i (c h) -> p i h c", h=H), AX.X,
                                                    ALU.add).then_inc(dadded, 1)
                            dve.wait_ge(gathered[s], came(s, v, RING, RING, 64))
                            dve.wait_ge(dadded, g + 1)
                            nc.vector.tensor_tensor(esc[s % 3][:, :, :], dsum[:, :, :], G[s][:, :, D:D + H],
                                                    ALU.add).then_inc(added, 1)
                            dve.wait_ge(added, g + 1)
                            nc.vector.scalar_tensor_tensor(out=leaky[s % 3][:, :, :], in0=esc[s % 3][:, :, :],
                                                           scalar=0.2, in1=esc[s % 3][:, :, :], op0=ALU.mult,
                                                           op1=ALU.max).then_inc(leaked, 1)

                        def attn_scan(g, s, v):
                            b = s % 2
                            dve.wait_ge(sturned, g + 1)
                            prev = run[1 - b][:, GE - 1:GE] if later(g, 1) else floor[:, :]
                            nc.vector.tensor_tensor_scan(run[b][:, :], bound[s][:, 0:GE], ps_l[b][:, :], prev,
                                                         ALU.min, ALU.max).then_inc(ran, 1)
                            dve.wait_ge(ran, g + 1)
                            if later(g, 2):
                                dve.wait_ge(spread, g - 1)
                            nc.vector.tensor_tensor_scan(top[b][:, ::-1], bound[s][:, GE:0:-1], run[b][:, ::-1],
                                                         -BIG, ALU.min, ALU.max).then_inc(topped, 1)
                            dve.wait_ge(topped, g + 1)
                            if later(g, 1):
                                dve.wait_ge(rescaled, g)
                            nc.vector.scalar_tensor_tensor(out=shift[:, :], in0=prev.broadcast_to([H, 1 + KH]),
                                                           scalar=top[b][:, 0:1], in1=ownhalf[:, :],
                                                           op0=ALU.subtract, op1=ALU.min).then_inc(shifted, 1)

                        def attn_below(g, s, v):
                            b = s % 2
                            dve.wait_ge(spread, g + 1)
                            if later(g, 2):
                                dve.wait_ge(eemade, (g - 1) * 2)
                            nc.vector.tensor_tensor(bel[b][:, :, :], leaky[s % 3][:, :, :],
                                                    ps_top[b][:, 0:TI * H].rearrange("p (i h) -> p i h", h=H),
                                                    ALU.subtract).then_inc(belowed, 1)

                        def attn_message(g, s, v):
                            b = s % 2
                            dve.wait_ge(eemade, g * 2 + 1)
                            dve.wait_ge(gathered[s], came(s, v, RING, RING, 64))
                            if later(g, 2):
                                dve.wait_ge(summed, g - 1)
                            n = TI - ACT_TI
                            nc.vector.tensor_tensor(
                                msg[b][:, 0:n, :].rearrange("p i (h d) -> p i h d", h=H),
                                G[s][:, 0:n, 0:D].rearrange("p i (h d) -> p i h d", h=H),
                                eeo[b][:, 0:n, 0:H].unsqueeze(3).broadcast_to([P, n, H, DH]), ALU.mult).then_inc(messaged, 1)

                        nc.vector.memset(xrel[:, :], 0.0).then_inc(xmerged, 1)
                        if attn:
                            nc.vector.memset(nbx[:, :], 0.0).then_inc(xd, 1)
                            nc.vector.memset(eeo[0][:, :, H:H + 1], 1.0)
                            nc.vector.memset(eeo[1][:, :, H:H + 1], 1.0)
                            nc.vector.memset(floor[:, :], -BIG)
                            nc.vector.memset(ownhalf[:, 0:1], 0.0)
                            nc.vector.memset(nothing[:, :], 0.0)
                            for i in range(RING):
                                m = nc.vector.memset(bound[i][:, GE:GE + 1], BIG)
                            m.then_inc(onesset, 1)
                            for k in range(KH):
                                hm = headmask[:, k * P:(k + 1) * P:DH]
                                m = nc.vector.tensor_reduce(ownhalf[:, 1 + k:2 + k], hm, AX.X, ALU.add)
                            m.then_inc(onesset, 1)
                            dve.wait_ge(onesset, 2)
                            nc.vector.tensor_scalar(ownhalf[:, 1:], ownhalf[:, 1:], BIG, -BIG, ALU.mult,
                                                    ALU.add).then_inc(onesset, 1)
                            dve.wait_ge(onesset, 3)
                        if mlp:
                            stages = [(1 - RING, index), (0, mlp_gate), (3, further), (4, merge), (1, window),
                                      (1, mlp_message)]
                        elif attn:
                            stages = [(3, attn_below), (5, further), (1, attn_leaky), (0, attn_expand),
                                      (2, attn_scan), (5, merge), (3, window), (3, attn_message),
                                      (1 - RING, index)]
                        else:
                            stages = [(1 - RING, index), (0, window), (0, further), (1, merge)]
                        either(dve, lambda: pipelined(dve, NG, RING, stages))
                        dve.wait_ge(merged, NG * (2 if attn else 1))

                    @block.tensor
                    def _(pe):
                        def segment_sum(o, m, w, slot_ee):
                            for k in range(KH):
                                for i in range(TI):
                                    last = nc.tensor.matmul(o[:, k, :], m[:, i, k * P:(k + 1) * P], w[:, i, :],
                                                            start=(i == 0), stop=(i == TI - 1))
                            if attn:
                                for i in range(TI):
                                    last = nc.tensor.matmul(o[0:H + 1, KH, :], slot_ee[:, i, :], w[:, i, :],
                                                            start=(i == 0), stop=(i == TI - 1))
                            return last

                        def summing(g, s, v):
                            b = s % 2
                            if far[0]:
                                lo, hi = extra_lo(pe, g), extra_hi(pe, g)
                            if mlp or attn:
                                pe.wait_ge(messaged, g + 1)
                                if attn:
                                    pe.wait_ge(messaged_a, g + 1)
                            else:
                                pe.wait_ge(gathered[s], came(s, v, RING, RING, 64))
                            pe.wait_ge(onehot, g + 1)
                            slot_ee = eeo[b] if attn else None
                            if far[0]:
                                pe.nop(nofuse=True)
                                with between(pe, lo, hi) as q:
                                    pe.wait_ge(xonehot, q + 1)
                                    segment_sum(ps_x, operand(g, s), xoh, slot_ee).then_inc(xsummed, 1)
                            if later(g, 2):
                                pe.wait_ge(merged, (g - 1) * (2 if attn else 1))
                            segment_sum(ps_s[b], operand(g, s), oh[b], slot_ee).then_inc(summed, 1)

                        def mlp_turn(g, s, v):
                            b = s % 2
                            pe.wait_ge(attr_in[b], came(s, v, 2, RING, 16))
                            if later(g, 1):
                                pe.wait_ge(attred, g)
                            for i in range(TI):
                                m = nc.tensor.transpose(ps_a[:, i * P:(i + 1) * P], attr[b][:, i, :], ident[:, :])
                            m.then_inc(turned, 1)

                        def mlp_hidden(g, s, v):
                            b = s % 2
                            pe.wait_ge(attred, g + 1)
                            if later(g, 1):
                                pe.wait_ge(relued, g * KH)
                            for k in range(KH):
                                nc.tensor.matmul(ps_h[:, k, :], w_e1T[:, k * P:(k + 1) * P], attrT[b][:, :],
                                                 start=True, stop=True).then_inc(hidden, 1)

                        def mlp_embed(g, s, v):
                            b = s % 2
                            pe.wait_ge(relued, (g + 1) * KH)
                            if later(g, 1):
                                pe.wait_ge(biased, g)
                            for i in range(TI):
                                for k in range(KH):
                                    m = nc.tensor.matmul(ps_e[:, i, :], hid[b][:, k, i * P:(i + 1) * P],
                                                         wT["fuse"][:, k, :], start=(k == 0), stop=(k == KH - 1))
                            m.then_inc(embedded, 1)

                        def dst_scores(w, o, whole):
                            wv, m = o.rearrange("n (p i) -> n i p", i=TI), None
                            for i in range(TI):
                                m = nc.tensor.matmul(ps_d[:, i, :], wv[:, i, :], w, start=whole, stop=whole)
                            return m

                        def zeros(o, start):
                            return nc.tensor.matmul(ps_d[:, :, :], o[:, 0:P], nothing[:, :], start=start,
                                                    stop=not start)

                        def attn_score(g, s, v):
                            b = s % 2
                            if far[0]:
                                lo, hi = extra_lo(pe, g), extra_hi(pe, g)
                            pe.wait_ge(windowed, g + 1)
                            if later(g, 1):
                                pe.wait_ge(dadded, g)
                            pe.nop(nofuse=True)
                            if not far[0]:
                                dst_scores(dwin[s][:, :], ohT[b], True).then_inc(expanded, 1)
                                return
                            zeros(ohT[b], True)
                            dst_scores(dwin[s][:, :], ohT[b], False)
                            with between(pe, lo, hi) as q:
                                pe.wait_ge(xohT, q + 1)
                                pe.wait_ge(xwin, q * 16 + 16)
                                pe.nop(nofuse=True)
                                dst_scores(dwinx[:, :], ohTx, False).then_inc(xd, 1)
                            zeros(ohT[b], False).then_inc(expanded, 1)

                        def attn_turn(g, s, v):
                            b = s % 2
                            pe.wait_ge(leaked, g + 1)
                            if later(g, 2):
                                pe.wait_ge(ran, g - 1)
                            pe.nop(nofuse=True)
                            ov = ps_l[b].rearrange("h (p i) -> h i p", i=TI)
                            for i in range(TI):
                                m = nc.tensor.transpose(ov[:, i, :], leaky[s % 3][:, i, :], ident[:, :])
                            m.then_inc(sturned, 1)

                        def attn_spread(g, s, v):
                            b = s % 2
                            pe.wait_ge(topped, g + 1)
                            if later(g, 2):
                                pe.wait_ge(eemade, (g - 1) * 2)
                            pe.nop(nofuse=True)
                            tv = top[b][:, :].rearrange("h (p i) -> h i p", i=TI)
                            for i in range(TI):
                                nc.tensor.transpose(ps_top[b][:, i * H:(i + 1) * H], tv[:, i, :], ident[0:H, 0:H])
                            pe.wait_ge(rescaled, g + 1)
                            pe.nop(nofuse=True)
                            nc.tensor.matmul(ps_top[b][:, TI * H:], halfmask[:, :], resc[s][:, 1:], start=True,
                                             stop=True).then_inc(spread, 1)

                        if mlp:
                            stages = [(0, mlp_turn), (3, summing), (1, mlp_embed), (0, mlp_hidden)]
                        elif attn:
                            stages = [(0, attn_score), (1, attn_turn), (2, attn_spread), (4, summing)]
                        else:
                            stages = [(0, summing)]
                        either(pe, lambda: pipelined(pe, NG, RING, stages))

                    @block.scalar
                    def _(act):
                        if mlp:
                            def attr_move(g, s, v):
                                b = s % 2
                                act.wait_ge(turned, g + 1)
                                if later(g, 2):
                                    act.wait_ge(hidden, (g - 1) * KH)
                                nc.scalar.activation(attrT[b][:, :], ps_a[:, :], ACT.Copy).then_inc(attred, 1)

                            def relu_hidden(g, s, v):
                                b = s % 2
                                if later(g, 2):
                                    act.wait_ge(embedded, g - 1)
                                for k in range(KH):
                                    act.wait_ge(hidden, g * KH + k + 1)
                                    nc.scalar.activation(hid[b][:, k, :], ps_h[:, k, :], ACT.Relu,
                                                         bias=cols_of["b_e1"][:, k:k + 1]).then_inc(relued, 1)

                            def relu_message(g, s, v):
                                b = s % 2
                                act.wait_ge(premsg, g + 1)
                                nc.scalar.activation(msg[b][:, :, :], msg[b][:, :, :], ACT.Relu).then_inc(messaged, 1)

                            pipelined(act, NG, RING, [(0, attr_move), (2, relu_message), (0, relu_hidden)])
                        if attn:
                            def rescale(g, s, v):
                                act.wait_ge(shifted, g + 1)
                                if later(g, RING):
                                    act.wait_ge(merged, (g - RING + 1) * 2)
                                nc.scalar.activation(resc[s][:, :], shift[:, :], ACT.Exp).then_inc(rescaled, 1)

                            def expo(g, s, v):
                                b = s % 2
                                act.wait_ge(belowed, g + 1)
                                if later(g, 2):
                                    act.wait_ge(summed, g - 1)
                                nc.scalar.activation(eeo[b][:, :, 0:H], bel[b][:, :, :], ACT.Exp).then_inc(eemade, 1)
                                nc.scalar.activation(rescf[s][:, :], ps_top[b][:, TI * H:TI * H + KH],
                                                     ACT.Copy).then_inc(eemade, 1)

                            def message(g, s, v):
                                b = s % 2
                                act.wait_ge(gathered[s], came(s, v, RING, RING, 64))
                                act.wait_ge(eemade, g * 2 + 1)
                                for i in range(TI - ACT_TI, TI):
                                    for h in range(H):
                                        m = nc.scalar.activation(msg[b][:, i, h * DH:(h + 1) * DH],
                                                                 G[s][:, i, h * DH:(h + 1) * DH], ACT.Copy,
                                                                 scale=eeo[b][:, i, h:h + 1])
                                m.then_inc(messaged_a, 1)
                            act.wait_ge(onesset, 3)
                            pipelined(act, NG, RING, [(3, expo), (2, rescale), (3, message)])

        def node_phase(tag, kind, resid=None, rtab=None, to=None, second=None):
            mlp, attn, sage, last = (kind == k for k in ("mlp", "attn", "sage", "sagelast"))
            anysage = sage or last
            weight = wT["W_g1"] if mlp else None
            if anysage:
                weight = wT[{"n2": "Wl1", "n3": "Wl2", "n4": "Wl3"}[tag]]
            nxt = wT[{"n0": "attn", "n1": "Wr1", "n2": "Wr2", "n3": "Wr3", "n4": "W_root"}[tag]]
            nbias = {"n1": "bl1", "n2": "bl2", "n3": "bl3"}.get(tag)
            NXW = D + 2 * H if mlp else D
            OUTW = HCW if mlp else D
            B = 4
            with ExitStack() as scope:
                sb, ps = scoped(scope, tag)
                st = [sb(f"st{i}", [P, KH, P]) for i in range(B)]
                rd = [sb(f"rd{i}", [P, D]) for i in range(B)]
                rs = [sb(f"rs{i}", [P, D]) for i in range(B)] if last else rd
                y = [sb(f"y{i}", [P, D]) for i in range(B)]
                e = [sb(f"e{i}", [P, D]) for i in range(B)]
                u = [sb(f"u{i}", [P, D]) for i in range(B)]
                hT = [sb(f"hT{i}", [P, KH, P]) for i in range(B)]
                outt = [sb(f"outt{i}", [P, OUTW]) for i in range(B)]
                fin = [sb(f"fin{i}", [P, D]) for i in range(B)]
                stats = [sb(f"stats{i}", [P, 6]) for i in range(B)]
                mv = [sb(f"mv{i}", [P, 2]) for i in range(B)]
                sd = [sb(f"sd{i}", [P, 1]) for i in range(B)]
                rstd = [sb(f"rstd{i}", [P, 1]) for i in range(B)]
                dst_ = sb("dst_", [H + 1, P])
                dtile = [sb(f"dtile{i}", [P, H + 1]) for i in range(2)]
                rden = [sb(f"rden{i}", [P, H]) for i in range(2)]
                mlpT = [sb(f"mlpT{i}", [P, KH, P]) for i in range(2)]
                ps_a = [ps(f"ps_a{i}", [P, D]) for i in range(2)]
                ps_t = [ps(f"ps_t{i}", [P, KH, P]) for i in range(2)]
                ps_n = [ps(f"ps_n{i}", [P, 512]) for i in range(2)]
                if mlp:
                    ps_m = ps("ps_m", [P, KH, P])
                    ps_b = ps("ps_b", [P, D])
                    (y1, stat1, mean1, root_1, inv1, normed, y2, y2r, stat2, mean2, root_2, inv2) = sems(
                        tag, "y1 stat1 mean1 root_1 inv1 normed y2 y2r stat2 mean2 root_2 inv2")
                else:
                    ps_d = ps("ps_d", [P, H + 1])
                if last:
                    means = sb("means", [P, NT])
                    variances = sb("variances", [P, NT])
                    rstds = sb("rstds", [P, NT])
                    yd, ud, eluded, zd, kept, stated, averaged, meaned, rooted, inverted = sems(
                        tag, "yd ud eluded zd kept stated averaged meaned rooted inverted")
                if mlp:
                    dall = sb("dall", [P, NT, H])
                    dparts = sb("dparts", [P, NT, PARTS * H], BF16)
                    nowhere = sb("nowhere", [P, PARTS * H], BF16)
                    split, = sems(tag, "split")
                (staged, summed, c, finished, turned, moved, nexted, outed, dstaged, dturned, biased,
                 rooted1, mid, midmoved, first) = sems(
                    tag, "staged summed c finished turned moved nexted outed dstaged dturned biased rooted1 mid midmoved "
                         "first")
                sdone, inverted1, cleared = sems(tag, "sdone inverted1 cleared")
                loaded = sems(tag, "ld0 ld1 ld2 ld3")
                stored = sems(tag, "st0 st1 st2 st3")
                LD = 2 if last else 1
                ST = 1 if last else 2

                CH = {"mlp": 0, "attn": 6, "sage": 2, "sagelast": 0}[kind]
                CE = 1
                CR = 6

                with nc.Block() as block:
                    @block.gpsimd
                    def _(pool):
                        half = (NT // 2) * P
                        if not last:
                            if half:
                                pool.wait_ge(staged, NT // 2)
                                nc.gpsimd.memset(agg[:, :, 0:half], 0.0).then_inc(cleared, 1)
                            pool.wait_ge(staged, NT)
                            nc.gpsimd.memset(agg[:, :, half:NW], 0.0).then_inc(cleared, 1)
                            pool.wait_ge(cleared, 2 if half else 1)

                    @block.sync
                    def _(sp):
                        def load(t, s, v):
                            r = rows(t)
                            if later(t, B):
                                sp.wait_ge(zd if last else finished, t - B + 1)
                            if anysage:
                                sp.dma_start(rd[s][0:r, :], rtab[bass.ds(t * P, r), :]).then_inc(loaded[s], 16)
                            if not sage:
                                sp.dma_start(rs[s][0:r, :], resid[bass.ds(t * P, r), :]).then_inc(loaded[s], 16)

                        def store(t, s, v):
                            r = rows(t)
                            sp.wait_ge(finished, t + 1)
                            sp.dma_start(to[bass.ds(t * P, r), :], fin[s][0:r, :]).then_inc(stored[s], 16)
                            if mlp:
                                sp.wait_ge(outed, t + 1)
                                sp.dma_start(t_hc[bass.ds(t * P, r), :], outt[s][0:r, 0:HCW]).then_inc(stored[s], 16)
                            elif not last:
                                sp.wait_ge(outed, t + 1)
                                sp.dma_start(second[bass.ds(t * P, r), :], outt[s][0:r, :]).then_inc(stored[s], 16)
                        if mlp:
                            sp.wait_ge(first, 1)
                            sp.dma_start(t_dst[N:N + P, :], nowhere[:, :]).then_inc(sdone, 16)
                            sp.wait_ge(sdone, 16)
                        if last:
                            pipelined(sp, NT, B, [(0, load)])
                            pipelined(sp, NT, B, [(0, store)])
                        else:
                            pipelined(sp, NT, B, [(0, load), (5 if mlp else 4, store)])
                        if mlp:
                            sp.wait_ge(split, 2 * PARTS)
                            sp.dma_start(t_dst[0:(NT - 1) * P, :].rearrange("(t p) c -> p t c", p=P),
                                         dparts[:, 0:NT - 1, :]).then_inc(sdone, 16)
                            sp.dma_start(t_dst[(NT - 1) * P:N, :], dparts[0:LASTR, NT - 1, :]).then_inc(sdone, 16)
                            sp.wait_ge(sdone, 16 * 3)
                        for s in range(B):
                            n = len(range(s, NT, B))
                            if n:
                                sp.wait_ge(stored[s], 16 * n * ST)

                    @block.scalar
                    def _(act):
                        def stage(t, s, v):
                            r = rows(t)
                            if later(t, B):
                                act.wait_ge(summed, t - B + 1)
                            nc.scalar.activation(st[s][:, :, 0:r], agg[:, :, bass.ds(t * P, r)],
                                                 ACT.Copy).then_inc(staged, 1)
                            if attn:
                                if later(t, 1):
                                    act.wait_ge(dturned, t)
                                nc.scalar.activation(dst_[:, 0:r], den[:, bass.ds(t * P, r)],
                                                     ACT.Copy).then_inc(dstaged, 1)

                        def exp_(t, s, v):
                            r = rows(t)
                            if last:
                                act.wait_ge(yd, t + 1)
                            else:
                                act.wait_ge(c, CH * t + CE)
                            nc.scalar.activation(e[s][0:r, :], y[s][0:r, :], ACT.Exp).then_inc(biased, 1)

                        def root(t, s, after, count, done):
                            r = rows(t)
                            act.wait_ge(after, count)
                            nc.scalar.activation(sd[s][0:r, :], mv[s][0:r, 1:2], ACT.Sqrt,
                                                 bias=epsc[0:r, :]).then_inc(done, 1)

                        def keep(t, s, v):
                            r = rows(t)
                            act.wait_ge(zd, t + 1)
                            act.nop(nofuse=True)
                            nc.scalar.activation(agg[0:r, :, bass.ds(t * P, P)],
                                                 u[s][0:r, :].rearrange("p (k n) -> p k n", k=KH),
                                                 ACT.Copy).then_inc(kept, 1)

                        def mid_(t, s, v):
                            r = rows(t)
                            act.wait_ge(mid, t + 1)
                            if later(t, 2):
                                act.wait_ge(biased, t - 1)
                            for k in range(KH):
                                m = nc.scalar.activation(mlpT[s % 2][:, k, 0:r], ps_m[:, k, 0:r], ACT.Relu,
                                                         bias=cols_of["ln_b"][:, k:k + 1],
                                                         scale=cols_of["ln_g"][:, k:k + 1])
                            m.then_inc(midmoved, 1)

                        def move(t, s, v):
                            r = rows(t)
                            act.wait_ge(turned, t + 1)
                            if later(t, B):
                                act.wait_ge(nexted, t - B + 1)
                            nc.scalar.activation(hT[s][:, :, 0:r], ps_t[s % 2][:, :, 0:r], ACT.Copy).then_inc(moved, 1)

                        def out_(t, s, v):
                            r = rows(t)
                            act.wait_ge(nexted, t + 1)
                            if last:
                                nc.scalar.activation(aux[:, :, bass.ds(t * P, r)],
                                                     ps_n[s % 2][:, 0:D].rearrange("p (k n) -> p k n", k=KH)[:, :, 0:r],
                                                     ACT.Copy).then_inc(outed, 1)
                                return
                            if later(t, B):
                                act.wait_ge(stored[s], v * 16 * ST)
                            if mlp:
                                act.nop(nofuse=True)
                                nc.scalar.activation(dall[0:r, bass.ds(t, 1), :],
                                                     ps_n[s % 2][0:r, HCW:HCW + H].unsqueeze(1), ACT.Copy)
                            nc.scalar.activation(outt[s][0:r, :], ps_n[s % 2][0:r, 0:OUTW], ACT.Copy
                                                 ).then_inc(outed, 1)

                        if mlp:
                            pipelined(act, NT, B, [
                                (0, stage), (4, move), (2, mid_),
                                (3, lambda t, s, v: root(t, s, mean2, t + 1, root_2)),
                                (1, lambda t, s, v: root(t, s, mean1, t + 1, root_1)), (4, out_)])
                        elif attn:
                            pipelined(act, NT, B, [
                                (0, stage), (3, move),
                                (1, lambda t, s, v: root(t, s, c, CH * t + CR, rooted1))])
                        elif sage:
                            pipelined(act, NT, B, [(0, stage), (3, move), (1, exp_)])
                        else:
                            pipelined(act, NT, B, [(0, stage), (2, keep), (1, exp_)])
                            act.wait_ge(meaned, NT)
                            nc.scalar.activation(rstds[:, :], variances[:, :], ACT.Sqrt,
                                                 bias=epsc[:, :]).then_inc(rooted, 1)
                            pipelined(act, NT, B, [(0, move), (1, out_)])
                        if last or mlp:
                            act.wait_ge(outed, NT)

                    @block.vector
                    def _(dve):
                        def fin_free(t, s, v):
                            if later(t, B):
                                dve.wait_ge(stored[s], v * 16 * ST)
                                dve.wait_ge(turned, t - B + 1)

                        def front(t, s, v):
                            r = rows(t)
                            b = s % 2
                            dve.wait_ge(loaded[s], (v + 1) * 16 * LD)
                            if attn:
                                dve.wait_ge(dturned, t + 1)
                                dve.wait_ge(summed, t + 1)
                                nc.vector.tensor_scalar(dtile[b][0:r, 0:H], ps_d[0:r, 0:H], 1e-30, None, ALU.max)
                                nc.vector.tensor_scalar(dtile[b][0:r, H:H + 1], ps_d[0:r, H:H + 1], 1.0, None,
                                                        ALU.max).then_inc(c, 1)
                                dve.wait_ge(c, CH * t + 1)
                                nc.vector.reciprocal(rden[b][0:r, :], dtile[b][0:r, 0:H])
                                nc.vector.reciprocal(invdeg[0:r, bass.ds(t, 1)], dtile[b][0:r, H:H + 1]
                                                     ).then_inc(c, 1)
                                dve.wait_ge(c, CH * t + 2)
                                nc.vector.tensor_tensor(
                                    u[s][0:r, :].rearrange("p (h d) -> p h d", h=H),
                                    ps_a[b][0:r, :].rearrange("p (h d) -> p h d", h=H),
                                    rden[b][0:r, :].unsqueeze(2).broadcast_to([r, H, DH]), ALU.mult
                                ).then_inc(c, 1)
                                dve.wait_ge(c, CH * t + 3)
                                nc.vector.scalar_tensor_tensor(out=y[s][0:r, :], in0=rs[s][0:r, :], scalar=2.0,
                                                               in1=u[s][0:r, :], op0=ALU.mult, op1=ALU.add
                                                               ).then_inc(c, 1)
                                dve.wait_ge(c, CH * t + 4)
                                nc.vector.bn_stats(stats[s][0:r, :], y[s][0:r, :]).then_inc(c, 1)
                                dve.wait_ge(c, CH * t + 5)
                                dve.nop(nofuse=True)
                                nc.vector.bn_aggr(mv[s][0:r, :], stats[s][0:r, :]).then_inc(c, 1)
                            else:
                                dve.wait_ge(summed, t + 1)
                                nc.vector.scalar_tensor_tensor(out=y[s][0:r, :], in0=ps_a[b][0:r, :],
                                                               scalar=invdeg[0:r, bass.ds(t, 1)],
                                                               in1=rd[s][0:r, :], op0=ALU.mult, op1=ALU.add
                                                               ).then_inc(c, 1)
                                dve.wait_ge(c, CH * t + 1)
                                nc.vector.tensor_scalar(u[s][0:r, :], y[s][0:r, :], 0.0, -1.0, ALU.max,
                                                        ALU.add).then_inc(c, 1)

                        def front_end(t, s, v):
                            r = rows(t)
                            if attn:
                                dve.wait_ge(rooted1, t + 1)
                                nc.vector.reciprocal(rstd[s][0:r, :], sd[s][0:r, :]).then_inc(inverted1, 1)
                                dve.wait_ge(inverted1, t + 1)
                                fin_free(t, s, v)
                                nc.vector.tensor_scalar(fin[s][0:r, :], y[s][0:r, :], mv[s][0:r, 0:1],
                                                        rstd[s][0:r, :], ALU.subtract, ALU.mult
                                                        ).then_inc(finished, 1)
                            else:
                                dve.wait_ge(c, CH * t + 2)
                                dve.wait_ge(biased, t + 1)
                                fin_free(t, s, v)
                                nc.vector.scalar_tensor_tensor(out=fin[s][0:r, :], in0=e[s][0:r, :], scalar=1.0,
                                                               in1=u[s][0:r, :], op0=ALU.min, op1=ALU.add
                                                               ).then_inc(finished, 1)

                        def mlp_first(t, s, v):
                            r = rows(t)
                            dve.wait_ge(summed, t + 1)
                            nc.vector.tensor_tensor(y[s][0:r, :], ps_a[s % 2][0:r, :], rows_of["b_g1"][0:r, :],
                                                    ALU.add).then_inc(y1, 1)
                            dve.wait_ge(y1, t + 1)
                            nc.vector.bn_stats(stats[s][0:r, :], y[s][0:r, :]).then_inc(stat1, 1)
                            dve.wait_ge(stat1, t + 1)
                            dve.nop(nofuse=True)
                            nc.vector.bn_aggr(mv[s][0:r, :], stats[s][0:r, :]).then_inc(mean1, 1)

                        def mlp_norm(t, s, v):
                            r = rows(t)
                            dve.wait_ge(root_1, t + 1)
                            nc.vector.reciprocal(rstd[s][0:r, :], sd[s][0:r, :]).then_inc(inv1, 1)
                            dve.wait_ge(inv1, t + 1)
                            nc.vector.tensor_scalar(u[s][0:r, :], y[s][0:r, :], mv[s][0:r, 0:1], rstd[s][0:r, :],
                                                    ALU.subtract, ALU.mult).then_inc(normed, 1)

                        def mlp_second(t, s, v):
                            r = rows(t)
                            dve.wait_ge(biased, t + 1)
                            dve.wait_ge(normed, t + 1)
                            nc.vector.tensor_tensor(y[s][0:r, :], ps_b[0:r, :], rows_of["b_g2"][0:r, :],
                                                    ALU.add).then_inc(y2, 1)
                            dve.wait_ge(y2, t + 1)
                            dve.wait_ge(loaded[s], (v + 1) * 16 * LD)
                            nc.vector.tensor_tensor(y[s][0:r, :], y[s][0:r, :], rs[s][0:r, :],
                                                    ALU.add).then_inc(y2r, 1)
                            dve.wait_ge(y2r, t + 1)
                            nc.vector.bn_stats(stats[s][0:r, :], y[s][0:r, :]).then_inc(stat2, 1)
                            dve.wait_ge(stat2, t + 1)
                            dve.nop(nofuse=True)
                            nc.vector.bn_aggr(mv[s][0:r, :], stats[s][0:r, :]).then_inc(mean2, 1)

                        def mlp_final(t, s, v):
                            r = rows(t)
                            dve.wait_ge(root_2, t + 1)
                            nc.vector.reciprocal(rstd[s][0:r, :], sd[s][0:r, :]).then_inc(inv2, 1)
                            dve.wait_ge(inv2, t + 1)
                            fin_free(t, s, v)
                            nc.vector.tensor_scalar(fin[s][0:r, :], y[s][0:r, :], mv[s][0:r, 0:1], rstd[s][0:r, :],
                                                    ALU.subtract, ALU.mult).then_inc(finished, 1)

                        def last_sum(t, s, v):
                            r = rows(t)
                            dve.wait_ge(loaded[s], (v + 1) * 16 * LD)
                            dve.wait_ge(summed, t + 1)
                            nc.vector.scalar_tensor_tensor(out=y[s][0:r, :], in0=ps_a[s % 2][0:r, :],
                                                           scalar=invdeg[0:r, bass.ds(t, 1)],
                                                           in1=rd[s][0:r, :], op0=ALU.mult, op1=ALU.add
                                                           ).then_inc(yd, 1)
                            dve.wait_ge(yd, t + 1)
                            if later(t, B):
                                dve.wait_ge(kept, t - B + 1)
                            nc.vector.tensor_scalar(u[s][0:r, :], y[s][0:r, :], 0.0, -1.0, ALU.max,
                                                    ALU.add).then_inc(ud, 1)

                        def last_elu(t, s, v):
                            r = rows(t)
                            dve.wait_ge(biased, t + 1)
                            dve.wait_ge(ud, t + 1)
                            nc.vector.scalar_tensor_tensor(out=y[s][0:r, :], in0=e[s][0:r, :], scalar=1.0,
                                                           in1=u[s][0:r, :], op0=ALU.min, op1=ALU.add
                                                           ).then_inc(eluded, 1)
                            dve.wait_ge(eluded, t + 1)
                            nc.vector.tensor_tensor(u[s][0:r, :], y[s][0:r, :], rs[s][0:r, :],
                                                    ALU.add).then_inc(zd, 1)
                            dve.wait_ge(zd, t + 1)
                            nc.vector.bn_stats(stats[s][0:r, :], u[s][0:r, :]).then_inc(stated, 1)
                            dve.wait_ge(stated, t + 1)
                            dve.nop(nofuse=True)
                            nc.vector.bn_aggr(mv[s][0:r, :], stats[s][0:r, :]).then_inc(averaged, 1)
                            dve.wait_ge(averaged, t + 1)
                            nc.vector.tensor_copy(means[0:r, bass.ds(t, 1)], mv[s][0:r, 0:1])
                            nc.vector.tensor_copy(variances[0:r, bass.ds(t, 1)], mv[s][0:r, 1:2]
                                                  ).then_inc(meaned, 1)

                        def last_norm(t, s, v):
                            r = rows(t)
                            fin_free(t, s, v)
                            nc.vector.tensor_scalar(fin[s][0:r, :].rearrange("p (k n) -> p k n", k=KH),
                                                    agg[0:r, :, bass.ds(t * P, P)], means[0:r, bass.ds(t, 1)],
                                                    rstds[0:r, bass.ds(t, 1)], ALU.subtract, ALU.mult
                                                    ).then_inc(finished, 1)

                        def addbias(t, s, v):
                            r = rows(t)
                            dve.wait_ge(nexted, t + 1)
                            if later(t, B):
                                dve.wait_ge(stored[s], v * 16 * ST)
                            nc.vector.tensor_tensor(outt[s][0:r, :], ps_n[s % 2][0:r, 0:D], rows_of[nbias][0:r, :],
                                                    ALU.add).then_inc(outed, 1)

                        if mlp:
                            nc.vector.memset(dall[:, :, :], 0.0)
                            nc.vector.memset(nowhere[:, :], 0.0).then_inc(first, 1)
                            pipelined(dve, NT, B, [(2, mlp_norm), (3, mlp_second), (1, mlp_first), (3, mlp_final)])
                            dve.wait_ge(outed, NT)
                            for k in range(PARTS):
                                part = dparts[:, :, k * H:(k + 1) * H]
                                nc.vector.tensor_copy(part, dall[:, :, :]).then_inc(split, 1)
                                dve.wait_ge(split, 2 * k + 1)
                                nc.vector.tensor_tensor(dall[:, :, :], dall[:, :, :], part,
                                                        ALU.subtract).then_inc(split, 1)
                                dve.wait_ge(split, 2 * k + 2)
                        elif last:
                            nc.vector.memset(variances[:, :], 1.0)
                            pipelined(dve, NT, B, [(2, last_elu), (1, last_sum)])
                            dve.wait_ge(rooted, 1)
                            nc.vector.reciprocal(rstds[:, :], rstds[:, :]).then_inc(inverted, 1)
                            dve.wait_ge(inverted, 1)
                            dve.wait_ge(kept, NT)
                            pipelined(dve, NT, B, [(0, last_norm)])
                        else:
                            pipelined(dve, NT, B, [(2, front_end), (1, front), (3, addbias)])

                    @block.tensor
                    def _(pe):
                        def product(o, lhs, w, r, width, sem):
                            for k in range(KH):
                                m = nc.tensor.matmul(o[0:r, 0:width], lhs[:, k, 0:r], w[:, k, 0:width],
                                                     start=(k == 0), stop=(k == KH - 1))
                            m.then_inc(sem, 1)

                        def sum_(t, s, v):
                            r = rows(t)
                            b = s % 2
                            pe.wait_ge(staged, t + 1)
                            if later(t, 2):
                                if mlp or last:
                                    pe.wait_ge(y1 if mlp else yd, t - 1)
                                else:
                                    pe.wait_ge(c, CH * (t - 1))
                            if attn:
                                pe.wait_ge(dstaged, t + 1)
                                if later(t, 1):
                                    pe.wait_ge(c, CH * t)
                                pe.nop(nofuse=True)
                                nc.tensor.transpose(ps_d[0:r, :], dst_[:, 0:r], ident[0:H + 1, 0:H + 1]
                                                    ).then_inc(dturned, 1)
                                for k in range(KH):
                                    m = nc.tensor.transpose(ps_a[b][0:r, k * P:(k + 1) * P], st[s][:, k, 0:r],
                                                            ident[:, :])
                                m.then_inc(summed, 1)
                            else:
                                product(ps_a[b], st[s], weight, r, D, summed)

                        def mid_turn(t, s, v):
                            r = rows(t)
                            pe.wait_ge(normed, t + 1)
                            if later(t, 1):
                                pe.wait_ge(midmoved, t)
                            for k in range(KH):
                                m = nc.tensor.transpose(ps_m[:, k, 0:r], u[s][0:r, k * P:(k + 1) * P],
                                                        ident[0:r, 0:r])
                            m.then_inc(mid, 1)

                        def second_product(t, s, v):
                            pe.wait_ge(midmoved, t + 1)
                            if later(t, 1):
                                pe.wait_ge(y2, t)
                            product(ps_b, mlpT[s % 2], wT["W_g2"], rows(t), D, biased)

                        def turn(t, s, v):
                            r = rows(t)
                            pe.wait_ge(finished, t + 1)
                            if later(t, 2):
                                pe.wait_ge(moved, t - 1)
                            for k in range(KH):
                                m = nc.tensor.transpose(ps_t[s % 2][:, k, 0:r], fin[s][0:r, k * P:(k + 1) * P],
                                                        ident[0:r, 0:r])
                            m.then_inc(turned, 1)

                        def table(t, s, v):
                            r = rows(t)
                            pe.wait_ge(moved, t + 1)
                            if later(t, 2):
                                pe.wait_ge(outed, t - 1)
                            if last:
                                for a in range(KH):
                                    for k in range(KH):
                                        m = nc.tensor.matmul(ps_n[s % 2][:, a * P:a * P + r],
                                                             nxt[:, k, a * P:(a + 1) * P], hT[s][:, k, 0:r],
                                                             start=(k == 0), stop=(k == KH - 1))
                                m.then_inc(nexted, 1)
                            else:
                                product(ps_n[s % 2], hT[s], nxt, r, NXW, nexted)

                        if mlp:
                            pipelined(pe, NT, B, [(4, turn), (2, mid_turn), (1, sum_), (4, table),
                                                  (2, second_product)])
                        elif last:
                            pipelined(pe, NT, B, [(0, sum_)])
                            pipelined(pe, NT, B, [(0, turn), (1, table)])
                        else:
                            pipelined(pe, NT, B, [(3, turn), (1, sum_), (3, table)])

        def clear_agg(tag):
            done, = sems(tag, "cleared")
            with nc.Block() as block:
                @block.vector
                def _(dve):
                    nc.vector.memset(agg[:, 0, :], 0.0).then_inc(done, 1)
                    dve.wait_ge(done, 2)

                @block.gpsimd
                def _(pool):
                    nc.gpsimd.memset(agg[:, 1, :], 0.0).then_inc(done, 1)

        def last_phase(tag):
            CW = 512
            NC_ = -(-N // CW)
            with ExitStack() as scope:
                sb, ps = scoped(scope, tag)
                stats = sb("bstats", [P, KH, NC_, 6])
                mv = sb("bmv", [P, KH, 2])
                sd = sb("bsd", [P, KH])
                scl = sb("scl", [P, KH])
                off = sb("off", [P, KH])
                ps_o = [[ps(f"ps_o{i}{a}", [P, CW]) for a in range(KH)] for i in range(2)]
                (prod, placed, v, rooted, normed) = sems(tag, "prod placed v rooted normed")
                with nc.Block() as block:
                    @block.tensor
                    def _(pe):
                        for c in range(NC_):
                            n = min(CW, N - c * CW)
                            if c >= 2:
                                pe.wait_ge(placed, (c - 1) * KH)
                            for a in range(KH):
                                for k in range(KH):
                                    m = nc.tensor.matmul(ps_o[c % 2][a][:, 0:n], wT["W_rel"][:, k, a * P:(a + 1) * P],
                                                         agg[:, k, c * CW:c * CW + n], start=(k == 0),
                                                         stop=(k == KH - 1))
                            m.then_inc(prod, 1)

                    @block.vector
                    def _(dve):
                        for c in range(NC_):
                            n = min(CW, N - c * CW)
                            dve.wait_ge(prod, c + 1)
                            for a in range(KH):
                                nc.vector.scalar_tensor_tensor(
                                    out=agg[:, a, c * CW:c * CW + n], in0=ps_o[c % 2][a][:, 0:n],
                                    scalar=cols_of["b_rel"][:, a:a + 1], in1=aux[:, a, c * CW:c * CW + n],
                                    op0=ALU.add, op1=ALU.add).then_inc(placed, 1)
                            dve.wait_ge(placed, (c + 1) * KH)
                            for a in range(KH):
                                m = nc.vector.bn_stats(stats[:, a, c, :], agg[:, a, c * CW:c * CW + n])
                        m.then_inc(v, 1)
                        dve.wait_ge(v, 1)
                        for a in range(KH):
                            m = nc.vector.bn_aggr(mv[:, a, :], stats[:, a, :, :])
                        m.then_inc(v, 1)
                        dve.wait_ge(rooted, 1)
                        nc.vector.reciprocal(scl[:, :], sd[:, :]).then_inc(v, 1)
                        dve.wait_ge(v, 3)
                        nc.vector.tensor_tensor(scl[:, :], scl[:, :], cols_of["gamma"][:, :], ALU.mult).then_inc(v, 1)
                        dve.wait_ge(v, 4)
                        nc.vector.tensor_tensor(off[:, :], mv[:, :, 0], scl[:, :], ALU.mult).then_inc(v, 1)
                        dve.wait_ge(v, 5)
                        nc.vector.tensor_tensor(off[:, :], cols_of["beta"][:, :], off[:, :],
                                                ALU.subtract).then_inc(v, 1)
                        dve.wait_ge(v, 6)

                    @block.scalar
                    def _(act):
                        act.wait_ge(v, 2)
                        nc.scalar.activation(sd[:, :], mv[:, :, 1], ACT.Sqrt, bias=epsc[:, :]).then_inc(rooted, 1)
                B = 4
                st = [sb(f"fst{i}", [P, KH, P]) for i in range(B)]
                xr = [sb(f"fx{i}", [P, D]) for i in range(B)]
                y = [sb(f"fy{i}", [P, D]) for i in range(B)]
                u = [sb(f"fu{i}", [P, D]) for i in range(B)]
                fin = [sb(f"ffin{i}", [P, D]) for i in range(B)]
                st6 = [sb(f"fs{i}", [P, 6]) for i in range(B)]
                mv2 = [sb(f"fm{i}", [P, 2]) for i in range(B)]
                sd2 = [sb(f"fd{i}", [P, 1]) for i in range(B)]
                rstd = [sb(f"fr{i}", [P, 1]) for i in range(B)]
                ps_f = [ps(f"ps_f{i}", [P, D]) for i in range(2)]
                staged, turned, c, root, inverted, finished = sems(tag, "staged turned c root inverted finished")
                loaded = sems(tag, "fl0 fl1 fl2 fl3")
                stored = sems(tag, "fs0 fs1 fs2 fs3")

                with nc.Block() as block:
                    @block.sync
                    def _(sp):
                        def load(t, s, v):
                            r = rows(t)
                            if later(t, B):
                                sp.wait_ge(finished, t - B + 1)
                            sp.dma_start(xr[s][0:r, :], t_x3[bass.ds(t * P, r), :]).then_inc(loaded[s], 16)

                        def store(t, s, v):
                            r = rows(t)
                            sp.wait_ge(finished, t + 1)
                            sp.dma_start(out[bass.ds(t * P, r), :], fin[s][0:r, :]).then_inc(stored[s], 16)
                        pipelined(sp, NT, B, [(0, load), (3, store)])
                        for s in range(B):
                            n = len(range(s, NT, B))
                            if n:
                                sp.wait_ge(stored[s], 16 * n)

                    @block.scalar
                    def _(act):
                        def stage(t, s, v):
                            r = rows(t)
                            if later(t, B):
                                act.wait_ge(turned, t - B + 1)
                            for a in range(KH):
                                m = nc.scalar.activation(st[s][:, a, 0:r], agg[:, a, bass.ds(t * P, r)], ACT.Relu,
                                                         bias=off[:, a:a + 1], scale=scl[:, a:a + 1])
                            m.then_inc(staged, 1)

                        def root1(t, s, v):
                            r = rows(t)
                            act.wait_ge(c, t * 4 + 4)
                            nc.scalar.activation(sd2[s][0:r, :], mv2[s][0:r, 1:2], ACT.Sqrt,
                                                 bias=epsc[0:r, :]).then_inc(root, 1)
                        pipelined(act, NT, B, [(0, stage), (1, root1)])

                    @block.tensor
                    def _(pe):
                        def turn(t, s, v):
                            r = rows(t)
                            pe.wait_ge(staged, t + 1)
                            if later(t, 2):
                                pe.wait_ge(c, (t - 1) * 4)
                            for a in range(KH):
                                m = nc.tensor.transpose(ps_f[s % 2][0:r, a * P:(a + 1) * P], st[s][:, a, 0:r],
                                                        ident[:, :])
                            m.then_inc(turned, 1)
                        pipelined(pe, NT, B, [(0, turn)])

                    @block.vector
                    def _(dve):
                        def chain(t, s, v):
                            r = rows(t)
                            dve.wait_ge(turned, t + 1)
                            dve.wait_ge(loaded[s], (v + 1) * 16)
                            nc.vector.tensor_tensor(y[s][0:r, :], ps_f[s % 2][0:r, :], xr[s][0:r, :],
                                                    ALU.add).then_inc(c, 1)
                            dve.wait_ge(c, t * 4 + 1)
                            nc.vector.scalar_tensor_tensor(out=u[s][0:r, :], in0=y[s][0:r, :], scalar=0.0,
                                                           in1=xr[s][0:r, :], op0=ALU.max, op1=ALU.add).then_inc(c, 1)
                            dve.wait_ge(c, t * 4 + 2)
                            nc.vector.bn_stats(st6[s][0:r, :], u[s][0:r, :]).then_inc(c, 1)
                            dve.wait_ge(c, t * 4 + 3)
                            dve.nop(nofuse=True)
                            nc.vector.bn_aggr(mv2[s][0:r, :], st6[s][0:r, :]).then_inc(c, 1)

                        def finish(t, s, v):
                            r = rows(t)
                            dve.wait_ge(root, t + 1)
                            nc.vector.reciprocal(rstd[s][0:r, :], sd2[s][0:r, :]).then_inc(inverted, 1)
                            dve.wait_ge(inverted, t + 1)
                            if later(t, B):
                                dve.wait_ge(stored[s], v * 16)
                            nc.vector.tensor_scalar(fin[s][0:r, :], u[s][0:r, :], mv2[s][0:r, 0:1],
                                                    rstd[s][0:r, :], ALU.subtract, ALU.mult).then_inc(finished, 1)
                        pipelined(dve, NT, B, [(1, finish), (0, chain)])

        def copy_out(table):
            done, = sems("co", "copied_out")
            with nc.Block() as block:
                @block.sync
                def _(sp):
                    sp.dma_start(out, table).then_inc(done, 16)
                    sp.wait_ge(done, 16)

        phase(edge_tables)
        phase(weights)
        phase(first_table)
        phase(edge_phase, "e0", "mlp", t_x0, D)
        phase(node_phase, "n0", "mlp", resid=ins["x"], to=t_x1)
        layer0.close()
        if depth == 1:
            return copy_out(t_x1)
        phase(edge_phase, "e1", "attn", t_hc, HCW)
        phase(node_phase, "n1", "attn", resid=t_x1, to=t_x2, second=t_r[0])
        if depth == 2:
            return copy_out(t_x2)
        phase(edge_phase, "e2", "sum", t_x2, D)
        phase(node_phase, "n2", "sage", rtab=t_r[0], to=t_h1, second=t_r[1])
        phase(edge_phase, "e3", "sum", t_h1, D)
        phase(node_phase, "n3", "sage", rtab=t_r[1], to=t_h2, second=t_r[2])
        phase(edge_phase, "e4", "sum", t_h2, D)
        phase(node_phase, "n4", "sagelast", resid=t_x2, rtab=t_r[2], to=t_x3)
        if depth == 3:
            return copy_out(t_x3)
        phase(clear_agg, "z5")
        phase(edge_phase, "e5", "weighted", t_x3, D)
        phase(last_phase, "n5")


DEPTH = 4


def kernel(**inputs):
    import numpy as _np
    import concourse.bacc as _bacc
    from concourse import mybir as _mybir
    from concourse.bass_utils import run_bass_kernel_spmd as _run

    nc = _bacc.Bacc("TRN2", target_bir_lowering=False, num_devices=1)
    arrays, args = {}, {}
    for name, value in inputs.items():
        a = _np.ascontiguousarray(value)
        arrays[f"in_{name}_dram"] = a
        args[name] = nc.dram_tensor(f"in_{name}_dram", a.shape, _mybir.dt.from_np(a.dtype), kind="ExternalInput").ap()
    shape = inputs["x"].shape
    out = nc.dram_tensor("out_0_dram", shape, _mybir.dt.float32, kind="ExternalOutput").ap()
    gnn_kernel(nc, args, out, DEPTH)
    r = _run(nc, [arrays], core_ids=[0])
    return r.results[0]["out_0_dram"]
```
